# Optimizing a Trainium2 kernel written in Bass

```python
import numpy as np
import jax
import jax.numpy as jnp

def _softmax(x, axis=-1):
    return jax.nn.softmax(x, axis=axis)

def _gelu(x):
    return jax.nn.gelu(x, approximate=True)

def _silu(x):
    return jax.nn.silu(x)

def _sigmoid(x):
    return jax.nn.sigmoid(x)

def _layernorm(x, axis=-1, eps=1e-05):
    m = jnp.mean(x, axis=axis, keepdims=True)
    v = jnp.var(x, axis=axis, keepdims=True)
    return (x - m) / jnp.sqrt(v + eps)

def _scatter_add(tgt, idx, src, axis=0):
    return tgt.at[idx].add(src)

def _segment_sum(src, seg, n):
    return jax.ops.segment_sum(src, seg, n)
kernel_name = 'mk_gnn_resnorm_d4_gnn_r8_bb7d9e'

def setup_inputs(seed: int=0):
    np.random.seed(seed)
    _w = jnp.asarray

    def _rec_inputs():
        import jax
        import jax.numpy as jnp
        _gk = jax.random.key(seed)
        x = -0.0002117 + 1 * jax.random.normal(jax.random.fold_in(_gk, 1), (1250, 512), jnp.float32)
        _s = jax.random.randint(jax.random.fold_in(_gk, 2), (10000,), 0, 1250, jnp.int32)
        _d = jax.random.randint(jax.random.fold_in(_gk, 3), (10000,), 0, 1250, jnp.int32)
        _loop = jnp.arange(1250, dtype=jnp.int32)
        src = jnp.concatenate([_s, _d, _loop])
        dst = jnp.concatenate([_d, _s, _loop])
        _o = jnp.argsort(dst, stable=True)
        src = src[_o]
        dst = dst[_o]
        edge_type_2 = jax.random.randint(jax.random.fold_in(_gk, 13), (21250,), 0, 2, jnp.int32)
        return (x, src, dst, edge_type_2)
    x, src, dst, edge_type_2 = _rec_inputs()

    def _L0_gnn_setup():
        import jax, jax.numpy as jnp
        import numpy as np
        N = 6250
        E = 100000
        D = 512

        def _gcn_conv(x, edge_index, W, b):
            n = x.shape[0]
            xw = x @ W.T
            loop = jnp.arange(n, dtype=edge_index.dtype)
            row = jnp.concatenate([edge_index[0], loop])
            col = jnp.concatenate([edge_index[1], loop])
            deg = jax.ops.segment_sum(jnp.ones_like(row, dtype=xw.dtype), col, num_segments=n)
            dinv = jnp.where(deg > 0, jax.lax.rsqrt(deg), 0.0)
            norm = dinv[row] * dinv[col]
            msgs = norm[:, None] * xw[row]
            out = jax.ops.segment_sum(msgs, col, num_segments=n)
            return out + b

        def _batch_norm(h, gamma, beta, eps=1e-05):
            mean = jnp.mean(h, axis=0)
            var = jnp.var(h, axis=0)
            return (h - mean) * jax.lax.rsqrt(var + eps) * gamma + beta
        key = jax.random.key(seed)
        k1, k2, k3, k4, k5, k6 = jax.random.split(key, 6)
        x = jax.random.normal(k1, (N, D), dtype=jnp.float32)
        edge_index = jax.random.randint(k2, (2, E), 0, N, dtype=jnp.int64)
        W = jax.random.normal(k3, (D, D), dtype=jnp.float32) * (1.0 / np.sqrt(D))
        b = jnp.zeros((D,), dtype=jnp.float32)
        gamma = jnp.ones((D,), dtype=jnp.float32)
        beta = jnp.zeros((D,), dtype=jnp.float32)
        return {'x': x, 'edge_index': edge_index, 'W': W, 'b': b, 'gamma': gamma, 'beta': beta}
    _L0_gnn_all = _L0_gnn_setup()
    _L0_gnn_in = {k: v for k, v in _L0_gnn_all.items() if k in ('W', 'b', 'gamma', 'beta')}
    del _L0_gnn_all

    def _L1_gnn_setup():
        import jax, jax.numpy as jnp
        import numpy as np
        N, E, D = (1250, 20000, 512)

        def _sage_layer(h, src, dst, W_self, W_neigh, b, n_nodes):
            agg = jax.ops.segment_sum(h[src], dst, num_segments=n_nodes)
            deg = jax.ops.segment_sum(jnp.ones_like(dst, dtype=h.dtype), dst, num_segments=n_nodes)
            h_neigh = agg / jnp.maximum(deg, 1.0)[:, None]
            return jax.nn.relu(h @ W_self + h_neigh @ W_neigh + b)
        key = jax.random.key(seed)
        ks = jax.random.split(key, 8)
        scale = 1.0 / np.sqrt(D)
        return {'feats': jax.random.normal(ks[0], (N, D), dtype=jnp.float32), 'src': jax.random.randint(ks[1], (E,), 0, N, dtype=jnp.int32), 'dst': jax.random.randint(ks[2], (E,), 0, N, dtype=jnp.int32), 'W_self1': jax.random.normal(ks[3], (D, D), dtype=jnp.float32) * scale, 'W_neigh1': jax.random.normal(ks[4], (D, D), dtype=jnp.float32) * scale, 'b1': jnp.zeros((D,), dtype=jnp.float32), 'W_self2': jax.random.normal(ks[5], (D, D), dtype=jnp.float32) * scale, 'W_neigh2': jax.random.normal(ks[6], (D, D), dtype=jnp.float32) * scale, 'b2': jnp.zeros((D,), dtype=jnp.float32)}
    _L1_gnn_all = _L1_gnn_setup()
    _L1_gnn_in = {k: v for k, v in _L1_gnn_all.items() if k in ('W_self1', 'W_neigh1', 'b1', 'W_self2', 'W_neigh2', 'b2')}
    del _L1_gnn_all

    def _L2_gnn_setup():
        import jax, jax.numpy as jnp
        import numpy as np
        NUM_RELATIONS = 2
        NUM_BASES = 30
        HIDDEN = 512
        N_NODES = 1250
        N_EDGES = 20000

        def rgcn_gate_layer(x, row, col, edge_type, basis, att, gate_w, root, bias):
            H = x.shape[1]
            w = jnp.einsum('rb,bio->rio', att, basis)
            x_j = x[col]
            msgs = []
            for r in range(NUM_RELATIONS):
                gate = jax.nn.sigmoid(x_j @ gate_w[r, :, 0])
                msgs.append(gate[:, None] * x_j @ w[r])
            msg = jnp.where((edge_type == 0)[:, None], msgs[0], msgs[1])
            agg = jax.ops.segment_sum(msg, row, num_segments=x.shape[0])
            return agg + x @ root + bias
        key = jax.random.key(seed)
        ks = jax.random.split(key, 16)
        H, R, B = (HIDDEN, NUM_RELATIONS, NUM_BASES)
        bound = 1.0 / np.sqrt(B * H)
        u = lambda k, shape: jax.random.uniform(k, shape, jnp.float32, -bound, bound)
        inp = {'x': jax.random.normal(ks[0], (N_NODES, H), jnp.float32), 'edge_index': jax.random.randint(ks[1], (2, N_EDGES), 0, N_NODES, jnp.int32), 'edge_type': jax.random.randint(ks[2], (N_EDGES,), 0, R, jnp.int32), 'basis1': u(ks[3], (B, H, H)), 'att1': u(ks[4], (R, B)), 'gate_w1': u(ks[5], (R, H, 1)), 'root1': u(ks[6], (H, H)), 'bias1': u(ks[7], (H,)), 'basis2': u(ks[8], (B, H, H)), 'att2': u(ks[9], (R, B)), 'gate_w2': u(ks[10], (R, H, 1)), 'root2': u(ks[11], (H, H)), 'bias2': u(ks[12], (H,))}
        return inp
    _L2_gnn_all = _L2_gnn_setup()
    _L2_gnn_in = {k: v for k, v in _L2_gnn_all.items() if k in ('basis1', 'att1', 'gate_w1', 'root1', 'bias1', 'basis2', 'att2', 'gate_w2', 'root2', 'bias2')}
    del _L2_gnn_all

    def _L3_gnn_setup():
        import jax, jax.numpy as jnp
        import numpy as np
        N_NODES = 1250
        N_EDGES = 20000
        D = 512
        key = jax.random.key(seed)
        k_h, k_e, k_w1, k_w2 = jax.random.split(key, 4)
        h = jax.random.normal(k_h, (N_NODES, D), dtype=jnp.float32)
        edge_index = jax.random.randint(k_e, (2, N_EDGES), 0, N_NODES, dtype=jnp.int64)
        scale = 1.0 / np.sqrt(D)
        W1 = jax.random.normal(k_w1, (D, D), dtype=jnp.float32) * scale
        b1 = jnp.zeros((D,), dtype=jnp.float32)
        W2 = jax.random.normal(k_w2, (D, D), dtype=jnp.float32) * scale
        b2 = jnp.zeros((D,), dtype=jnp.float32)
        return {'h': h, 'edge_index': edge_index, 'W1': W1, 'b1': b1, 'W2': W2, 'b2': b2}
    _L3_gnn_all = _L3_gnn_setup()
    _L3_gnn_in = {k: v for k, v in _L3_gnn_all.items() if k in ('W1', 'b1', 'W2', 'b2')}
    del _L3_gnn_all
    return {'x': x, 'src': src, 'dst': dst, 'edge_type_2': edge_type_2, 'L0_gnn_W': _L0_gnn_in['W'], 'L0_gnn_b': _L0_gnn_in['b'], 'L0_gnn_gamma': _L0_gnn_in['gamma'], 'L0_gnn_beta': _L0_gnn_in['beta'], 'L1_gnn_W_self1': _L1_gnn_in['W_self1'], 'L1_gnn_W_neigh1': _L1_gnn_in['W_neigh1'], 'L1_gnn_b1': _L1_gnn_in['b1'], 'L1_gnn_W_self2': _L1_gnn_in['W_self2'], 'L1_gnn_W_neigh2': _L1_gnn_in['W_neigh2'], 'L1_gnn_b2': _L1_gnn_in['b2'], 'L2_gnn_basis1': _L2_gnn_in['basis1'], 'L2_gnn_att1': _L2_gnn_in['att1'], 'L2_gnn_gate_w1': _L2_gnn_in['gate_w1'], 'L2_gnn_root1': _L2_gnn_in['root1'], 'L2_gnn_bias1': _L2_gnn_in['bias1'], 'L2_gnn_basis2': _L2_gnn_in['basis2'], 'L2_gnn_att2': _L2_gnn_in['att2'], 'L2_gnn_gate_w2': _L2_gnn_in['gate_w2'], 'L2_gnn_root2': _L2_gnn_in['root2'], 'L2_gnn_bias2': _L2_gnn_in['bias2'], 'L3_gnn_W1': _L3_gnn_in['W1'], 'L3_gnn_b1': _L3_gnn_in['b1'], 'L3_gnn_W2': _L3_gnn_in['W2'], 'L3_gnn_b2': _L3_gnn_in['b2']}

def reference(x, src, dst, edge_type_2, L0_gnn_W, L0_gnn_b, L0_gnn_gamma, L0_gnn_beta, L1_gnn_W_self1, L1_gnn_W_neigh1, L1_gnn_b1, L1_gnn_W_self2, L1_gnn_W_neigh2, L1_gnn_b2, L2_gnn_basis1, L2_gnn_att1, L2_gnn_gate_w1, L2_gnn_root1, L2_gnn_bias1, L2_gnn_basis2, L2_gnn_att2, L2_gnn_gate_w2, L2_gnn_root2, L2_gnn_bias2, L3_gnn_W1, L3_gnn_b1, L3_gnn_W2, L3_gnn_b2):
    import jax
    import jax.numpy as jnp

    def _L0_gnn_ref(x, edge_index, W, b, gamma, beta):
        import jax, jax.numpy as jnp
        import numpy as np
        N = 6250
        E = 100000
        D = 512

        def _gcn_conv(x, edge_index, W, b):
            n = x.shape[0]
            xw = x @ W.T
            loop = jnp.arange(n, dtype=edge_index.dtype)
            row = jnp.concatenate([edge_index[0], loop])
            col = jnp.concatenate([edge_index[1], loop])
            deg = jax.ops.segment_sum(jnp.ones_like(row, dtype=xw.dtype), col, num_segments=n)
            dinv = jnp.where(deg > 0, jax.lax.rsqrt(deg), 0.0)
            norm = dinv[row] * dinv[col]
            msgs = norm[:, None] * xw[row]
            out = jax.ops.segment_sum(msgs, col, num_segments=n)
            return out + b

        def _batch_norm(h, gamma, beta, eps=1e-05):
            mean = jnp.mean(h, axis=0)
            var = jnp.var(h, axis=0)
            return (h - mean) * jax.lax.rsqrt(var + eps) * gamma + beta
        identity = x
        h = _gcn_conv(x, edge_index, W, b)
        h = _batch_norm(h, gamma, beta)
        h = jax.nn.gelu(h, approximate=False)
        return h + identity

    def _L1_gnn_ref(feats, src, dst, W_self1, W_neigh1, b1, W_self2, W_neigh2, b2):
        import jax, jax.numpy as jnp
        import numpy as np
        N, E, D = (1250, 20000, 512)

        def _sage_layer(h, src, dst, W_self, W_neigh, b, n_nodes):
            agg = jax.ops.segment_sum(h[src], dst, num_segments=n_nodes)
            deg = jax.ops.segment_sum(jnp.ones_like(dst, dtype=h.dtype), dst, num_segments=n_nodes)
            h_neigh = agg / jnp.maximum(deg, 1.0)[:, None]
            return jax.nn.relu(h @ W_self + h_neigh @ W_neigh + b)
        n_nodes = feats.shape[0]
        h = _sage_layer(feats, src, dst, W_self1, W_neigh1, b1, n_nodes)
        h = _sage_layer(h, src, dst, W_self2, W_neigh2, b2, n_nodes)
        return h

    def _L2_gnn_ref(x, edge_index, edge_type, basis1, att1, gate_w1, root1, bias1, basis2, att2, gate_w2, root2, bias2):
        import jax, jax.numpy as jnp
        import numpy as np
        NUM_RELATIONS = 2
        NUM_BASES = 30
        HIDDEN = 512
        N_NODES = 1250
        N_EDGES = 20000

        def rgcn_gate_layer(x, row, col, edge_type, basis, att, gate_w, root, bias):
            H = x.shape[1]
            w = jnp.einsum('rb,bio->rio', att, basis)
            x_j = x[col]
            msgs = []
            for r in range(NUM_RELATIONS):
                gate = jax.nn.sigmoid(x_j @ gate_w[r, :, 0])
                msgs.append(gate[:, None] * x_j @ w[r])
            msg = jnp.where((edge_type == 0)[:, None], msgs[0], msgs[1])
            agg = jax.ops.segment_sum(msg, row, num_segments=x.shape[0])
            return agg + x @ root + bias
        row, col = (edge_index[0], edge_index[1])
        h = jax.nn.relu(rgcn_gate_layer(x, row, col, edge_type, basis1, att1, gate_w1, root1, bias1))
        out = rgcn_gate_layer(h, row, col, edge_type, basis2, att2, gate_w2, root2, bias2)
        return out

    def _L3_gnn_ref(h, edge_index, W1, b1, W2, b2):
        import jax, jax.numpy as jnp
        import numpy as np
        N_NODES = 1250
        N_EDGES = 20000
        D = 512
        send, rec = (edge_index[0], edge_index[1])
        agg = jax.ops.segment_sum(h[send], rec, num_segments=h.shape[0])
        x = h + agg
        x = jax.nn.relu(x @ W1 + b1)
        x = x @ W2 + b2
        return x
    edge_index = jnp.stack([src, dst])
    x = _layernorm(x + _L0_gnn_ref(x, edge_index, L0_gnn_W, L0_gnn_b, L0_gnn_gamma, L0_gnn_beta), axis=-1)
    x = _layernorm(x + _L1_gnn_ref(x, src, dst, L1_gnn_W_self1, L1_gnn_W_neigh1, L1_gnn_b1, L1_gnn_W_self2, L1_gnn_W_neigh2, L1_gnn_b2), axis=-1)
    x = _layernorm(x + _L2_gnn_ref(x, edge_index, edge_type_2, L2_gnn_basis1, L2_gnn_att1, L2_gnn_gate_w1, L2_gnn_root1, L2_gnn_bias1, L2_gnn_basis2, L2_gnn_att2, L2_gnn_gate_w2, L2_gnn_root2, L2_gnn_bias2), axis=-1)
    x = _layernorm(x + _L3_gnn_ref(x, edge_index, L3_gnn_W1, L3_gnn_b1, L3_gnn_W2, L3_gnn_b2), axis=-1)
    return x

_drawn_inputs = setup_inputs


def setup_inputs(seed=0):
    import zlib

    import numpy as np

    out = dict(_drawn_inputs(seed))
    spreads = {'L0_gnn_b': (0.0, 0.8),
     'L0_gnn_gamma': (1.0, 0.2),
     'L0_gnn_beta': (0.0, 0.1),
     'L1_gnn_b1': (0.0, 0.1),
     'L1_gnn_b2': (0.0, 0.1),
     'L3_gnn_b1': (0.0, 0.535),
     'L3_gnn_b2': (0.0, 0.394)}
    factors = {'L2_gnn_basis1': 8.0,
     'L2_gnn_att1': 8.0,
     'L2_gnn_gate_w1': 8.0,
     'L2_gnn_root1': 8.0,
     'L2_gnn_bias1': 8.0,
     'L2_gnn_basis2': 8.0,
     'L2_gnn_att2': 8.0,
     'L2_gnn_gate_w2': 8.0,
     'L2_gnn_root2': 4.6,
     'L2_gnn_bias2': 4.896}
    for name, (base, spread) in spreads.items():
        noise = np.random.default_rng([zlib.crc32(name.encode()), seed]).standard_normal(out[name].shape)
        drawn = base * np.exp(spread * noise) if base else spread * noise
        out[name] = jnp.asarray(drawn.astype(out[name].dtype))
    for name, factor in factors.items():
        out[name] = (out[name] * factor).astype(out[name].dtype)
    return out
```

```python
import concourse.bass as bass
from concourse import mybir
from contextlib import ExitStack
import numpy as np

N, D, E = 1250, 512, 21250
REL, BASES = 2, 30
P = 128
NT = -(-N // P)
NP = NT * P
LAST = N - (NT - 1) * P
KT = D // P
WIN = 64
NWIN = NP // WIN
CHUNKS = 172
PAD = 4000
TYPE_STEP = 4096
EPS = 1e-5
LN_SCALE = 512.0
TOP = 2.0 ** 14

UNITS = [
    dict(mats=["W0"], nz=1, own=None, zexp=24, bias=None, ln=True),
    dict(mats=["Wn1", "Ws1"], nz=1, own=1, zexp=18, bias="b1", ln=False),
    dict(mats=["Wn2", "Ws2"], nz=1, own=1, zexp=24, bias="b2", ln=True),
    dict(mats=["acc0", "acc1", "root1"], nz=2, own=2, zexp=18, bias="rb1", ln=False),
    dict(mats=["acc0", "acc1", "root2"], nz=2, own=2, zexp=24, bias="rb2", ln=True),
    dict(mats=["V1"], nz=1, own=0, zexp=18, bias="vb1", ln=False),
    dict(mats=["V2"], nz=0, own=0, zexp=0, bias="vb2", ln=True),
]


def resnorm_gnn_kernel(nc, x, src_t, dst_t, typ_t, dst_r, W0, b0, gamma, beta,
                       Ws1, Wn1, b1, Ws2, Wn2, b2,
                       basis1, att1, gate1, root1, rb1, basis2, att2, gate2, root2, rb2,
                       V1, vb1, V2, vb2, out, xres):
    f32, f16, i32 = mybir.dt.float32, mybir.dt.float16, mybir.dt.int32
    ALU, ACT, AX = mybir.AluOpType, mybir.ActivationFunctionType, mybir.AxisListType
    RMAX = bass.bass_isa.ReduceOp.max
    dram = dict(W0=W0, Wn1=Wn1, Ws1=Ws1, Wn2=Wn2, Ws2=Ws2, root1=root1, root2=root2, V1=V1, V2=V2,
                b1=b1, b2=b2, rb1=rb1, rb2=rb2, vb1=vb1, vb2=vb2)
    NU = len(UNITS)
    ctx = ExitStack()
    with ctx:
        def sb(name, shape, dt):
            return ctx.enter_context(nc.sbuf_tensor(name, shape, dt))

        def sem(name):
            return ctx.enter_context(nc.semaphore(name))

        A = sb("A", [P, REL, NT, NP], f16)
        AT = sb("AT", [P, NT, NP], f16)
        S = sb("S", [P, NT, D], f32)
        S16 = S[:, :, :].bitcast(f16)
        Zraw = sb("Zraw", [P, REL * 2 * NT * D], f16)
        Z = Zraw[:, :].rearrange("p (r h t d) -> p r h t d", r=REL, h=2, t=NT)
        hT = sb("hT", [P, 2, 2, D], f16)
        W = sb("W", [P, 3, 2, KT, D], f16)
        acc = sb("acc", [P, REL, KT, D], f32)
        stage = sb("stage", [P, 2, 2, D], f32)
        w1 = sb("w1", [P, 2, D], f32)
        w2 = sb("w2", [P, 2, D], f32)
        xr = sb("xr", [P, 2, D], f32)
        bias = sb("bias", [P, D], f32)
        gw = sb("gw", [P, REL, D], f32)
        ident = sb("ident", [P, P], f16)
        att = sb("att", [P, REL, BASES], f32)
        dg = sb("dg", [P, REL, NT], f32)
        dout = sb("dout", [P, NT], f32)
        deg = sb("deg", [P, NT], f32)
        rdeg = sb("rdeg", [P, NT], f32)
        dinv = sb("dinv", [P, NT], f32)
        zsc0 = sb("zsc0", [P, NT], f32)
        zsc = sb("zsc", [P, REL, NT], f32)
        aggc = sb("aggc", [P, NU, NT], f32)
        mcol = sb("mcol", [P, 8], f32)
        mw = sb("mw", [P, 2], f32)
        mwg = sb("mwg", [P, NU], f32)
        mb = sb("mb", [P, 1], f32)
        gin = sb("gin", [P, 3], f32)
        gmax = sb("gmax", [P, 3], f32)
        sW = sb("sW", [P, NU], f32)
        iW = sb("iW", [P, NU], f32)
        s_in = sb("s_in", [P, NU], f32)
        i_in = sb("i_in", [P, NU], f32)
        ownc = sb("ownc", [P, NU], f32)
        tmpc = sb("tmpc", [P, 4], f32)
        stt = sb("stt", [P, 2, 6], f32)
        mv = sb("mv", [P, NT, 2], f32)
        mvr = sb("mvr", [P, 2, 2], f32)
        glr = sb("glr", [P, 2, REL], f32)
        sd = sb("sd", [P, NT], f32)
        rs = sb("rs", [P, NT], f32)
        rsl = sb("rsl", [P, NT], f32)
        glog = sb("glog", [P, REL, NT], f32)
        gate = sb("gate", [P, REL, NT], f32)
        epsc = sb("epsc", [P, 1], f32)
        tbl = sb("tbl", [1, NWIN, 4], i32)

        at = [0]

        def zview(nbytes):
            a = at[0]
            at[0] += nbytes // 2
            return Zraw[:, a:at[0]]

        oh_src = [zview(2 * NP) for _ in range(2)]
        oh_dst = [zview(2 * P) for _ in range(2)]
        iota_n = zview(2 * NP)
        iota_w = zview(4 * P).bitcast(f32)
        negw = zview(4 * NWIN).bitcast(f32)
        src_i, dst_i, typ_i = (zview(4 * CHUNKS).bitcast(i32) for _ in range(3))
        src_f, key_f = (zview(4 * CHUNKS).bitcast(f32) for _ in range(2))
        HC = CHUNKS // 2
        dstr = zview(4 * 2 * P).bitcast(i32).rearrange("p (g e) -> p g e", g=2)
        wlo = zview(4 * NWIN).bitcast(f32)
        whi = zview(4 * NWIN).bitcast(f32)
        cid = zview(4 * 4).bitcast(f32)
        mnx = zview(4 * 4).bitcast(f32)
        fl = zview(4 * 2 * NWIN).bitcast(f32)
        rng = zview(4 * 2 * NWIN).bitcast(f32)
        rngr = zview(4 * 2 * NWIN).bitcast(f32)
        w_st = zview(4 * NWIN).bitcast(f32)
        w_n = zview(4 * NWIN).bitcast(i32)
        w_c = [zview(4 * NWIN).bitcast(f32) for _ in range(2)]
        at[0] = 2 * NT * D
        b0b, gamb, betb, mean, bnsc, csum, csq = (zview(4 * D).bitcast(f32) for _ in range(7))
        onesn = zview(4 * P).bitcast(f32)
        assert at[0] <= REL * 2 * NT * D

        T = ctx.enter_context(nc.psum_tensor("T", [P, 2, D], f32))
        Dp = ctx.enter_context(nc.psum_tensor("Dp", [P, 2, 3, D], f32))
        Df = Dp[:, :, :, :].rearrange("p a j d -> p a (j d)")

        e_src, e_dst, e_typ, e_row, e_x = (sem(n) for n in ("e_src", "e_dst", "e_typ", "e_row", "e_x"))
        s_const = sem("s_const")
        s_chain = sem("s_chain")
        s_carry_pool, s_carry_dve = sem("s_carry_pool"), sem("s_carry_dve")
        s_pch = sem("s_pch")
        LN = [u for u in range(NU) if UNITS[u]["ln"]]
        s_rng = sem("s_rng")
        s_rngr = sem("s_rngr")
        s_tbl = sem("s_tbl")
        s_oh = sem("s_oh")
        s_ohu = sem("s_ohu")
        s_win = sem("s_win")
        s_wev = sem("s_wev")
        s_at = sem("s_at")
        s_ate = sem("s_ate")
        s_gin = sem("s_gin")
        s_gmax = sem("s_gmax")
        s_dsq = sem("s_dsq")
        s_att = [sem("s_att0"), sem("s_att1")]
        st_full = [sem("st_full0"), sem("st_full1")]
        st_free = sem("st_free")
        s_bias = sem("s_bias")
        s_gw = sem("s_gw")
        s_bn = sem("s_bn")
        s_mw = sem("s_mw")
        s_mwr = sem("s_mwr")
        s_sW = sem("s_sW")
        s_whi = sem("s_whi")
        s_wlo = sem("s_wlo")
        s_t = sem("s_t")
        s_hT = sem("s_hT")
        s_d = sem("s_d")
        s_ready = {u: sem(f"s_ready{u}") for u in range(NU)}
        s_zhi = {u: sem(f"s_zhi{u}") for u in range(6)}
        s_zlo = {u: sem(f"s_zlo{u}") for u in range(6)}
        s_own = {u: sem(f"s_own{u}") for u in range(1, 7)}
        s_agg = {u: sem(f"s_agg{u}") for u in range(6)}
        s_pre = {u: sem(f"s_pre{u}") for u in range(1, 6)}
        s_v = {u: sem(f"s_v{u}") for u in LN}
        s_bs = {u: sem(f"s_bs{u}") for u in LN}
        s_mv = {u: sem(f"s_mv{u}") for u in LN}
        s_sd = {u: sem(f"s_sd{u}") for u in LN}
        s_rs = {u: sem(f"s_rs{u}") for u in LN[1:]}
        s_rsl = {u: sem(f"s_rsl{u}") for u in LN[1:]}
        s_r = {u: sem(f"s_r{u}") for u in range(NU)}
        s_hi = {u: sem(f"s_hi{u}") for u in range(6)}
        s_xs = {u: sem(f"s_xs{u}") for u in LN[:3]}
        s_gl = {u: sem(f"s_gl{u}") for u in (2, 3)}
        s_xl = {u: [sem(f"s_xl{u}_{j}") for j in range(2)] for u in (0, 2, 4, 6)}
        s_xst = {u: [sem(f"s_xst{u}_{j}") for j in range(2)] for u in (0, 2, 4, 6)}
        s_gt = {u: sem(f"s_gt{u}") for u in (3, 4)}
        s_gz = {u: sem(f"s_gz{u}") for u in (0, 3, 4)}
        b_h, b_sum, b_mean, b_meanc, b_c, b_sq, b_q, b_var, b_sd, b_rc, b_sc = (
            sem("b_" + n) for n in ("h", "sum", "mean", "meanc", "c", "sq", "q", "var", "sd", "rc", "sc"))
        b_n1, b_n2, b_g = sem("b_n1"), sem("b_n2"), sem("b_g")

        ds = bass.ds

        def wait(eng, s, n):
            if not isinstance(n, int) or n > 0:
                eng.wait_ge(s, n)

        def tile_moved(eng, s, t, j):
            if not isinstance(t, int) or t >= 0:
                eng.wait_ge(s[j], (t + (2 - j)) * 8)

        def pairs_of_tiles(eng, body, peel_last=False):
            body(0, 0)
            body(1, 1)
            with eng.Fori(2, (NT - 2 if peel_last else NT) - 1, 2) as i:
                body(i, 0)
                body(i + 1, 1)
            if peel_last:
                body(NT - 2, 0)
                body(NT - 1, 1)

        def stage_plan():
            plan, n = [], 0
            for u, unit in enumerate(UNITS):
                if "acc0" in unit["mats"]:
                    plan.append(("basis", u, n))
                    n += 2 * BASES
                plain = [m for m in unit["mats"] if m[:3] != "acc"]
                plan.append(("max", u, n))
                n += 2 * len(plain)
                plan.append(("split", u, n))
                n += 2 * len(plain)
            return {(kind, u): n for kind, u, n in plan}

        PLAN = stage_plan()

        def plain_mats(u):
            return [m for m in UNITS[u]["mats"] if m[:3] != "acc"]

        def halves_split(u):
            return sum(2 * len(v["mats"]) for v in UNITS[:u + 1])

        block = ctx.enter_context(nc.Block())

        @block.sync
        def _(sp):
            sp.dma_start(dstr[0:HC, :, :], dst_r).then_inc(e_row, 16)
            sp.dma_start(dst_i, dst_t).then_inc(e_dst, 16)
            sp.dma_start(typ_i, typ_t).then_inc(e_typ, 16)
            sp.dma_start(src_i, src_t).then_inc(e_src, 16)
            sp.wait_ge(s_const, 1)
            sp.dma_start(S[:, 0:NT - 1, :], x[0:(NT - 1) * P, :].rearrange("(t p) d -> p t d", p=P)).then_inc(e_x, 16)
            sp.dma_start(S[0:LAST, NT - 1, :], x[(NT - 1) * P:N, :]).then_inc(e_x, 16)
            for tile, vec in ((b0b, b0), (gamb, gamma), (betb, beta)):
                sp.dma_start(tile, vec.rearrange("(a d) -> a d", a=1).broadcast_to([P, D])).then_inc(s_bn, 16)

            def load_half(n, m, h):
                wait(sp, st_free, n - 1)
                sp.dma_start(stage[:, n % 2, :, :],
                             m[2 * h * P:2 * (h + 1) * P, :].rearrange("(q p) d -> p q d", p=P)).then_inc(st_full[n % 2], 16)

            for u, unit in enumerate(UNITS):
                if unit["mats"][0] == "acc0":
                    basis, at_d = (basis1, att1) if u == 3 else (basis2, att2)
                    L = 0 if u == 3 else 1
                    if L:
                        sp.wait_ge(s_wlo, halves_split(3))
                    sp.dma_start(att[:, :, :].rearrange("p r b -> p (r b)"),
                                 at_d.rearrange("(a r) b -> a (r b)", a=1).broadcast_to([P, REL * BASES])).then_inc(s_att[L], 16)
                    base = PLAN["basis", u]
                    for h in range(2):
                        with sp.Fori(0, BASES - 1, 2) as b:
                            for j in range(2):
                                sp.wait_ge(st_free, b + (base + h * BASES + j - 1))
                                sp.dma_start(stage[:, j, :, :],
                                             basis[ds(b + j, 1), 2 * h * P:2 * (h + 1) * P, :]
                                             .rearrange("a (q p) d -> p (a q) d", p=P)).then_inc(st_full[j], 16)
                for kind in ("max", "split"):
                    n = PLAN[kind, u]
                    for m in plain_mats(u):
                        for h in range(2):
                            load_half(n, dram[m], h)
                            n += 1
                    if kind == "max" and unit["bias"]:
                        if u >= 2:
                            sp.wait_ge(s_own[u - 1], NT)
                        sp.dma_start(bias[:, :], dram[unit["bias"]].rearrange("(a d) -> a d", a=1)
                                     .broadcast_to([P, D])).then_inc(s_bias, 16)
                if u in (2, 3):
                    g = gate1 if u == 2 else gate2
                    if u == 3:
                        sp.wait_ge(s_gl[2], 3 * NT)
                    for r in range(REL):
                        sp.dma_start(gw[:, r, :], g[r:r + 1, :, 0].broadcast_to([P, D])).then_inc(s_gw, 16)

        @block.gpsimd
        def _(pool):
            pool.memset(S[:, NT - 1, :], 0.0).then_inc(s_const, 1)
            pool.memset(ident[:, :], 0.0).then_inc(s_pch, 1)
            pool.wait_ge(s_pch, 1)
            pool.affine_select(out=ident[:, :], in_=ident[:, :], compare_op=ALU.not_equal, fill=1.0, base=0,
                               pattern=[[-1, P]], channel_multiplier=1).then_inc(s_const, 1)
            kw = dict(allow_small_or_imprecise_dtypes=True)
            pool.iota(iota_n, [[1, NP]], base=0, channel_multiplier=0, **kw).then_inc(s_const, 1)
            pool.iota(iota_w, [[TYPE_STEP, REL], [1, WIN]], base=0, channel_multiplier=0, **kw).then_inc(s_const, 1)
            pool.iota(negw, [[-WIN, NWIN]], base=0, channel_multiplier=0, **kw).then_inc(s_const, 1)
            pool.iota(wlo, [[WIN, NWIN]], base=0, channel_multiplier=0, **kw).then_inc(s_const, 1)
            pool.iota(whi, [[WIN, NWIN]], base=WIN - 1, channel_multiplier=0, **kw).then_inc(s_const, 1)
            pool.iota(cid[:, 0:2], [[-1, 2]], base=256, channel_multiplier=-2, **kw).then_inc(s_const, 1)
            pool.iota(cid[:, 2:4], [[1, 2]], base=1, channel_multiplier=2, **kw).then_inc(s_const, 1)
            pool.memset(rng, 0.0).then_inc(s_const, 1)
            pool.memset(epsc[:, :], EPS).then_inc(s_const, 1)
            pool.memset(onesn, 1.0 / N).then_inc(s_const, 1)
            pool.memset(csum, 0.0).then_inc(s_const, 1)
            pool.memset(csq, 0.0).then_inc(s_const, 1)
            pool.wait_ge(s_rng, 1)
            pool.partition_all_reduce(rngr, rng, P, RMAX).then_inc(s_rngr, 1)
            pool.wait_ge(s_gin, 1)
            pool.partition_all_reduce(gmax[:, :], gin[:, :], P, RMAX).then_inc(s_gmax, 1)

            def reduce_weights(u):
                pool.wait_ge(s_mw, u + 1)
                pool.partition_all_reduce(mwg[:, u:u + 1], mw[:, u % 2:u % 2 + 1], P, RMAX).then_inc(s_mwr, 1)

            def load_x(u, t, j):
                source = x if u == 0 else xres
                rows = P if u > 0 or not (isinstance(t, int) and t == NT - 1) else LAST
                pool.sem_inc(s_carry_pool, 1)
                pool.dma_start(xr[0:rows, j, :], source[ds(t * P, rows), :]).then_inc(s_xl[u][j], 16)

            def low_part(u, t, j):
                r = w1 if UNITS[u]["ln"] else w2
                pool.wait_ge(s_hi[u], t + 1)
                pool.tensor_tensor(S16[:, ds(t, 1), D:2 * D], r[:, j:j + 1, :], S16[:, ds(t, 1), 0:D],
                                   ALU.subtract).then_inc(s_ready[u + 1], 1)

            reduce_weights(0)
            reduce_weights(1)
            for src, dst_, ready, done in ((lambda t: S[:, t, :], csum, b_h, b_sum),
                                           (lambda t: w1[:, t % 2, :], csq, b_sq, b_q)):
                for t in range(NT):
                    rows = P if t < NT - 1 else LAST
                    pool.wait_ge(ready, t + 1)
                    wait(pool, done, t)
                    pool.tensor_tensor(dst_[0:rows, :], dst_[0:rows, :], src(t)[0:rows, :], ALU.add).then_inc(done, 1)
            for t in range(NT):
                wait(pool, s_v[0], t - 1)
                load_x(0, t, t % 2)
            for t in range(NT):
                low_part(0, t, t % 2)
                pool.wait_ge(s_xs[0], t + 1)
                pool.dma_start(xres[t * P:(t + 1) * P, :], w2[:, t % 2, :]).then_inc(s_xst[0][t % 2], 16)
            for u in range(1, 6):
                if u < 6:
                    reduce_weights(u + 1)
                if UNITS[u]["ln"]:
                    for j in range(2):
                        pool.wait_ge(s_xst[u - 2][j], 8 * NT)

                    if u == 4:
                        pool.wait_ge(s_gl[3], 3 * NT)

                    def body(t, j):
                        if u == 2:
                            wait(pool, s_gl[2], 3 * t - 3)
                        else:
                            wait(pool, s_v[u], t - 1)
                        load_x(u, t, j)
                        if not isinstance(t, int) or t > 0:
                            store(t - 1, 1 - j)

                    def store(t, j):
                        low_part(u, t, j)
                        pool.wait_ge(s_xs[u], t + 1)
                        pool.sem_inc(s_carry_pool, 1)
                        pool.dma_start(xres[ds(t * P, P), :], w2[:, j, :]).then_inc(s_xst[u][j], 16)

                    pairs_of_tiles(pool, body)
                    store(NT - 1, 1)
                else:
                    pairs_of_tiles(pool, lambda t, j: low_part(u, t, j))
            for j in range(2):
                pool.wait_ge(s_xst[4][j], 8 * NT)

            def last(t, j):
                wait(pool, s_v[6], t - 1)
                load_x(6, t, j)
                if not isinstance(t, int) or t > 0:
                    pool.wait_ge(s_r[6], t)
                    pool.sem_inc(s_carry_pool, 1)
                    pool.dma_start(out[ds(t * P - P, P), :], w1[:, 1 - j, :]).then_inc(s_xst[6][1 - j], 16)

            pairs_of_tiles(pool, last)
            pool.wait_ge(s_r[6], NT)
            pool.dma_start(out[(NT - 1) * P:N, :], w1[0:LAST, 1, :]).then_inc(s_xst[6][1], 16)
            for j in range(2):
                pool.wait_ge(s_xst[6][j], 8 * NT)

        @block.tensor
        def _(pe):
            def chunk_product(n, j, slot, start, stop):
                pe.wait_ge(s_oh, 2 * n + 2)
                for c in range(0, NP, D):
                    w = min(D, NP - c)
                    last = nc.tensor.matmul(Df[:, j, c:c + w], oh_dst[slot], oh_src[slot][:, c:c + w],
                                            start=start, stop=stop)
                last.then_inc(s_win if stop else s_ohu, 1)

            def window(w, j):
                row = tbl[0:1, ds(w, 1), :]
                np_ = pe.value_load(row[:, :, 1:2], min_val=3, max_val=CHUNKS)
                base = pe.value_load(row[:, :, 2:3], min_val=0, max_val=NWIN * CHUNKS)
                final = pe.value_load(row[:, :, 3:4], min_val=0, max_val=NWIN * CHUNKS)
                wait(pe, s_wev, 2 * w - 2)
                for s in range(2):
                    chunk_product(base * 2 + s, j, s, True if s == 0 else False, False)
                with pe.Fori(1, np_ - 1) as i:
                    for s in range(2):
                        chunk_product((base + i) * 2 + s, j, s, False, False)
                for s in range(2):
                    chunk_product(final * 2 + s, j, s, False, s == 1)
                pe.wait_ge(s_win, w + 1)
                pe.sem_inc(s_ohu, 1)

            pe.sem_inc(s_ohu, 2)
            pe.wait_ge(s_tbl, 1)
            window(0, 0)
            window(1, 1)
            with pe.Fori(2, NWIN - 1, 2) as w:
                window(w, 0)
                window(w + 1, 1)

            pe.wait_ge(s_wev, 2 * NWIN)

            def transpose_counts(m, j):
                wait(pe, s_ate, m - 1)
                for t in range(NT):
                    for r in range(REL):
                        last = nc.tensor.matmul(Df[:, j, t * P:(t + 1) * P], A[:, r, t, ds(m * P, P)], ident[:, :],
                                                start=(r == 0), stop=(r == REL - 1))
                last.then_inc(s_at, 1)

            pairs_of_tiles(pe, transpose_counts)

            for u, unit in enumerate(UNITS):
                nm, nz = len(unit["mats"]), unit["nz"]

                def turn(t, j):
                    pe.wait_ge(s_ready[u], t + 1)
                    wait(pe, s_hT, t + NT * u)
                    for h in range(2):
                        for k in range(KT):
                            last = nc.tensor.matmul(T[:, h, k * P:(k + 1) * P],
                                                    S16[:, ds(t, 1), h * D + k * P:h * D + (k + 1) * P]
                                                    .rearrange("p a c -> p (a c)"), ident[:, :], start=True, stop=True)
                    last.then_inc(s_t, 1)

                def dense(t, j):
                    if not (isinstance(t, int) and t == NT - 1):
                        turn(t + 1, 1 - j)
                    pe.wait_ge(s_hT, t + NT * u + 1)
                    if nz:
                        wait(pe, s_zlo[u], (t - 1) * nz)
                    if unit["own"] is not None:
                        wait(pe, s_own[u], t - 1)
                    if isinstance(t, int) and t < 2 and nm == 3:
                        pe.wait_ge(s_pre[u - 1], NT - 1 + t)
                    for m in range(nm):
                        n = 0
                        for hp, wp in ((0, 0), (1, 0), (0, 1)):
                            for k in range(KT):
                                last = nc.tensor.matmul(Dp[:, j, m, :], hT[:, j, hp, k * P:(k + 1) * P],
                                                        W[:, m, wp, k, :], start=(n == 0), stop=(n == 3 * KT - 1))
                                n += 1
                    last.then_inc(s_d, 1)

                def agg(t, j):
                    wait(pe, s_pre[u] if u else b_h, t - 1)
                    rels = [(A[:, r], r) for r in range(REL)] if nz == 2 else [(AT, 0)]
                    n, count = 0, 2 * NT * nz
                    dstp = Dp[:, j, 2, :]
                    for a, r in rels:
                        for k in range(NT):
                            if isinstance(t, int) and t == 0:
                                pe.wait_ge(s_zlo[u], (k + 1) * nz)
                            for h in range(2):
                                last = nc.tensor.matmul(dstp, a[:, k, ds(t * P, P)], Z[:, r, h, k, :],
                                                        start=(n == 0), stop=(n == count - 1 and u > 0))
                                n += 1
                    if u == 0:
                        for h in range(2):
                            last = nc.tensor.matmul(dstp, ident[:, :],
                                                    Z[:, 0, h, ds(t, 1), :].rearrange("p a d -> p (a d)"),
                                                    start=False, stop=(h == 1))
                    last.then_inc(s_agg[u], 1)

                pe.wait_ge(s_wlo, halves_split(u))
                turn(0, 0)
                pairs_of_tiles(pe, dense, peel_last=True)
                if nz:
                    if unit["own"] is not None:
                        pe.wait_ge(s_own[u], NT)
                    pairs_of_tiles(pe, agg)
                if u == 0:
                    for total, ready, done in ((csum, b_sum, b_mean), (csq, b_q, b_var)):
                        pe.wait_ge(ready, NT)
                        if total is csq:
                            pe.wait_ge(b_meanc, 1)
                        nc.tensor.matmul(T[:, 0, :], onesn, total, start=True, stop=True).then_inc(done, 1)

        @block.scalar
        def _(act):
            def window_out(w, j, t):
                act.wait_ge(s_win, w + 1)
                for r in range(REL):
                    nc.scalar.activation(A[WIN * j:WIN * (j + 1), r, ds(t, 1), :],
                                         Dp[WIN * r:WIN * (r + 1), j, :, :].rearrange("p j d -> p (j d)")[:, 0:NP],
                                         ACT.Copy, accum_out=dg[WIN * j:WIN * (j + 1), r, ds(t, 1)]).then_inc(s_wev, 1)

            with act.Fori(0, NT) as t:
                window_out(t * 2, 0, t)
                window_out(t * 2 + 1, 1, t)

            def counts_out(m, j):
                act.wait_ge(s_at, m + 1)
                nc.scalar.activation(AT[:, ds(m, 1), :], Df[:, j, 0:NP], ACT.Copy,
                                     accum_out=dout[:, ds(m, 1)]).then_inc(s_ate, 1)

            pairs_of_tiles(act, counts_out)
            act.wait_ge(s_dsq, 1)
            nc.scalar.activation(dinv[:, :], dinv[:, :], ACT.Sqrt).then_inc(s_dsq, 1)

            def split_weights(u):
                act.wait_ge(s_sW, u + 1)
                n = PLAN["split", u]
                for m, name in enumerate(UNITS[u]["mats"]):
                    for h in range(2):
                        if name[:3] == "acc":
                            source = acc[:, m, 2 * h:2 * h + 2, :]
                        else:
                            act.wait_ge(st_full[n % 2], 16 * (n // 2 + 1))
                            source = stage[:, n % 2, :, :]
                            n += 1
                        nc.scalar.activation(W[:, m, 0, 2 * h:2 * h + 2, :], source, ACT.Copy,
                                             scale=sW[:, u:u + 1]).then_inc(s_whi, 1)

            act.wait_ge(s_gz[0], 1)
            for t in range(NT):
                wait(act, s_ready[0], t - 1)
                nc.scalar.activation(w1[:, t % 2, :], S[:, t, :], ACT.Copy, scale=s_in[:, 0:1]).then_inc(b_n1, 1)
                act.wait_ge(b_n1, t + 1)
                nc.scalar.activation(S16[:, t, 0:D], w1[:, t % 2, :], ACT.Copy).then_inc(b_n2, 1)
            split_weights(0)

            for u, unit in enumerate(UNITS):
                nz = unit["nz"]

                def hT_out(t, j):
                    act.wait_ge(s_t, t + NT * u + 1)
                    wait(act, s_d, t + NT * u - 1)
                    nc.scalar.activation(hT[:, j, :, :], T[:, :, :], ACT.Copy).then_inc(s_hT, 1)

                def ln_step(t, j):
                    act.wait_ge(s_mv[u], t + 1)
                    nc.scalar.activation(sd[:, ds(t, 1)], mvr[:, j, 1:2], ACT.Sqrt,
                                         bias=epsc[:, 0:1]).then_inc(s_sd[u], 1)
                    if u < NU - 1:
                        act.wait_ge(s_r[u], t + 1)
                        nc.scalar.activation(S16[:, ds(t, 1), 0:D], w1[:, j:j + 1, :], ACT.Copy).then_inc(s_hi[u], 1)
                        nc.scalar.activation(w2[:, j, :], w1[:, j, :], ACT.Copy, scale=1.0 / LN_SCALE).then_inc(s_xs[u], 1)

                def z_out(t, j):
                    if not (isinstance(t, int) and t == NT - 1):
                        hT_out(t + 1, 1 - j)
                    if not nz:
                        ln_step(t, j)
                        return
                    act.wait_ge(s_d, t + NT * u + 1)
                    for r in range(nz):
                        if u == 0:
                            scale = zsc0[:, ds(t, 1)]
                        elif nz == 2:
                            scale = zsc[:, r, ds(t, 1)]
                        else:
                            scale = 2.0 ** -unit["zexp"]
                        nc.scalar.activation(Z[:, r, 0, ds(t, 1), :], Dp[:, j, r:r + 1, :], ACT.Copy,
                                             scale=scale).then_inc(s_zhi[u], 1)

                if nz == 2:
                    act.wait_ge(s_gl[u - 1], 3 * NT)
                    nc.scalar.activation(gate[:, :, :], glog[:, :, :], ACT.Sigmoid,
                                         scale=i_in[:, u:u + 1]).then_inc(s_gt[u], 1)
                    act.wait_ge(s_gz[u], 1)
                hT_out(0, 0)
                pairs_of_tiles(act, z_out, peel_last=True)
                if u + 1 < NU:
                    split_weights(u + 1)

                def relu_step(t, j):
                    act.wait_ge(s_pre[u], t + 1)
                    wait(act, s_ready[u + 1], t - 1)
                    if u == 3:
                        wait(act, s_gl[3], 3 * t - 3)
                    nc.scalar.activation(w2[:, j, :], w1[:, j, :], ACT.Relu, scale=s_in[:, u + 1:u + 2]).then_inc(s_r[u], 1)
                    nc.scalar.activation(S16[:, ds(t, 1), 0:D], w1[:, j:j + 1, :], ACT.Relu,
                                         scale=s_in[:, u + 1:u + 2]).then_inc(s_hi[u], 1)

                if u == 0:
                    for t in range(NT):
                        act.wait_ge(b_c, t + 1)
                        wait(act, b_q, t - 1)
                        nc.scalar.activation(w1[:, t % 2, :], S[:, t, :], ACT.Square).then_inc(b_sq, 1)
                    act.wait_ge(b_var, 1)
                    nc.scalar.activation(bnsc, T[:, 0, :], ACT.Sqrt, bias=epsc[:, 0:1]).then_inc(b_sd, 1)
                    for t in range(NT):
                        act.wait_ge(b_n2, NT + t + 1)
                        wait(act, s_v[0], t - 1)
                        nc.scalar.activation(w2[:, t % 2, :], w1[:, t % 2, :], ACT.Gelu).then_inc(b_g, 1)
                    act.wait_ge(s_mv[0], NT)
                    nc.scalar.activation(sd[:, :], mv[:, :, 1], ACT.Sqrt, bias=epsc[:, 0:1]).then_inc(s_sd[0], 1)
                    for t in range(NT):
                        act.wait_ge(s_r[0], t + 1)
                        nc.scalar.activation(S16[:, t, 0:D], w1[:, t % 2, :], ACT.Copy).then_inc(s_hi[0], 1)
                        tile_moved(act, s_xst[0], t - 2, t % 2)
                        nc.scalar.activation(w2[:, t % 2, :], w1[:, t % 2, :], ACT.Copy,
                                             scale=1.0 / LN_SCALE).then_inc(s_xs[0], 1)
                elif unit["ln"]:
                    if nz:
                        pairs_of_tiles(act, ln_step)
                else:
                    for j in range(2):
                        act.wait_ge(s_xst[u - 1][j], 8 * NT)
                    pairs_of_tiles(act, relu_step)

        @block.vector
        def _(dve):
            v = nc.vector
            chain = [0]

            def link(ins):
                chain[0] += 1
                ins.then_inc(s_chain, 1)
                dve.wait_ge(s_chain, chain[0])

            dve.wait_ge(e_row, 16)
            dve.wait_ge(s_const, 14)
            v.tensor_reduce(mnx[0:HC, 0:2], dstr[0:HC, :, :], AX.X, ALU.min)
            link(v.tensor_reduce(mnx[0:HC, 2:4], dstr[0:HC, :, :], AX.X, ALU.max))
            for g in range(2):
                link(v.tensor_scalar(fl[0:HC, 0:NWIN], wlo[0:HC, :], mnx[0:HC, 2 + g:3 + g], None, ALU.is_le))
                link(v.scalar_tensor_tensor(fl[0:HC, NWIN:2 * NWIN], whi[0:HC, :], mnx[0:HC, g:g + 1],
                                            fl[0:HC, 0:NWIN], ALU.is_ge, ALU.mult))
                for q in range(2):
                    part = rng[0:HC, q * NWIN:(q + 1) * NWIN]
                    last = v.scalar_tensor_tensor(part, fl[0:HC, NWIN:2 * NWIN], cid[0:HC, 2 * q + g:2 * q + g + 1],
                                                  part, ALU.mult, ALU.max)
                    link(last)
            v.nop().then_inc(s_rng, 1)
            dve.wait_ge(e_typ, 16)
            dve.wait_ge(e_dst, 16)
            dve.wait_ge(e_src, 16)
            v.tensor_copy(src_f, src_i)
            link(v.tensor_copy(key_f, dst_i))
            link(v.scalar_tensor_tensor(key_f, typ_i, float(TYPE_STEP), key_f, ALU.mult, ALU.add))
            dve.wait_ge(s_rngr, 1)
            link(v.tensor_scalar(w_st, rngr[:, 0:NWIN], -1.0, 256.0, ALU.mult, ALU.add))
            link(v.tensor_scalar(w_st, w_st, float(CHUNKS - 6), None, ALU.min))
            link(v.scalar_tensor_tensor(w_c[0], rngr[:, NWIN:2 * NWIN], 1.0, w_st, ALU.add, ALU.subtract))
            link(v.tensor_scalar(w_n, w_c[0], 6.0, None, ALU.max))
            link(v.tensor_scalar(w_n, w_n, 1, None, ALU.logical_shift_right))
            link(v.tensor_copy(w_c[0], w_n))
            a = 0
            step = 1
            while step < NWIN:
                v.tensor_copy(w_c[1 - a][:, 0:step], w_c[a][:, 0:step])
                link(v.tensor_tensor(w_c[1 - a][:, step:NWIN], w_c[a][:, step:NWIN], w_c[a][:, 0:NWIN - step], ALU.add))
                a, step = 1 - a, 2 * step
            v.tensor_copy(tbl[0:1, :, 0], w_st[0:1, :])
            v.tensor_copy(tbl[0:1, :, 1], w_n[0:1, :])
            v.tensor_scalar(tbl[0:1, :, 3], w_c[a][0:1, :], -1.0, None, ALU.add)
            v.tensor_tensor(tbl[0:1, :, 2], w_c[a][0:1, :], w_n[0:1, :], ALU.subtract).then_inc(s_tbl, 1)
            dve.wait_ge(e_x, 32)
            v.tensor_reduce(gin[:, 2:3], S[:, :, :].rearrange("p t d -> p (t d)"), AX.X, ALU.max,
                            apply_absolute_value=True)
            dve.wait_ge(s_tbl, 1)

            def one_hots(n, c, w, slot):
                dve.wait_ge(s_ohu, n + 1)
                v.tensor_scalar(oh_dst[slot], iota_w, key_f[:, ds(c, 1)], negw[:, ds(w, 1)],
                                ALU.subtract, ALU.is_equal).then_inc(s_oh, 1)
                v.tensor_scalar(oh_src[slot], iota_n, src_f[:, ds(c, 1)], None, ALU.is_equal).then_inc(s_oh, 1)

            def window(w):
                row = tbl[0:1, ds(w, 1), :]
                st = dve.value_load(row[:, :, 0:1], min_val=0, max_val=CHUNKS - 6)
                np_ = dve.value_load(row[:, :, 1:2], min_val=3, max_val=CHUNKS // 2)
                base = dve.value_load(row[:, :, 2:3], min_val=0, max_val=NWIN * CHUNKS)
                with dve.Fori(0, np_) as i:
                    c = nc.s_assert_within(dve.snap(st + i * 2), 0, CHUNKS - 2, skip_runtime_bounds_check_because=
                                           "st <= CHUNKS - 6 and 2 * np_ <= chunks from st on, plus padding")
                    for s in range(2):
                        one_hots((base + i) * 2 + s, c + s, w, s)

            with dve.Fori(0, NWIN) as w:
                window(w)

            dve.wait_ge(s_wev, 2 * NWIN)
            link(v.tensor_tensor(deg[:, :], dg[:, 0, :], dg[:, 1, :], ALU.add))
            v.tensor_reduce(gin[:, 0:1], deg[:, :], AX.X, ALU.max)
            link(v.tensor_scalar(rdeg[:, :], deg[:, :], 1.0, None, ALU.max))
            link(v.tensor_scalar(dinv[:, :], deg[:, :], 1.0, None, ALU.add))
            link(v.reciprocal(rdeg[:, :], rdeg[:, :]))
            v.reciprocal(dinv[:, :], dinv[:, :]).then_inc(s_dsq, 1)
            dve.wait_ge(s_ate, NT)
            v.tensor_reduce(gin[:, 1:2], dout[:, :], AX.X, ALU.max).then_inc(s_gin, 1)
            dve.wait_ge(s_dsq, 2)
            link(v.tensor_scalar(zsc0[:, :], dinv[:, :], 2.0 ** -UNITS[0]["zexp"], None, ALU.mult))

            def power_scale(s, i, m):
                link(v.tensor_scalar(tmpc[:, 0:1], m, 1e-30, None, ALU.max))
                link(v.tensor_scalar(tmpc[:, 1:2].bitcast(i32), tmpc[:, 0:1].bitcast(i32), 0x7F800000, None,
                                     ALU.bitwise_and))
                link(v.tensor_scalar(i, tmpc[:, 1:2], 1.0 / TOP, None, ALU.mult))
                link(v.reciprocal(s, i))

            def weights_max(u):
                unit, k = UNITS[u], 0
                if unit["mats"][0] == "acc0":
                    L = 0 if u == 3 else 1
                    if L:
                        dve.wait_ge(s_whi, halves_split(3))
                    dve.wait_ge(s_att[L], 16)
                    link(v.memset(acc[:, :, :, :], 0.0))
                    base = PLAN["basis", u]
                    for h in range(2):
                        with dve.Fori(0, BASES - 1, 2) as b:
                            for j in range(2):
                                n0 = base + h * BASES
                                dve.wait_ge(st_full[j], b * 8 + (16 * (n0 // 2) + 16))
                                if h or j:
                                    dve.wait_ge(st_free, b + n0 + j)
                                else:
                                    dve.wait_ge(st_free, b + n0)
                                for r in range(REL):
                                    part = acc[:, r, 2 * h:2 * h + 2, :].rearrange("p q d -> p (q d)")
                                    last = v.scalar_tensor_tensor(part, stage[:, j, :, :].rearrange("p q d -> p (q d)"),
                                                                  att[:, r, ds(b + j, 1)], part, ALU.mult, ALU.add)
                                last.then_inc(st_free, 1)
                    dve.wait_ge(st_free, base + 2 * BASES)
                    for r in range(REL):
                        v.tensor_reduce(mcol[:, k:k + 1], acc[:, r, :, :].rearrange("p q d -> p (q d)"), AX.X, ALU.max,
                                        apply_absolute_value=True)
                        k += 1
                n = PLAN["max", u]
                for m in plain_mats(u):
                    for h in range(2):
                        dve.wait_ge(st_full[n % 2], 16 * (n // 2 + 1))
                        last = v.tensor_reduce(mcol[:, k:k + 1], stage[:, n % 2, :, :].rearrange("p q d -> p (q d)"),
                                               AX.X, ALU.max, apply_absolute_value=True)
                        last.then_inc(st_free, 1)
                        n, k = n + 1, k + 1
                dve.wait_ge(st_free, n)
                v.tensor_reduce(mw[:, u % 2:u % 2 + 1], mcol[:, 0:k], AX.X, ALU.max).then_inc(s_mw, 1)

            def scales(u):
                unit = UNITS[u]
                dve.wait_ge(s_mwr, u + 1)
                power_scale(sW[:, u:u + 1], iW[:, u:u + 1], mwg[:, u:u + 1])
                v.nop().then_inc(s_sW, 1)
                link(v.tensor_tensor(ownc[:, u:u + 1], i_in[:, u:u + 1], iW[:, u:u + 1], ALU.mult))
                if unit["nz"]:
                    up = 2.0 ** unit["zexp"]
                    if u in (1, 2):
                        link(v.tensor_scalar(aggc[:, u, :], rdeg[:, :], ownc[:, u:u + 1], up, ALU.mult, ALU.mult))
                    elif u == 0:
                        link(v.tensor_scalar(aggc[:, u, :], dinv[:, :], ownc[:, u:u + 1], up, ALU.mult, ALU.mult))
                    else:
                        link(v.tensor_scalar(aggc[:, u, 0:1], ownc[:, u:u + 1], up, None, ALU.mult))
                if unit["bias"]:
                    dve.wait_ge(s_bias, 16 * u)
                if unit["nz"] and not unit["ln"]:
                    link(v.tensor_reduce(mb[:, :], bias[:, :], AX.X, ALU.max, apply_absolute_value=True))
                    if u == 1:
                        link(v.tensor_scalar(tmpc[:, 2:3], mwg[:, u:u + 1], 2.0 * D, None, ALU.mult))
                    else:
                        g = 1 if u == 3 else 0
                        link(v.tensor_scalar(tmpc[:, 2:3], gmax[:, g:g + 1], 1.0, float(D), ALU.add, ALU.mult))
                        link(v.tensor_tensor(tmpc[:, 2:3], tmpc[:, 2:3], mwg[:, u:u + 1], ALU.mult))
                    link(v.tensor_tensor(tmpc[:, 3:4], tmpc[:, 2:3], mb[:, :], ALU.add))
                    power_scale(s_in[:, u + 1:u + 2], i_in[:, u + 1:u + 2], tmpc[:, 3:4])

            def split_low(u):
                n = PLAN["split", u]
                i = halves_split(u - 1)
                for m, name in enumerate(UNITS[u]["mats"]):
                    for h in range(2):
                        i += 1
                        dve.wait_ge(s_whi, i)
                        acc_mat = name[:3] == "acc"
                        source = acc[:, m, 2 * h:2 * h + 2, :] if acc_mat else stage[:, n % 2, :, :]
                        last = v.scalar_tensor_tensor(
                            W[:, m, 1, 2 * h:2 * h + 2, :].rearrange("p q d -> p (q d)"),
                            source.rearrange("p q d -> p (q d)"), sW[:, u:u + 1],
                            W[:, m, 0, 2 * h:2 * h + 2, :].rearrange("p q d -> p (q d)"), ALU.mult, ALU.subtract)
                        last.then_inc(s_wlo, 1)
                        if not acc_mat:
                            dve.wait_ge(s_wlo, i)
                            v.nop().then_inc(st_free, 1)
                            n += 1

            for u in (1, 3, 5):
                v.memset(s_in[:, u:u + 1], LN_SCALE)
                link(v.memset(i_in[:, u:u + 1], 1.0 / LN_SCALE))
            weights_max(0)
            dve.wait_ge(s_gmax, 1)
            power_scale(s_in[:, 0:1], i_in[:, 0:1], gmax[:, 2:3])
            v.nop().then_inc(s_gz[0], 1)
            scales(0)
            for t in range(NT):
                dve.wait_ge(b_n2, t + 1)
                v.tensor_tensor(S16[:, t, D:2 * D], w1[:, t % 2, :], S16[:, t, 0:D], ALU.subtract).then_inc(s_ready[0], 1)
            split_low(0)

            for u, unit in enumerate(UNITS):
                nz = unit["nz"]

                def z_low(t, j):
                    for r in range(nz):
                        if u == 0:
                            scale = zsc0[:, ds(t, 1)]
                        elif nz == 2:
                            scale = zsc[:, r, ds(t, 1)]
                        else:
                            scale = 2.0 ** -unit["zexp"]
                        dve.wait_ge(s_zhi[u], t * nz + (r + 1))
                        v.scalar_tensor_tensor(Z[:, r, 1, ds(t, 1), :], Dp[:, j, r:r + 1, :], scale,
                                               Z[:, r, 0, ds(t, 1), :], ALU.mult, ALU.subtract).then_inc(s_zlo[u], 1)
                    if nz and unit["own"] is not None:
                        o = unit["own"]
                        v.scalar_tensor_tensor(S[:, ds(t, 1), :], Dp[:, j, o:o + 1, :], ownc[:, u:u + 1],
                                               bias[:, :].rearrange("p (a d) -> p a d", a=1),
                                               ALU.mult, ALU.add).then_inc(s_own[u], 1)

                def stats(t, j):
                    dve.wait_ge(s_v[u], t + 1)
                    v.bn_stats(stt[:, j, :], w2[:, j, :]).then_inc(s_bs[u], 1)
                    dve.wait_ge(s_bs[u], t + 1)
                    dve.sem_inc(s_carry_dve, 1)
                    v.bn_aggr(mvr[:, j, :], stt[:, j, :]).then_inc(s_mv[u], 1)

                def normalize(t, j, scale, source):
                    dve.wait_ge(s_sd[u], t + 1)
                    v.reciprocal(rs[:, ds(t, 1)], sd[:, ds(t, 1)]).then_inc(s_rs[u], 1)
                    dve.wait_ge(s_rs[u], t + 1)
                    v.tensor_scalar(rsl[:, ds(t, 1)], rs[:, ds(t, 1)], scale, None, ALU.mult).then_inc(s_rsl[u], 1)
                    dve.wait_ge(s_rsl[u], t + 1)
                    v.tensor_scalar(w1[:, j:j + 1, :], source, mvr[:, j, 0:1],
                                    rsl[:, ds(t, 1)], ALU.subtract, ALU.mult).then_inc(s_r[u], 1)

                def gates(t, j, operand):
                    for r in range(REL):
                        dve.wait_ge(s_r[u], t + 1)
                        v.tensor_tensor_reduce(out=xr[:, j, :], in0=operand[:, j, :], in1=gw[:, r, :], scale=1.0,
                                               scalar=0.0, op0=ALU.mult, op1=ALU.add,
                                               accum_out=glr[:, j, r:r + 1]).then_inc(s_gl[u], 1)
                        dve.wait_ge(s_gl[u], t * 3 + (r + 1))
                    v.tensor_copy(glog[:, :, ds(t, 1)], glr[:, j, :]).then_inc(s_gl[u], 1)

                def after_agg(t, j):
                    dve.wait_ge(s_agg[u], t + 1)
                    if unit["ln"]:
                        wait(dve, s_ready[u + 1], t - 1)
                        wait(dve, s_xs[u], t - 1)
                    else:
                        wait(dve, s_hi[u], t - 1)
                    c = aggc[:, u, ds(t, 1)] if u in (1, 2) else aggc[:, u, 0:1]
                    v.scalar_tensor_tensor(w1[:, j:j + 1, :], Dp[:, j, 2:3, :], c, S[:, ds(t, 1), :],
                                           ALU.mult, ALU.add).then_inc(s_pre[u], 1)
                    if unit["ln"]:
                        join_residual(t, j, ALU.max if u == 2 else ALU.add)
                        stats(t, j)
                        normalize(t, j, LN_SCALE, w2[:, j:j + 1, :])
                        if u == 2:
                            gates(t, j, w1)
                    elif u == 3:
                        gates(t, j, w2)

                def join_residual(t, j, op):
                    dve.wait_ge(s_pre[u], t + 1)
                    tile_moved(dve, s_xl[u], t, j)
                    if u < NU - 1:
                        tile_moved(dve, s_xst[u], t - 2, j)
                    v.scalar_tensor_tensor(w2[:, j, :], w1[:, j, :], 0.0, xr[:, j, :], op, ALU.add).then_inc(s_v[u], 1)

                def last_tile(t, j):
                    dve.wait_ge(s_d, NT * u + t + 1)
                    tile_moved(dve, s_xst[u], t - 2, j)
                    v.scalar_tensor_tensor(w1[:, j, :], Dp[:, j, 0, :], ownc[:, u:u + 1], bias[:, :],
                                           ALU.mult, ALU.add).then_inc(s_own[u], 1)
                    dve.wait_ge(s_own[u], t + 1)
                    tile_moved(dve, s_xl[u], t, j)
                    v.tensor_tensor(w2[:, j, :], w1[:, j, :], xr[:, j, :], ALU.add).then_inc(s_v[u], 1)
                    stats(t, j)
                    normalize(t, j, 1.0, w2[:, j:j + 1, :])

                if nz == 2:
                    dve.wait_ge(s_gt[u], 1)
                    v.tensor_scalar(zsc[:, :, :], gate[:, :, :], 2.0 ** -unit["zexp"], None, ALU.mult).then_inc(s_gz[u], 1)
                    dve.wait_ge(s_gz[u], 1)
                if not nz:
                    dve.wait_ge(s_ready[u], NT)
                    pairs_of_tiles(dve, last_tile)
                    break
                pairs_of_tiles(dve, z_low)
                weights_max(u + 1)
                scales(u + 1)
                split_low(u + 1)
                if u in (2, 3):
                    dve.wait_ge(s_gw, 32 * (u - 1))
                if u > 0:
                    pairs_of_tiles(dve, after_agg)
                    continue

                dve.wait_ge(s_bn, 48)
                for t in range(NT):
                    dve.wait_ge(s_agg[0], t + 1)
                    v.scalar_tensor_tensor(S[:, t, :], Dp[:, t % 2, 2, :], aggc[:, 0, t:t + 1], b0b,
                                           ALU.mult, ALU.add).then_inc(b_h, 1)
                dve.wait_ge(b_mean, 1)
                v.tensor_copy(mean, T[:, 0, :]).then_inc(b_meanc, 1)
                dve.wait_ge(b_meanc, 1)
                for t in range(NT):
                    dve.wait_ge(b_h, t + 1)
                    v.tensor_tensor(S[:, t, :], S[:, t, :], mean, ALU.subtract).then_inc(b_c, 1)
                dve.wait_ge(b_sd, 1)
                link(v.reciprocal(mean, bnsc))
                link(v.tensor_tensor(bnsc, mean, gamb, ALU.mult))
                for t in range(NT):
                    dve.wait_ge(b_q, NT)
                    dve.wait_ge(b_c, t + 1)
                    wait(dve, b_g, t - 1)
                    v.tensor_tensor(w1[:, t % 2, :], S[:, t, :], bnsc, ALU.mult).then_inc(b_n1, 1)
                    dve.wait_ge(b_n1, NT + t + 1)
                    v.tensor_tensor(w1[:, t % 2, :], w1[:, t % 2, :], betb, ALU.add).then_inc(b_n2, 1)
                    dve.wait_ge(b_g, t + 1)
                    tile_moved(dve, s_xl[0], t, t % 2)
                    v.scalar_tensor_tensor(S[:, t, :], xr[:, t % 2, :], 2.0, w2[:, t % 2, :],
                                           ALU.mult, ALU.add).then_inc(s_v[0], 1)
                    dve.wait_ge(s_v[0], t + 1)
                    v.bn_stats(stt[:, t % 2, :], S[:, t, :]).then_inc(s_bs[0], 1)
                    dve.wait_ge(s_bs[0], t + 1)
                    v.bn_aggr(mv[:, t, :], stt[:, t % 2, :]).then_inc(s_mv[0], 1)
                dve.wait_ge(s_sd[0], 1)
                link(v.reciprocal(rs[:, :], sd[:, :]))
                link(v.tensor_scalar(rsl[:, :], rs[:, :], LN_SCALE, None, ALU.mult))
                for t in range(NT):
                    wait(dve, s_ready[1], t - 1)
                    wait(dve, s_xs[0], t - 1)
                    v.tensor_scalar(w1[:, t % 2, :], S[:, t, :], mv[:, t, 0:1], rsl[:, t:t + 1],
                                    ALU.subtract, ALU.mult).then_inc(s_r[0], 1)


_OUTS = [((N, D), "float32")]


def kernel(**inputs):
    import concourse.bacc as _bacc
    from concourse import mybir as _mybir
    from concourse.bass_utils import run_bass_kernel_spmd as _run

    def chunked(a):
        flat = np.full((CHUNKS * P,), PAD, a.dtype)
        flat[:E] = a
        return flat.reshape(CHUNKS, P)

    g = {k: np.asarray(v) for k, v in inputs.items()}
    src, dst, typ = chunked(g["src"]), chunked(g["dst"]), chunked(g["edge_type_2"])
    typ = np.where(np.arange(CHUNKS * P).reshape(CHUNKS, P) < E, typ, 0).astype(typ.dtype)
    lay = {
        "x": g["x"], "src_t": src.T, "dst_t": dst.T, "typ_t": typ.T, "dst_r": dst.reshape(CHUNKS // 2, 2, P),
        "W0": g["L0_gnn_W"].T, "b0": g["L0_gnn_b"], "gamma": g["L0_gnn_gamma"], "beta": g["L0_gnn_beta"],
        "Ws1": g["L1_gnn_W_self1"], "Wn1": g["L1_gnn_W_neigh1"], "b1": g["L1_gnn_b1"],
        "Ws2": g["L1_gnn_W_self2"], "Wn2": g["L1_gnn_W_neigh2"], "b2": g["L1_gnn_b2"],
    }
    for n in ("1", "2"):
        for a, b in (("basis", "basis"), ("att", "att"), ("gate", "gate_w"), ("root", "root"), ("rb", "bias")):
            lay[a + n] = g[f"L2_gnn_{b}{n}"]
    lay.update({"V1": g["L3_gnn_W1"], "vb1": g["L3_gnn_b1"], "V2": g["L3_gnn_W2"], "vb2": g["L3_gnn_b2"]})

    nc = _bacc.Bacc("TRN2", target_bir_lowering=False, num_devices=1)
    arrays, args = {}, {}
    for name, a in lay.items():
        a = np.ascontiguousarray(a)
        arrays[f"in_{name}"] = a
        args[name] = nc.dram_tensor(f"in_{name}", a.shape, _mybir.dt.from_np(a.dtype), kind="ExternalInput").ap()
    for i, (shape, dtype) in enumerate(_OUTS):
        args["out"] = nc.dram_tensor(f"out_{i}", shape, _mybir.dt.from_np(np.dtype(dtype)), kind="ExternalOutput").ap()
    args["xres"] = nc.dram_tensor("xres", (NP, D), _mybir.dt.float32, kind="Internal").ap()
    resnorm_gnn_kernel(nc, **args)
    r = _run(nc, [arrays], core_ids=[0])
    return r.results[0]["out_0"]
```

```python
import concourse.bass as bass
from concourse import mybir
from contextlib import ExitStack
import numpy as np

N, D, E = 1250, 512, 21250
REL, BASES = 2, 30
P = 128
NT = -(-N // P)
NP = NT * P
LAST = N - (NT - 1) * P
KT = D // P
WIN = 64
NWIN = NP // WIN
CHUNKS = 170
PAD = 4000
OH = 4
EPS = 1e-5
LN_SCALE = 512.0
TOP = 2.0 ** 14

UNITS = [
    dict(mats=["W0"], nz=1, own=None, zexp=24, bias=None, ln=True),
    dict(mats=["Wn1", "Ws1"], nz=1, own=1, zexp=18, bias="b1", ln=False),
    dict(mats=["Wn2", "Ws2"], nz=1, own=1, zexp=24, bias="b2", ln=True),
    dict(mats=["acc0", "acc1", "root1"], nz=2, own=2, zexp=18, bias="rb1", ln=False),
    dict(mats=["acc0", "acc1", "root2"], nz=2, own=2, zexp=24, bias="rb2", ln=True),
    dict(mats=["V1"], nz=1, own=0, zexp=18, bias="vb1", ln=False),
    dict(mats=["V2"], nz=0, own=0, zexp=0, bias="vb2", ln=True),
]


def resnorm_gnn_kernel(nc, x, src_t, dst_t, typ_t, dst_r, W0, b0, gamma, beta,
                       Ws1, Wn1, b1, Ws2, Wn2, b2,
                       basis1, att1, gate1, root1, rb1, basis2, att2, gate2, root2, rb2,
                       V1, vb1, V2, vb2, out, xres):
    f32, f16, i32 = mybir.dt.float32, mybir.dt.float16, mybir.dt.int32
    ALU, ACT, AX = mybir.AluOpType, mybir.ActivationFunctionType, mybir.AxisListType
    RMAX = bass.bass_isa.ReduceOp.max
    dram = dict(W0=W0, Wn1=Wn1, Ws1=Ws1, Wn2=Wn2, Ws2=Ws2, root1=root1, root2=root2, V1=V1, V2=V2,
                b1=b1, b2=b2, rb1=rb1, rb2=rb2, vb1=vb1, vb2=vb2)
    NU = len(UNITS)
    ctx = ExitStack()
    with ctx:
        def sb(name, shape, dt):
            return ctx.enter_context(nc.sbuf_tensor(name, shape, dt))

        def sem(name):
            return ctx.enter_context(nc.semaphore(name))

        A = sb("A", [P, REL, NT, NP], f16)
        AT = sb("AT", [P, NT, NP], f16)
        S = sb("S", [P, NT, D], f32)
        S16 = S[:, :, :].bitcast(f16)
        Zraw = sb("Zraw", [P, REL * 2 * NT * D], f16)
        Z = Zraw[:, :].rearrange("p (r h t d) -> p r h t d", r=REL, h=2, t=NT)
        hT = sb("hT", [P, 2, 2, D], f16)
        W = sb("W", [P, 3, 2, KT, D], f16)
        acc = sb("acc", [P, REL, KT, D], f32)
        stage = sb("stage", [P, 2, 2, D], f32)
        w1 = sb("w1", [P, 2, D], f32)
        w2 = sb("w2", [P, 2, D], f32)
        xr = sb("xr", [P, 2, D], f32)
        bias = sb("bias", [P, D], f32)
        gw = sb("gw", [P, REL, D], f32)
        ident = sb("ident", [P, P], f16)
        att = sb("att", [P, REL, BASES], f32)
        dg = sb("dg", [P, REL, NT], f32)
        dout = sb("dout", [P, NT], f32)
        deg = sb("deg", [P, NT], f32)
        rdeg = sb("rdeg", [P, NT], f32)
        dinv = sb("dinv", [P, NT], f32)
        zsc0 = sb("zsc0", [P, NT], f32)
        zsc = sb("zsc", [P, REL, NT], f32)
        aggc = sb("aggc", [P, NU, NT], f32)
        mcol = sb("mcol", [P, 8], f32)
        mw = sb("mw", [P, 2], f32)
        mwg = sb("mwg", [P, NU], f32)
        mb = sb("mb", [P, 1], f32)
        gin = sb("gin", [P, 2], f32)
        gmax = sb("gmax", [P, 2], f32)
        xin = sb("xin", [P, 1], f32)
        xmax = sb("xmax", [P, 1], f32)
        sW = sb("sW", [P, NU], f32)
        iW = sb("iW", [P, NU], f32)
        s_in = sb("s_in", [P, NU], f32)
        i_in = sb("i_in", [P, NU], f32)
        ownc = sb("ownc", [P, NU], f32)
        tmpc = sb("tmpc", [P, 4], f32)
        stt = sb("stt", [P, 2, 6], f32)
        mv = sb("mv", [P, NT, 2], f32)
        mvr = sb("mvr", [P, 2, 2], f32)
        glr = sb("glr", [P, 2, REL], f32)
        sd = sb("sd", [P, NT], f32)
        rs = sb("rs", [P, NT], f32)
        rsl = sb("rsl", [P, NT], f32)
        glog = sb("glog", [P, REL, NT], f32)
        gate = sb("gate", [P, REL, NT], f32)
        epsc = sb("epsc", [P, 1], f32)
        tbl = sb("tbl", [1, NWIN, 4], i32)

        at = [0]

        def zview(nbytes):
            a = at[0]
            at[0] += nbytes // 2
            return Zraw[:, a:at[0]]

        oh_src = zview(2 * NP * OH)
        oh_dst = zview(2 * P * OH)
        iota_n = zview(2 * NP)
        code = zview(2 * P)
        negw = zview(4 * NWIN).bitcast(f32)
        src_i, dst_i, typ_i = (zview(4 * CHUNKS).bitcast(i32) for _ in range(3))
        src_f, key_f = (zview(4 * CHUNKS).bitcast(f32) for _ in range(2))
        HC = CHUNKS // 2
        dstr = zview(4 * 2 * P).bitcast(i32).rearrange("p (g e) -> p g e", g=2)
        wlo = zview(4 * NWIN).bitcast(f32)
        whi = zview(4 * NWIN).bitcast(f32)
        cid = zview(4 * 4).bitcast(f32)
        mnx = zview(4 * 4).bitcast(f32)
        fl = zview(4 * 2 * NWIN).bitcast(f32)
        rng = zview(4 * 2 * NWIN).bitcast(f32)
        rngr = zview(4 * 2 * NWIN).bitcast(f32)
        w_st = zview(4 * NWIN).bitcast(f32)
        w_n = zview(4 * NWIN).bitcast(i32)
        w_c = [zview(4 * NWIN).bitcast(f32) for _ in range(2)]
        at[0] = 2 * NT * D
        b0b, gamb, betb, mean, bnsc, csum, csq, shift = (zview(4 * D).bitcast(f32) for _ in range(8))
        onesn = zview(4 * P).bitcast(f32)
        assert at[0] <= REL * 2 * NT * D

        x_first = Zraw[:, 0:5 * 2 * D].bitcast(f32).rearrange("p (t d) -> p t d", t=5)
        x_next = W[:, 2, :, :, :].rearrange("p h k d -> p (h k d)").bitcast(f32).rearrange("p (t d) -> p t d", t=4)

        def x_again(t):
            return x_first[:, t, :] if t < 5 else x_next[:, t - 5, :] if t < 9 else xr[:, 1, :]

        T = ctx.enter_context(nc.psum_tensor("T", [P, 2, D], f32))
        Dp = ctx.enter_context(nc.psum_tensor("Dp", [P, 2, 3, D], f32))
        Df = Dp[:, :, :, :].rearrange("p a j d -> p a (j d)")

        LN = [u for u in range(NU) if UNITS[u]["ln"]]
        e_src, e_dst, e_typ, e_row, e_x = (sem(n) for n in ("e_src", "e_dst", "e_typ", "e_row", "e_x"))
        s_pad = sem("s_pad")
        s_const = sem("s_const")
        s_chain = sem("s_chain")
        s_carry_dve = sem("s_carry_dve")
        s_pch = sem("s_pch")
        s_rng = sem("s_rng")
        s_rngr = sem("s_rngr")
        s_tbl = sem("s_tbl")
        s_oh = sem("s_oh")
        s_ohu = sem("s_ohu")
        s_win = sem("s_win")
        s_wev = sem("s_wev")
        s_at = sem("s_at")
        s_ate = sem("s_ate")
        s_xin, s_xmax, s_s0 = sem("s_xin"), sem("s_xmax"), sem("s_s0")
        s_gin = sem("s_gin")
        s_gmax = sem("s_gmax")
        s_dsq = sem("s_dsq")
        s_dout = sem("s_dout")
        s_att = [sem("s_att0"), sem("s_att1")]
        st_full = [sem("st_full0"), sem("st_full1")]
        st_free = [sem("st_free0"), sem("st_free1")]
        s_bias = sem("s_bias")
        s_gw = sem("s_gw")
        s_bn = sem("s_bn")
        s_mw = sem("s_mw")
        s_mwr = sem("s_mwr")
        s_sW = sem("s_sW")
        s_wsc = sem("s_wsc")
        s_whi = sem("s_whi")
        s_wlo = sem("s_wlo")
        s_t = sem("s_t")
        s_hT = sem("s_hT")
        s_d = sem("s_d")
        s_ready = {u: sem(f"s_ready{u}") for u in range(NU)}
        s_zhi = {u: sem(f"s_zhi{u}") for u in range(6)}
        s_zlo = {u: sem(f"s_zlo{u}") for u in range(6)}
        s_zlp = {u: sem(f"s_zlp{u}") for u in (3, 4)}
        s_own = {u: sem(f"s_own{u}") for u in range(1, 7)}
        s_agg = {u: sem(f"s_agg{u}") for u in range(6)}
        s_pre = {u: sem(f"s_pre{u}") for u in range(1, 6)}
        s_v = {u: sem(f"s_v{u}") for u in LN}
        s_bs = {u: sem(f"s_bs{u}") for u in LN}
        s_mv = {u: sem(f"s_mv{u}") for u in LN}
        s_sd = {u: sem(f"s_sd{u}") for u in LN}
        s_rs = {u: sem(f"s_rs{u}") for u in LN[1:]}
        s_r = {u: sem(f"s_r{u}") for u in range(NU)}
        s_hi = {u: sem(f"s_hi{u}") for u in range(6)}
        s_xs = {u: sem(f"s_xs{u}") for u in LN[:3]}
        s_gl = {u: sem(f"s_gl{u}") for u in (2, 3)}
        s_gt = {u: sem(f"s_gt{u}") for u in (3, 4)}
        s_gz = {u: sem(f"s_gz{u}") for u in (3, 4)}
        s_xl = {u: [sem(f"s_xl{u}_{j}") for j in range(2)] for u in LN[1:]}
        s_xst = {u: [sem(f"s_xst{u}_{j}") for j in range(2)] for u in LN}
        s_xa = [sem(f"s_xa{j}") for j in range(2)]
        b_h, b_sum, b_mean, b_shift, b_c, b_sq, b_q, b_var, b_sd, b_vr = (
            sem("b_" + n) for n in ("h", "sum", "mean", "shift", "c", "sq", "q", "var", "sd", "vr"))
        b_n1, b_n2, b_g = sem("b_n1"), sem("b_n2"), sem("b_g")
        x_sc, x_hi = sem("x_sc"), sem("x_hi")

        ds = bass.ds

        def wait(eng, s, n):
            if not isinstance(n, int) or n > 0:
                eng.wait_ge(s, n)

        def tile_moved(eng, s, t, j):
            if not isinstance(t, int) or t >= 0:
                eng.wait_ge(s[j], (t + (2 - j)) * 8)

        def tiles(eng, body, hook=None):
            def pair(place, p):
                for j in range(2):
                    body(p * 2 + j, j)
                    if hook:
                        hook(place, p, j)
            pair("P0", 0)
            pair("P1", 1)
            with eng.Fori(2, 4) as p:
                pair("loop", p)
            if hook:
                hook("after", 3, 1)
            pair("P4", 4)

        plan, events = {}, []

        def schedule(phase, place, kind, what, loop=1):
            g = sum(e[3] for e in events)
            events.append((kind, what, loop, loop * (what[2] if kind == "basis" else 1), g))
            plan.setdefault((phase, place), []).append((kind, what, g))

        def bases(phase, counts, b, L):
            for place in ("P0", "P1", "loop", "after", "P4"):
                n = counts.get(place, 0)
                if n:
                    loop = 2 if place == "loop" else 1
                    schedule(phase, place, "basis", (L, b, n), loop)
                    b += n * loop
                weights(phase, place)
            return b

        def plain_mats(u):
            return [m for m in UNITS[u]["mats"] if m[:3] != "acc"]

        WHERE = {u: ("P0", "P1", "after") for u in range(6)}
        WHERE[3] = ("after", "after", "after")

        def weights(phase, place):
            kind, u = phase
            if kind != "agg":
                return
            mats, u = UNITS[u + 1]["mats"], u + 1
            mx, first, rest = WHERE[u - 1]
            half = (len(mats) + 1) // 2
            for m, name in enumerate(mats):
                if place == mx and name[:3] != "acc":
                    schedule(phase, place + "+", "max", (u, m))
            for m, name in enumerate(mats):
                if place == (first if m < half else rest) and name[:3] != "acc":
                    schedule(phase, place + "+", "split", (u, m))

        schedule(("dense", -1), "", "max", (0, 0))
        schedule(("dense", -1), "", "split", (0, 0))
        b = bases(("dense", 0), dict(P1=1, P4=1), 0, 0)
        b = bases(("agg", 0), dict(P0=1, P1=1, loop=1, P4=1), b, 0)
        schedule(("bn", 0), "", "basis", (0, b, 2))
        b = bases(("dense", 1), dict(P0=2, P1=2, loop=1, P4=2), b + 2, 0)
        b = bases(("agg", 1), dict(P0=1, P1=1, loop=1, P4=1), b, 0)
        b = bases(("dense", 2), dict(P0=2, P1=2, loop=1, P4=2), b, 0)
        assert b == BASES
        bases(("agg", 2), {}, 0, 0)
        b = bases(("dense", 3), dict(P0=3, P1=3, loop=3, P4=3), 0, 1)
        b = bases(("agg", 3), dict(P0=5, P1=4, loop=3, P4=0), b, 1)
        assert b == BASES
        for u in (4, 5):
            bases(("dense", u), {}, 0, 0)
            bases(("agg", u), {}, 0, 0)

        BASIS_END = {}
        for kind, what, loop, n, g in events:
            if kind == "basis":
                BASIS_END[3 if what[0] == 0 else 4] = g + n
        Z_SCALED = 35

        def halves_split(u):
            return sum(2 * len(v["mats"]) for v in UNITS[:u + 1])

        block = ctx.enter_context(nc.Block())

        @block.sync
        def _(sp):
            sp.dma_start(dstr[0:HC, :, :], dst_r).then_inc(e_row, 16)
            sp.dma_start(dst_i, dst_t).then_inc(e_dst, 16)
            sp.dma_start(typ_i, typ_t).then_inc(e_typ, 16)
            sp.dma_start(src_i, src_t).then_inc(e_src, 16)
            sp.wait_ge(s_pad, 1)
            sp.dma_start(S[:, 0:NT - 1, :], x[0:(NT - 1) * P, :].rearrange("(t p) d -> p t d", p=P)).then_inc(e_x, 16)
            sp.dma_start(S[0:LAST, NT - 1, :], x[(NT - 1) * P:N, :]).then_inc(e_x, 16)
            for tile, vec in ((b0b, b0), (gamb, gamma), (betb, beta)):
                sp.dma_start(tile, vec.rearrange("(a d) -> a d", a=1).broadcast_to([P, D])).then_inc(s_bn, 16)
            seen = set()

            def load_bias(u):
                if u >= 2:
                    sp.wait_ge(s_own[u - 1], NT)
                sp.dma_start(bias[:, :], dram[UNITS[u]["bias"]].rearrange("(a d) -> a d", a=1)
                             .broadcast_to([P, D])).then_inc(s_bias, 16)
                if u == 3:
                    load_gates(gate1)

            def load_gates(g):
                for r in range(REL):
                    sp.dma_start(gw[:, r, :], g[r:r + 1, :, 0].broadcast_to([P, D])).then_inc(s_gw, 16)

            def load_att(L):
                sp.dma_start(att[:, :, :].rearrange("p r b -> p (r b)"),
                             (att1, att2)[L].rearrange("(a r) b -> a (r b)", a=1)
                             .broadcast_to([P, REL * BASES])).then_inc(s_att[L], 16)

            for kind, what, loop, n, g in events:
                if kind == "basis":
                    L, b0_, count = what
                    if b0_ == 0:
                        load_att(L)

                    def basis_loads(i):
                        for j in range(2):
                            wait(sp, st_free[j], i + g)
                            sp.dma_start(stage[:, j, :, :], (basis1, basis2)[L]
                                         [ds(i + b0_, 1), 2 * j * P:2 * (j + 1) * P, :]
                                         .rearrange("a (q p) d -> p (a q) d", p=P)).then_inc(st_full[j], 16)

                    if n > 2:
                        with sp.Fori(0, n) as i:
                            basis_loads(i)
                    else:
                        for i in range(n):
                            basis_loads(i)
                    if L and b0_ == 0:
                        sp.wait_ge(s_gl[2], 3 * NT)
                        load_gates(gate2)
                else:
                    u, m = what
                    if kind == "max" and u not in seen and UNITS[u]["bias"]:
                        load_bias(u)
                        seen.add(u)
                    for j in range(2):
                        wait(sp, st_free[j], g)
                        sp.dma_start(stage[:, j, :, :], dram[UNITS[u]["mats"][m]][2 * j * P:2 * (j + 1) * P, :]
                                     .rearrange("(q p) d -> p q d", p=P)).then_inc(st_full[j], 16)

        @block.gpsimd
        def _(pool):
            kw = dict(allow_small_or_imprecise_dtypes=True)
            pool.iota(wlo, [[WIN, NWIN]], base=0, channel_multiplier=0, **kw).then_inc(s_const, 1)
            pool.iota(whi, [[WIN, NWIN]], base=WIN - 1, channel_multiplier=0, **kw).then_inc(s_const, 1)
            pool.iota(cid[:, 0:2], [[-1, 2]], base=256, channel_multiplier=-2, **kw).then_inc(s_const, 1)
            pool.iota(cid[:, 2:4], [[1, 2]], base=1, channel_multiplier=2, **kw).then_inc(s_const, 1)
            pool.memset(rng, 0.0).then_inc(s_const, 1)
            pool.iota(negw, [[-2 * WIN, NWIN]], base=0, channel_multiplier=0, **kw).then_inc(s_const, 1)
            pool.iota(code, [[1, REL], [2, WIN]], base=0, channel_multiplier=0, **kw).then_inc(s_const, 1)
            pool.iota(iota_n, [[1, NP]], base=0, channel_multiplier=0, **kw).then_inc(s_const, 1)
            pool.memset(ident[:, :], 0.0).then_inc(s_pch, 1)
            pool.wait_ge(s_pch, 1)
            pool.affine_select(out=ident[:, :], in_=ident[:, :], compare_op=ALU.not_equal, fill=1.0, base=0,
                               pattern=[[-1, P]], channel_multiplier=1).then_inc(s_const, 1)
            pool.wait_ge(s_rng, 1)
            pool.partition_all_reduce(rngr, rng, P, RMAX).then_inc(s_rngr, 1)
            pool.memset(epsc[:, :], EPS).then_inc(s_const, 1)
            pool.memset(onesn, 1.0 / N).then_inc(s_const, 1)
            pool.memset(csum, 0.0).then_inc(s_const, 1)
            pool.memset(csq, 0.0).then_inc(s_const, 1)

            def reduce_weights(u):
                pool.wait_ge(s_mw, u + 1)
                pool.partition_all_reduce(mwg[:, u:u + 1], mw[:, u % 2:u % 2 + 1], P, RMAX).then_inc(s_mwr, 1)

            def low_weights(u, m):
                for h in range(2):
                    n = halves_split(u - 1) + 2 * m + h
                    of_acc = UNITS[u]["mats"][m][:3] == "acc"
                    source = acc[:, m, 2 * h:2 * h + 2, :] if of_acc else stage[:, h, :, :]
                    pool.wait_ge(s_whi, n + 1)
                    pool.tensor_tensor(W[:, m, 1, 2 * h:2 * h + 2, :], source, W[:, m, 0, 2 * h:2 * h + 2, :],
                                       ALU.subtract).then_inc(s_wlo, 1)
                    if not of_acc:
                        pool.wait_ge(s_wlo, n + 1)
                        pool.sem_inc(st_free[h], 1)

            def weight_work(u, place, j):
                mats = UNITS[u + 1]["mats"]
                mx, first, rest = WHERE[u]
                half = (len(mats) + 1) // 2
                if j == 1 and place == mx:
                    reduce_weights(u + 1)
                for m in range(len(mats)):
                    if j == 1 and place == (first if m < half else rest):
                        low_weights(u + 1, m)

            pool.wait_ge(s_xin, 1)
            pool.partition_all_reduce(xmax[:, :], xin[:, :], P, RMAX).then_inc(s_xmax, 1)
            reduce_weights(0)
            for t in range(NT):
                pool.wait_ge(x_hi, t + 1)
                pool.tensor_tensor(S16[:, t, D:2 * D], w1[:, t % 2, :], S16[:, t, 0:D], ALU.subtract).then_inc(s_ready[0], 1)
            low_weights(0, 0)

            for t in range(NT):
                rows = P if t < NT - 1 else LAST
                for src, total, ready, done in ((S[:, t, :], csum, b_c, b_sum), (w1[:, t % 2, :], csq, b_sq, b_q)):
                    pool.wait_ge(ready, t + 1)
                    wait(pool, done, t)
                    pool.tensor_tensor(total[0:rows, :], total[0:rows, :], src[0:rows, :], ALU.add).then_inc(done, 1)
                weight_work(0, {1: "P0", 3: "P1", 7: "after"}.get(t), 1)
            pool.wait_ge(s_gin, 1)
            pool.partition_all_reduce(gmax[:, :], gin[:, :], P, RMAX).then_inc(s_gmax, 1)

            for u in range(0, 6):
                def low_part(t, j):
                    r = w1 if UNITS[u]["ln"] else w2
                    pool.wait_ge(s_hi[u], t + 1)
                    pool.tensor_tensor(S16[:, ds(t, 1), D:2 * D], r[:, j:j + 1, :], S16[:, ds(t, 1), 0:D],
                                       ALU.subtract).then_inc(s_ready[u + 1], 1)

                def low_product(t, j):
                    pool.wait_ge(s_zhi[u], t * 2 + 2)
                    pool.tensor_tensor(Z[:, 1, 1, ds(t, 1), :], w1[:, j:j + 1, :], Z[:, 1, 0, ds(t, 1), :],
                                       ALU.subtract).then_inc(s_zlp[u], 1)

                if UNITS[u]["nz"] == 2:
                    tiles(pool, low_product)
                if u == 0:
                    for t in range(NT):
                        low_part(t, t % 2)
                else:
                    tiles(pool, low_part, lambda place, p, j: weight_work(u, place, j))

        @block.tensor
        def _(pe):
            def chunk_product(n, j, start, stop):
                slot = pe.snap(n & (OH - 1))
                pe.wait_ge(s_oh, n * 2 + 2)
                for c in range(0, NP, D):
                    w = min(D, NP - c)
                    last = nc.tensor.matmul(Df[:, j, c:c + w], oh_dst[:, ds(slot * P, P)],
                                            oh_src[:, ds(slot * NP + c, w)], start=start, stop=stop)
                last.then_inc(s_win if stop else s_ohu, 1)

            def window(w, j):
                row = tbl[0:1, ds(w, 1), :]
                count = pe.value_load(row[:, :, 1:2], min_val=3, max_val=CHUNKS)
                base = pe.value_load(row[:, :, 2:3], min_val=0, max_val=NWIN * CHUNKS)
                final = pe.value_load(row[:, :, 3:4], min_val=0, max_val=NWIN * CHUNKS)
                wait(pe, s_wev, w * 2 - 2)
                chunk_product(base, j, True, False)
                with pe.Fori(1, count - 1) as i:
                    chunk_product(base + i, j, False, False)
                chunk_product(final, j, False, True)
                pe.wait_ge(s_win, w + 1)
                pe.sem_inc(s_ohu, 1)

            def turn_counts(t, g):
                pe.wait_ge(s_wev, t * 4 + 4)
                wait(pe, s_ate, t * 3 + (g - (1, 3, 2)[g] + 1))
                for q, m in enumerate(range(4 * g, min(4 * g + 4, NT))):
                    for r in range(REL):
                        last = nc.tensor.matmul(T[:, g % 2, q * P:(q + 1) * P],
                                                A[:, r, ds(t, 1), m * P:(m + 1) * P].rearrange("p a c -> p (a c)"),
                                                ident[:, :], start=(r == 0), stop=(r == REL - 1))
                last.then_inc(s_at, 1)

            pe.sem_inc(s_ohu, OH)
            pe.wait_ge(s_const, 9)
            pe.wait_ge(s_tbl, 1)
            window(0, 0)
            window(1, 1)
            for t in range(1, 2):
                window(2 * t, 0)
                turn_counts(t - 1, 0)
                turn_counts(t - 1, 1)
                window(2 * t + 1, 1)
                turn_counts(t - 1, 2)
            with pe.Fori(2, NT) as t:
                window(t * 2, 0)
                turn_counts(t - 1, 0)
                turn_counts(t - 1, 1)
                window(t * 2 + 1, 1)
                turn_counts(t - 1, 2)
            for g in range(3):
                turn_counts(NT - 1, g)
            pe.wait_ge(s_ate, 3 * NT)

            for u, unit in enumerate(UNITS):
                nm, nz = len(unit["mats"]), unit["nz"]

                def turn(t, j):
                    pe.wait_ge(s_ready[u], t + 1)
                    wait(pe, s_hT, t + NT * u)
                    for h in range(2):
                        for k in range(KT):
                            last = nc.tensor.matmul(T[:, h, k * P:(k + 1) * P],
                                                    S16[:, ds(t, 1), h * D + k * P:h * D + (k + 1) * P]
                                                    .rearrange("p a c -> p (a c)"), ident[:, :], start=True, stop=True)
                    last.then_inc(s_t, 1)

                def dense(t, j):
                    if not (isinstance(t, int) and t == NT - 1):
                        turn(t + 1, 1 - j)
                    pe.wait_ge(s_hT, t + (NT * u + 1))
                    if nz:
                        wait(pe, s_zlo[u], t - 1)
                    if nz == 2:
                        wait(pe, s_zlp[u], t - 1)
                    if unit["own"] is not None:
                        wait(pe, s_own[u], t - 1)
                    if isinstance(t, int) and t < 2 and nm == 3:
                        pe.wait_ge(s_pre[u - 1], NT - 1 + t)
                    for m in range(nm):
                        n = 0
                        for hp, wp in ((0, 0), (1, 0), (0, 1)):
                            for k in range(KT):
                                last = nc.tensor.matmul(Dp[:, j, m, :], hT[:, j, hp, k * P:(k + 1) * P],
                                                        W[:, m, wp, k, :], start=(n == 0), stop=(n == 3 * KT - 1))
                                n += 1
                    last.then_inc(s_d, 1)

                def agg(t, j):
                    wait(pe, s_pre[u] if u else b_h, t - 1)
                    rels = [(A[:, r], r) for r in range(REL)] if nz == 2 else [(AT, 0)]
                    n, count = 0, 2 * NT * nz
                    for a, r in rels:
                        for k in range(NT):
                            if isinstance(t, int) and t == 0:
                                pe.wait_ge(s_zlp[u] if r else s_zlo[u], k + 1)
                            for h in range(2):
                                last = nc.tensor.matmul(Dp[:, j, 2, :], a[:, k, ds(t * P, P)], Z[:, r, h, k, :],
                                                        start=(n == 0), stop=(n == count - 1 and u > 0))
                                n += 1
                    if u == 0:
                        for h in range(2):
                            last = nc.tensor.matmul(Dp[:, j, 2, :], ident[:, :],
                                                    Z[:, 0, h, ds(t, 1), :].rearrange("p a d -> p (a d)"),
                                                    start=False, stop=(h == 1))
                    last.then_inc(s_agg[u], 1)
                    if u == 0 and isinstance(t, int) and t == 1:
                        column_sum(0, S[:, 0, :], b_h, 1)

                def column_sum(bank, total, ready, n):
                    pe.wait_ge(ready, n)
                    nc.tensor.matmul(T[:, bank, :], onesn, total, start=True, stop=True).then_inc(b_mean, 1)

                pe.wait_ge(s_wlo, halves_split(u))
                turn(0, 0)
                tiles(pe, dense)
                if nz:
                    if unit["own"] is not None:
                        pe.wait_ge(s_own[u], NT)
                    if u == 0:
                        pe.wait_ge(s_hT, NT)
                        pe.wait_ge(s_const, 11)
                    tiles(pe, agg)
                if u == 0:
                    pe.wait_ge(b_shift, 1)
                    column_sum(0, csum, b_sum, NT)
                    column_sum(1, csq, b_q, NT)

        @block.scalar
        def _(act):
            def window_out(w, j, t):
                act.wait_ge(s_win, w + 1)
                for r in range(REL):
                    nc.scalar.activation(A[WIN * j:WIN * (j + 1), r, ds(t, 1), :],
                                         Dp[WIN * r:WIN * (r + 1), j, :, :].rearrange("p j d -> p (j d)")[:, 0:NP],
                                         ACT.Copy, accum_out=dg[WIN * j:WIN * (j + 1), r, ds(t, 1)]).then_inc(s_wev, 1)

            def turned_out(t, g):
                act.wait_ge(s_at, t * 3 + (g + 1))
                n = min(4, NT - 4 * g)
                nc.scalar.activation(AT[:, 4 * g:4 * g + n, ds(t * P, P)],
                                     T[:, g % 2, 0:n * P].rearrange("p (m c) -> p m c", m=n), ACT.Copy).then_inc(s_ate, 1)

            def tile_out(t):
                window_out(t * 2, 0, t)
                turned_out(t - 1, 0)
                turned_out(t - 1, 1)
                window_out(t * 2 + 1, 1, t)
                turned_out(t - 1, 2)

            def split_x(t):
                wait(act, s_ready[0], t - 1)
                nc.scalar.activation(w1[:, t % 2, :], S[:, t, :], ACT.Copy, scale=s_in[:, 0:1]).then_inc(x_sc, 1)
                act.wait_ge(x_sc, t + 1)
                nc.scalar.activation(S16[:, t, 0:D], w1[:, t % 2, :], ACT.Copy).then_inc(x_hi, 1)

            def high_weights(u, m, g):
                of_acc = UNITS[u]["mats"][m][:3] == "acc"
                act.wait_ge(s_sW, u + 1)
                n = halves_split(u - 1) + 2 * m
                source = [acc[:, m, 2 * h:2 * h + 2, :] if of_acc else stage[:, h, :, :] for h in range(2)]
                for h in range(2):
                    if not of_acc:
                        act.wait_ge(st_full[h], 16 * (g + 1))
                    nc.scalar.activation(source[h], source[h], ACT.Copy, scale=sW[:, u:u + 1]).then_inc(s_wsc, 1)
                for h in range(2):
                    act.wait_ge(s_wsc, n + h + 1)
                    nc.scalar.activation(W[:, m, 0, 2 * h:2 * h + 2, :], source[h], ACT.Copy).then_inc(s_whi, 1)

            def weight_work(u, place, j):
                mats = UNITS[u + 1]["mats"]
                _, first, rest = WHERE[u]
                half = (len(mats) + 1) // 2
                at_g = {what[1]: g for kind, what, g in plan.get((("agg", u), str(place) + "+"), []) if kind == "split"}
                for m in range(len(mats)):
                    if j == 1 and place == (first if m < half else rest):
                        high_weights(u + 1, m, at_g.get(m))

            window_out(0, 0, 0)
            window_out(1, 1, 0)
            tile_out(1)
            with act.Fori(2, NT - 2) as t:
                tile_out(t)
            act.wait_ge(s_s0, 1)
            for t in range(0, 5):
                split_x(t)
            tile_out(NT - 2)
            for t in range(5, NT):
                split_x(t)
            high_weights(0, 0, 1)
            tile_out(NT - 1)
            act.wait_ge(s_dsq, 1)
            nc.scalar.activation(dinv[:, :], dinv[:, :], ACT.Sqrt).then_inc(s_dsq, 1)
            for g in range(3):
                turned_out(NT - 1, g)

            for u, unit in enumerate(UNITS):
                nz = unit["nz"]

                def hT_out(t, j):
                    act.wait_ge(s_t, t + (NT * u + 1))
                    wait(act, s_d, t + (NT * u - 1))
                    nc.scalar.activation(hT[:, j, :, :], T[:, :, :], ACT.Copy).then_inc(s_hT, 1)

                def load_residual(t, j):
                    act.dma_start(xr[:, j, :], xres[ds(t * P, P), :]).then_inc(s_xl[u][j], 16)

                def ln_step(t, j):
                    act.wait_ge(s_mv[u], t + 1)
                    nc.scalar.activation(sd[:, ds(t, 1)], mvr[:, j, 1:2], ACT.Sqrt,
                                         bias=epsc[:, 0:1]).then_inc(s_sd[u], 1)
                    if not (isinstance(t, int) and t >= NT - 2):
                        load_residual(t + 2, j)
                    act.wait_ge(s_r[u], t + 1)
                    if u < NU - 1:
                        nc.scalar.activation(S16[:, ds(t, 1), 0:D], w1[:, j:j + 1, :], ACT.Copy).then_inc(s_hi[u], 1)
                        nc.scalar.activation(w2[:, j, :], w1[:, j, :], ACT.Copy, scale=1.0 / LN_SCALE).then_inc(s_xs[u], 1)
                        act.wait_ge(s_xs[u], t + 1)
                        act.dma_start(xres[ds(t * P, P), :], w2[:, j, :]).then_inc(s_xst[u][j], 16)
                    elif isinstance(t, int) and t == NT - 1:
                        act.dma_start(out[t * P:N, :], w1[0:LAST, j, :]).then_inc(s_xst[u][j], 16)
                    else:
                        act.dma_start(out[ds(t * P, P), :], w1[:, j, :]).then_inc(s_xst[u][j], 16)

                def z_out(t, j):
                    if not (isinstance(t, int) and t == NT - 1):
                        hT_out(t + 1, 1 - j)
                    if not nz:
                        ln_step(t, j)
                        return
                    act.wait_ge(s_d, t + (NT * u + 1))
                    for r in range(nz):
                        if u == 0:
                            scale = zsc0[:, ds(t, 1)]
                        elif nz == 2:
                            scale = zsc[:, r, ds(t, 1)]
                        else:
                            scale = 2.0 ** -unit["zexp"]
                        nc.scalar.activation(Z[:, r, 0, ds(t, 1), :], Dp[:, j, r:r + 1, :], ACT.Copy,
                                             scale=scale).then_inc(s_zhi[u], 1)
                        if nz == 2 and r == 0:
                            if isinstance(t, int) and t < 2:
                                act.wait_ge(s_ready[u], NT - 1 + t)
                                if u == 3:
                                    act.wait_ge(s_xs[2], NT - 1 + t)
                            wait(act, s_zlp[u], t - 1)
                            nc.scalar.activation(w1[:, j, :], Dp[:, j, 1, :], ACT.Copy,
                                                 scale=zsc[:, 1, ds(t, 1)])

                if nz == 2:
                    act.wait_ge(s_gl[u - 1], 3 * NT)
                    nc.scalar.activation(gate[:, :, :], glog[:, :, :], ACT.Sigmoid,
                                         scale=i_in[:, u:u + 1]).then_inc(s_gt[u], 1)
                    act.wait_ge(s_gz[u], 1)
                if u == 0:
                    act.wait_ge(s_chain, Z_SCALED)
                if unit["ln"] and u:
                    for j in range(2):
                        act.wait_ge(s_xst[u - 2][j], 8 * NT)
                    load_residual(0, 0)
                    load_residual(1, 1)
                hT_out(0, 0)
                tiles(act, z_out)

                def relu_step(t, j):
                    act.wait_ge(s_pre[u], t + 1)
                    wait(act, s_ready[u + 1], t - 1)
                    if u == 3:
                        wait(act, s_gl[3], t * 3 - 3)
                    nc.scalar.activation(w2[:, j, :], w1[:, j, :], ACT.Relu, scale=s_in[:, u + 1:u + 2]).then_inc(s_r[u], 1)
                    nc.scalar.activation(S16[:, ds(t, 1), 0:D], w1[:, j:j + 1, :], ACT.Relu,
                                         scale=s_in[:, u + 1:u + 2]).then_inc(s_hi[u], 1)

                def square_step(t, j):
                    act.wait_ge(b_c, t + 1)
                    wait(act, b_q, t - 1)
                    nc.scalar.activation(w1[:, j:j + 1, :], S[:, ds(t, 1), :], ACT.Square).then_inc(b_sq, 1)
                    wait(act, s_dout, t)
                    nc.scalar.activation(W[:, 2, :, :, :].rearrange("p h k d -> p (h k d)")[:, 0:NP]
                                         .rearrange("p (a c) -> p a c", a=1), AT[:, ds(t, 1), :], ACT.Copy,
                                         accum_out=dout[:, ds(t, 1)]).then_inc(s_dout, 1)

                def hook(place, p, j):
                    weight_work(u, place, j)

                if not nz:
                    for j in range(2):
                        act.wait_ge(s_xst[u][j], 8 * NT)
                elif not unit["ln"]:
                    for j in range(2):
                        act.wait_ge(s_xst[u - 1][j], 8 * NT)
                    tiles(act, relu_step, hook)
                elif u:
                    tiles(act, ln_step, hook)
                else:
                    tiles(act, square_step, hook)
                    act.wait_ge(s_agg[0], NT)
                    act.wait_ge(s_dout, NT)
                    act.dma_start(x_first, x[0:5 * P, :].rearrange("(t p) d -> p t d", p=P)).then_inc(s_xa[0], 16)
                    act.dma_start(x_next, x[5 * P:9 * P, :].rearrange("(t p) d -> p t d", p=P)).then_inc(s_xa[1], 16)
                    act.wait_ge(s_pad, 2)
                    act.dma_start(xr[0:LAST, 1, :], x[9 * P:N, :]).then_inc(s_xa[1], 16)
                    act.wait_ge(b_vr, 1)
                    nc.scalar.activation(csq, bnsc, ACT.Sqrt).then_inc(b_sd, 1)
                    for half in range(2):
                        for t in range(5 * half, 5 * half + 5):
                            act.wait_ge(b_n2, t + 1)
                            if t in (5, 6):
                                tile_moved(act, s_xst[0], t - 2, t % 2)
                            wait(act, s_v[0], t - 1)
                            nc.scalar.activation(w2[:, t % 2, :], w1[:, t % 2, :], ACT.Gelu).then_inc(b_g, 1)
                        act.wait_ge(s_mv[0], 5 * half + 5)
                        nc.scalar.activation(sd[:, 5 * half:5 * half + 5], mv[:, 5 * half:5 * half + 5, 1], ACT.Sqrt,
                                             bias=epsc[:, 0:1]).then_inc(s_sd[0], 1)
                        for t in range(5 * half, 5 * half + 5):
                            act.wait_ge(s_r[0], t + 1)
                            nc.scalar.activation(S16[:, t, 0:D], w1[:, t % 2, :], ACT.Copy).then_inc(s_hi[0], 1)
                            tile_moved(act, s_xst[0], t - 2, t % 2)
                            nc.scalar.activation(w2[:, t % 2, :], w1[:, t % 2, :], ACT.Copy,
                                                 scale=1.0 / LN_SCALE).then_inc(s_xs[0], 1)
                            act.wait_ge(s_xs[0], t + 1)
                            act.dma_start(xres[t * P:(t + 1) * P, :], w2[:, t % 2, :]).then_inc(s_xst[0][t % 2], 16)

        @block.vector
        def _(dve):
            v = nc.vector
            chain = [0]

            def link(ins):
                chain[0] += 1
                ins.then_inc(s_chain, 1)
                dve.wait_ge(s_chain, chain[0])

            v.memset(S[:, NT - 1, :], 0.0).then_inc(s_pad, 1)
            v.memset(xr[:, 1, :], 0.0).then_inc(s_pad, 1)
            dve.wait_ge(e_row, 16)
            v.tensor_reduce(mnx[0:HC, 0:2], dstr[0:HC, :, :], AX.X, ALU.min)
            link(v.tensor_reduce(mnx[0:HC, 2:4], dstr[0:HC, :, :], AX.X, ALU.max))
            dve.wait_ge(s_const, 5)
            for g in range(2):
                link(v.tensor_scalar(fl[0:HC, 0:NWIN], wlo[0:HC, :], mnx[0:HC, 2 + g:3 + g], None, ALU.is_le))
                link(v.scalar_tensor_tensor(fl[0:HC, NWIN:2 * NWIN], whi[0:HC, :], mnx[0:HC, g:g + 1],
                                            fl[0:HC, 0:NWIN], ALU.is_ge, ALU.mult))
                for q in range(2):
                    part = rng[0:HC, q * NWIN:(q + 1) * NWIN]
                    last = v.scalar_tensor_tensor(part, fl[0:HC, NWIN:2 * NWIN], cid[0:HC, 2 * q + g:2 * q + g + 1],
                                                  part, ALU.mult, ALU.max)
                link(last)
            v.nop().then_inc(s_rng, 1)
            dve.wait_ge(e_typ, 16)
            dve.wait_ge(e_dst, 16)
            dve.wait_ge(e_src, 16)
            v.tensor_copy(src_f, src_i)
            link(v.tensor_copy(key_f, typ_i))
            link(v.scalar_tensor_tensor(key_f, dst_i, 2.0, key_f, ALU.mult, ALU.add))
            dve.wait_ge(s_rngr, 1)
            link(v.tensor_scalar(w_st, rngr[:, 0:NWIN], -1.0, 256.0, ALU.mult, ALU.add))
            link(v.tensor_scalar(w_st, w_st, float(CHUNKS - 3), None, ALU.min))
            link(v.tensor_tensor(w_n, rngr[:, NWIN:2 * NWIN], w_st, ALU.subtract))
            link(v.tensor_scalar(w_n, w_n, 3.0, None, ALU.max))
            a, step = 0, 1
            while step < NWIN:
                source = w_c[a] if step > 1 else w_n
                v.tensor_copy(w_c[1 - a][:, 0:step], source[:, 0:step])
                link(v.tensor_tensor(w_c[1 - a][:, step:NWIN], source[:, step:NWIN], source[:, 0:NWIN - step], ALU.add))
                a, step = 1 - a, 2 * step
            v.tensor_copy(tbl[0:1, :, 0], w_st[0:1, :])
            v.tensor_copy(tbl[0:1, :, 1], w_n[0:1, :])
            v.tensor_scalar(tbl[0:1, :, 3], w_c[a][0:1, :], -1.0, None, ALU.add)
            v.tensor_tensor(tbl[0:1, :, 2], w_c[a][0:1, :], w_n[0:1, :], ALU.subtract).then_inc(s_tbl, 1)
            dve.wait_ge(s_tbl, 1)
            dve.wait_ge(s_const, 8)

            def windows(w0, w1_):
                with dve.Fori(w0, w1_) as w:
                    row = tbl[0:1, ds(w, 1), :]
                    first = dve.value_load(row[:, :, 0:1], min_val=0, max_val=CHUNKS - 3)
                    count = dve.value_load(row[:, :, 1:2], min_val=3, max_val=CHUNKS)
                    base = dve.value_load(row[:, :, 2:3], min_val=0, max_val=NWIN * CHUNKS)
                    with dve.Fori(0, count) as i:
                        c = nc.s_assert_within(dve.snap(first + i), 0, CHUNKS - 1, skip_runtime_bounds_check_because=
                                               "the chunks of a window end at the last chunk, or at the third from first")
                        n = dve.snap(base + i)
                        slot = dve.snap(n & (OH - 1))
                        dve.wait_ge(s_ohu, n + 1)
                        v.tensor_scalar(oh_dst[:, ds(slot * P, P)], code, key_f[:, ds(c, 1)], negw[:, ds(w, 1)],
                                        ALU.subtract, ALU.is_equal).then_inc(s_oh, 1)
                        v.tensor_scalar(oh_src[:, ds(slot * NP, NP)], iota_n, src_f[:, ds(c, 1)], None,
                                        ALU.is_equal).then_inc(s_oh, 1)

            def power_scale(s, i, m):
                link(v.tensor_scalar(tmpc[:, 0:1], m, 1e-30, None, ALU.max))
                link(v.tensor_scalar(tmpc[:, 1:2].bitcast(i32), tmpc[:, 0:1].bitcast(i32), 0x7F800000, None,
                                     ALU.bitwise_and))
                link(v.tensor_scalar(i, tmpc[:, 1:2], 1.0 / TOP, None, ALU.mult))
                link(v.reciprocal(s, i))

            def weights_max(u, gs):
                k = 0
                for m, name in enumerate(UNITS[u]["mats"]):
                    if name[:3] == "acc":
                        for h in range(2):
                            dve.wait_ge(st_free[h], BASIS_END[u])
                        v.tensor_reduce(mcol[:, k:k + 1], acc[:, m, :, :].rearrange("p q d -> p (q d)"), AX.X, ALU.max,
                                        apply_absolute_value=True)
                        k += 1
                        continue
                    for h in range(2):
                        dve.wait_ge(st_full[h], 16 * (gs[m] + 1))
                        v.tensor_reduce(mcol[:, k:k + 1], stage[:, h, :, :].rearrange("p q d -> p (q d)"),
                                        AX.X, ALU.max, apply_absolute_value=True).then_inc(st_free[h], 1)
                        k += 1
                for h in range(2):
                    dve.wait_ge(st_free[h], gs[m] + 1)
                v.tensor_reduce(mw[:, u % 2:u % 2 + 1], mcol[:, 0:k], AX.X, ALU.max).then_inc(s_mw, 1)

            def scales(u):
                unit = UNITS[u]
                dve.wait_ge(s_mwr, u + 1)
                power_scale(sW[:, u:u + 1], iW[:, u:u + 1], mwg[:, u:u + 1])
                v.nop().then_inc(s_sW, 1)
                link(v.tensor_tensor(ownc[:, u:u + 1], i_in[:, u:u + 1], iW[:, u:u + 1], ALU.mult))
                if unit["nz"] and u:
                    up = 2.0 ** unit["zexp"]
                    if u in (1, 2):
                        link(v.tensor_scalar(aggc[:, u, :], rdeg[:, :], ownc[:, u:u + 1], up, ALU.mult, ALU.mult))
                    else:
                        link(v.tensor_scalar(aggc[:, u, 0:1], ownc[:, u:u + 1], up, None, ALU.mult))
                if unit["bias"]:
                    dve.wait_ge(s_bias, 16 * u)
                if unit["nz"] and not unit["ln"]:
                    link(v.tensor_reduce(mb[:, :], bias[:, :], AX.X, ALU.max, apply_absolute_value=True))
                    if u == 1:
                        link(v.tensor_scalar(tmpc[:, 2:3], mwg[:, u:u + 1], 2.0 * D, None, ALU.mult))
                    else:
                        g = 1 if u == 3 else 0
                        dve.wait_ge(s_gmax, 1)
                        link(v.tensor_scalar(tmpc[:, 2:3], gmax[:, g:g + 1], 1.0, float(D), ALU.add, ALU.mult))
                        link(v.tensor_tensor(tmpc[:, 2:3], tmpc[:, 2:3], mwg[:, u:u + 1], ALU.mult))
                    link(v.tensor_tensor(tmpc[:, 3:4], tmpc[:, 2:3], mb[:, :], ALU.add))
                    power_scale(s_in[:, u + 1:u + 2], i_in[:, u + 1:u + 2], tmpc[:, 3:4])

            def basis_step(L, b, g, halves=(0, 1)):
                for h in halves:
                    dve.wait_ge(st_full[h], (g + 1) * 16)
                    for r in range(REL):
                        part = acc[:, r, 2 * h:2 * h + 2, :].rearrange("p q d -> p (q d)")
                        source = stage[:, h, :, :].rearrange("p q d -> p (q d)")
                        a = att[:, r, ds(b, 1)]
                        if isinstance(b, int) and b == 0:
                            last = v.tensor_scalar(part, source, a, None, ALU.mult)
                        else:
                            last = v.scalar_tensor_tensor(part, source, a, part, ALU.mult, ALU.add)
                    last.then_inc(st_free[h], 1)

            def planned(phase, place, p, j):
                for kind, what, g in plan.get((phase, place), []):
                    L, b0_, count = what
                    if b0_ == 0 and j == 0:
                        dve.wait_ge(s_att[L], 16)
                        if L:
                            dve.wait_ge(s_wlo, halves_split(3))
                    for s in range(count):
                        i = s + (0 if isinstance(p, int) else (p - 2) * count)
                        if isinstance(p, int):
                            bb, gg = b0_ + s, g + s
                        else:
                            bb, gg = p * count + (b0_ + s - 2 * count), p * count + (g + s - 2 * count)
                        if count == 1:
                            basis_step(L, bb, gg, (j,))
                        elif (s < (count + 1) // 2) == (j == 0):
                            basis_step(L, bb, gg)
                kind, u = phase
                if kind != "agg" or j == 0:
                    return
                gs = {what[1]: g for k, what, g in plan.get((phase, place + "+"), []) if k == "max"}
                if place == WHERE[u][0]:
                    weights_max(u + 1, gs)
                if place == WHERE[u][1]:
                    scales(u + 1)

            windows(0, 6)
            for u in (1, 3, 5):
                v.memset(s_in[:, u:u + 1], LN_SCALE)
                link(v.memset(i_in[:, u:u + 1], 1.0 / LN_SCALE))
            weights_max(0, {0: 0})
            dve.wait_ge(e_x, 32)
            v.tensor_reduce(xin[:, :], S[:, :, :].rearrange("p t d -> p (t d)"), AX.X, ALU.max,
                            apply_absolute_value=True).then_inc(s_xin, 1)
            windows(6, 12)
            dve.wait_ge(s_xmax, 1)
            power_scale(s_in[:, 0:1], i_in[:, 0:1], xmax[:, :])
            v.nop().then_inc(s_s0, 1)
            scales(0)
            windows(12, NWIN)

            dve.wait_ge(s_wev, 2 * NWIN)
            link(v.tensor_tensor(deg[:, :], dg[:, 0, :], dg[:, 1, :], ALU.add))
            link(v.tensor_scalar(dinv[:, :], deg[:, :], 1.0, None, ALU.add))
            v.reciprocal(dinv[:, :], dinv[:, :]).then_inc(s_dsq, 1)
            v.tensor_reduce(gin[:, 0:1], deg[:, :], AX.X, ALU.max)
            link(v.tensor_scalar(rdeg[:, :], deg[:, :], 1.0, None, ALU.max))
            link(v.reciprocal(rdeg[:, :], rdeg[:, :]))
            dve.wait_ge(s_dsq, 2)
            link(v.tensor_scalar(zsc0[:, :], dinv[:, :], 2.0 ** -UNITS[0]["zexp"], None, ALU.mult))
            assert chain[0] == Z_SCALED, chain[0]
            link(v.tensor_scalar(aggc[:, 0, :], dinv[:, :], ownc[:, 0:1], 2.0 ** UNITS[0]["zexp"], ALU.mult, ALU.mult))

            for u, unit in enumerate(UNITS):
                nz = unit["nz"]

                def z_low(t, j):
                    if u == 0:
                        scale = zsc0[:, ds(t, 1)]
                    elif nz == 2:
                        scale = zsc[:, 0, ds(t, 1)]
                    else:
                        scale = 2.0 ** -unit["zexp"]
                    dve.wait_ge(s_zhi[u], t * nz + 1)
                    v.scalar_tensor_tensor(Z[:, 0, 1, ds(t, 1), :], Dp[:, j, 0:1, :], scale,
                                           Z[:, 0, 0, ds(t, 1), :], ALU.mult, ALU.subtract).then_inc(s_zlo[u], 1)
                    if unit["own"] is not None:
                        o = unit["own"]
                        v.scalar_tensor_tensor(S[:, ds(t, 1), :], Dp[:, j, o:o + 1, :], ownc[:, u:u + 1],
                                               bias[:, :].rearrange("p (a d) -> p a d", a=1),
                                               ALU.mult, ALU.add).then_inc(s_own[u], 1)

                def stats(t, j):
                    dve.wait_ge(s_v[u], t + 1)
                    v.bn_stats(stt[:, j, :], w2[:, j, :]).then_inc(s_bs[u], 1)
                    dve.wait_ge(s_bs[u], t + 1)
                    dve.sem_inc(s_carry_dve, 1)
                    v.bn_aggr(mvr[:, j, :], stt[:, j, :]).then_inc(s_mv[u], 1)

                def normalize(t, j, scale, source):
                    dve.wait_ge(s_sd[u], t + 1)
                    v.reciprocal(rs[:, ds(t, 1)], sd[:, ds(t, 1)]).then_inc(s_rs[u], 1)
                    dve.wait_ge(s_rs[u], t * 2 + 1)
                    v.tensor_scalar(rsl[:, ds(t, 1)], rs[:, ds(t, 1)], scale, None, ALU.mult).then_inc(s_rs[u], 1)
                    dve.wait_ge(s_rs[u], t * 2 + 2)
                    v.tensor_scalar(w1[:, j:j + 1, :], source, mvr[:, j, 0:1],
                                    rsl[:, ds(t, 1)], ALU.subtract, ALU.mult).then_inc(s_r[u], 1)

                def gates(t, j, operand):
                    dve.wait_ge(s_r[u], t + 1)
                    if u == 3:
                        dve.wait_ge(s_hi[u], t + 1)
                    products = Z[:, 1, 0, 0, :] if u == 2 else w1[:, j, :]
                    for r in range(REL):
                        wait(dve, s_gl[u], t * 3 + r)
                        v.tensor_tensor_reduce(out=products, in0=operand[:, j, :], in1=gw[:, r, :], scale=1.0,
                                               scalar=0.0, op0=ALU.mult, op1=ALU.add,
                                               accum_out=glr[:, j, r:r + 1]).then_inc(s_gl[u], 1)
                    dve.wait_ge(s_gl[u], t * 3 + 2)
                    v.tensor_copy(glog[:, :, ds(t, 1)], glr[:, j, :]).then_inc(s_gl[u], 1)

                def after_agg(t, j):
                    dve.wait_ge(s_agg[u], t + 1)
                    if unit["ln"]:
                        wait(dve, s_ready[u + 1], t - 1)
                        wait(dve, s_xs[u], t - 1)
                    else:
                        wait(dve, s_hi[u], t - 1)
                        if u == 3:
                            wait(dve, s_gl[u], t * 3 - 3)
                    c = aggc[:, u, ds(t, 1)] if u in (1, 2) else aggc[:, u, 0:1]
                    v.scalar_tensor_tensor(w1[:, j:j + 1, :], Dp[:, j, 2:3, :], c, S[:, ds(t, 1), :],
                                           ALU.mult, ALU.add).then_inc(s_pre[u], 1)
                    first = isinstance(t, int) and t == 0
                    if unit["ln"]:
                        join_residual(t, j, ALU.max if u == 2 else ALU.add)
                        stats(t, j)
                        if u == 2 and not first:
                            gates(t - 1, 1 - j, w1)
                        normalize(t, j, LN_SCALE, w2[:, j:j + 1, :])
                    elif u == 3 and not first:
                        gates(t - 1, 1 - j, w2)

                def join_residual(t, j, op):
                    dve.wait_ge(s_pre[u], t + 1)
                    tile_moved(dve, s_xl[u], t, j)
                    tile_moved(dve, s_xst[u], t - 2, j)
                    v.scalar_tensor_tensor(w2[:, j, :], w1[:, j, :], 0.0, xr[:, j, :], op, ALU.add).then_inc(s_v[u], 1)

                def last_tile(t, j):
                    dve.wait_ge(s_d, t + (NT * u + 1))
                    tile_moved(dve, s_xst[u], t - 2, j)
                    v.scalar_tensor_tensor(w1[:, j, :], Dp[:, j, 0, :], ownc[:, u:u + 1], bias[:, :],
                                           ALU.mult, ALU.add).then_inc(s_own[u], 1)
                    dve.wait_ge(s_own[u], t + 1)
                    tile_moved(dve, s_xl[u], t, j)
                    v.tensor_tensor(w2[:, j, :], w1[:, j, :], xr[:, j, :], ALU.add).then_inc(s_v[u], 1)
                    stats(t, j)
                    normalize(t, j, 1.0, w2[:, j:j + 1, :])

                def conv_step(t, j):
                    dve.wait_ge(s_agg[0], t + 1)
                    v.scalar_tensor_tensor(S[:, ds(t, 1), :], Dp[:, j, 2:3, :], aggc[:, 0, ds(t, 1)],
                                           b0b.rearrange("p (a d) -> p a d", a=1), ALU.mult, ALU.add).then_inc(b_h, 1)
                    if isinstance(t, int) and t == 0:
                        return
                    if isinstance(t, int) and t == 1:
                        dve.wait_ge(b_mean, 1)
                        v.tensor_scalar(shift, T[:, 0, :], float(N) / P, None, ALU.mult).then_inc(b_shift, 1)
                        dve.wait_ge(b_shift, 1)
                        center(0)
                    center(t)

                def center(t):
                    dve.wait_ge(b_h, t + 1)
                    v.tensor_tensor(S[:, ds(t, 1), :], S[:, ds(t, 1), :], shift.rearrange("p (a d) -> p a d", a=1),
                                    ALU.subtract).then_inc(b_c, 1)

                if nz == 2:
                    dve.wait_ge(s_gt[u], 1)
                    v.tensor_scalar(zsc[:, :, :], gate[:, :, :], 2.0 ** -unit["zexp"], None, ALU.mult).then_inc(s_gz[u], 1)
                    dve.wait_ge(s_gz[u], 1)
                if not nz:
                    dve.wait_ge(s_ready[u], NT)
                    tiles(dve, last_tile)
                    break
                tiles(dve, z_low, lambda place, p, j: planned(("dense", u), place, p, j))
                if u in (2, 3):
                    dve.wait_ge(s_gw, 32 * (u - 1))
                if u == 0:
                    dve.wait_ge(s_bn, 48)
                tiles(dve, conv_step if u == 0 else after_agg, lambda place, p, j: planned(("agg", u), place, p, j))
                if u in (2, 3):
                    gates(NT - 1, 1, w1 if u == 2 else w2)
                if u > 0:
                    continue

                dve.wait_ge(s_dout, NT)
                v.tensor_reduce(gin[:, 1:2], dout[:, :], AX.X, ALU.max).then_inc(s_gin, 1)
                dve.wait_ge(b_mean, 3)
                link(v.tensor_copy(mean, T[:, 0, :]))
                link(v.tensor_tensor(bnsc, mean, mean, ALU.mult))
                link(v.tensor_tensor(bnsc, T[:, 1, :], bnsc, ALU.subtract))
                v.tensor_scalar(bnsc, bnsc, 0.0, EPS, ALU.max, ALU.add).then_inc(b_vr, 1)
                dve.wait_ge(b_sd, 1)
                link(v.reciprocal(csum, csq))
                link(v.tensor_tensor(bnsc, csum, gamb, ALU.mult))
                link(v.tensor_tensor(mean, mean, bnsc, ALU.mult))
                link(v.tensor_tensor(mean, betb, mean, ALU.subtract))

                def scale_tile(t):
                    if t in (5, 6):
                        dve.wait_ge(s_ready[1], t - 1)
                        dve.wait_ge(s_xs[0], t - 1)
                    elif t in (0, 1):
                        dve.wait_ge(b_q, NT)
                    else:
                        dve.wait_ge(b_g, t - 1)
                    v.tensor_tensor(w1[:, t % 2, :], S[:, t, :], bnsc, ALU.mult).then_inc(b_n1, 1)
                    dve.wait_ge(b_n1, t + 1)
                    v.tensor_tensor(w1[:, t % 2, :], w1[:, t % 2, :], mean, ALU.add).then_inc(b_n2, 1)

                def join_tile(t):
                    dve.wait_ge(b_g, t + 1)
                    dve.wait_ge(s_xa[0 if t < 5 else 1], 16 if t < 5 else 32)
                    v.scalar_tensor_tensor(S[:, t, :], x_again(t), 2.0, w2[:, t % 2, :],
                                           ALU.mult, ALU.add).then_inc(s_v[0], 1)
                    dve.wait_ge(s_v[0], t + 1)
                    v.bn_stats(stt[:, t % 2, :], S[:, t, :]).then_inc(s_bs[0], 1)
                    dve.wait_ge(s_bs[0], t + 1)
                    v.bn_aggr(mv[:, t, :], stt[:, t % 2, :]).then_inc(s_mv[0], 1)

                for half in range(2):
                    ts = range(5 * half, 5 * half + 5)
                    scale_tile(ts[0])
                    for t in ts[1:]:
                        scale_tile(t)
                        join_tile(t - 1)
                    join_tile(ts[-1])
                    dve.wait_ge(s_sd[0], half + 1)
                    cols = slice(5 * half, 5 * half + 5)
                    link(v.reciprocal(rs[:, cols], sd[:, cols]))
                    link(v.tensor_scalar(rsl[:, cols], rs[:, cols], LN_SCALE, None, ALU.mult))
                    for t in ts:
                        if t not in (0, 1, 5, 6):
                            dve.wait_ge(s_ready[1], t - 1)
                            dve.wait_ge(s_xs[0], t - 1)
                        v.tensor_scalar(w1[:, t % 2, :], S[:, t, :], mv[:, t, 0:1], rsl[:, t:t + 1],
                                        ALU.subtract, ALU.mult).then_inc(s_r[0], 1)
                planned(("bn", 0), "", 0, 0)
                planned(("bn", 0), "", 0, 1)


_OUTS = [((N, D), "float32")]


def kernel(**inputs):
    import concourse.bacc as _bacc
    from concourse import mybir as _mybir
    from concourse.bass_utils import run_bass_kernel_spmd as _run

    def chunked(a):
        flat = np.full((CHUNKS * P,), PAD, a.dtype)
        flat[:E] = a
        return flat.reshape(CHUNKS, P)

    g = {k: np.asarray(v) for k, v in inputs.items()}
    src, dst, typ = chunked(g["src"]), chunked(g["dst"]), chunked(g["edge_type_2"])
    typ = np.where(np.arange(CHUNKS * P).reshape(CHUNKS, P) < E, typ, 0).astype(typ.dtype)
    lay = {
        "x": g["x"], "src_t": src.T, "dst_t": dst.T, "typ_t": typ.T, "dst_r": dst.reshape(CHUNKS // 2, 2, P),
        "W0": g["L0_gnn_W"].T, "b0": g["L0_gnn_b"], "gamma": g["L0_gnn_gamma"], "beta": g["L0_gnn_beta"],
        "Ws1": g["L1_gnn_W_self1"], "Wn1": g["L1_gnn_W_neigh1"], "b1": g["L1_gnn_b1"],
        "Ws2": g["L1_gnn_W_self2"], "Wn2": g["L1_gnn_W_neigh2"], "b2": g["L1_gnn_b2"],
    }
    for n in ("1", "2"):
        for a, b in (("basis", "basis"), ("att", "att"), ("gate", "gate_w"), ("root", "root"), ("rb", "bias")):
            lay[a + n] = g[f"L2_gnn_{b}{n}"]
    lay.update({"V1": g["L3_gnn_W1"], "vb1": g["L3_gnn_b1"], "V2": g["L3_gnn_W2"], "vb2": g["L3_gnn_b2"]})

    nc = _bacc.Bacc("TRN2", target_bir_lowering=False, num_devices=1)
    arrays, args = {}, {}
    for name, a in lay.items():
        a = np.ascontiguousarray(a)
        arrays[f"in_{name}"] = a
        args[name] = nc.dram_tensor(f"in_{name}", a.shape, _mybir.dt.from_np(a.dtype), kind="ExternalInput").ap()
    for i, (shape, dtype) in enumerate(_OUTS):
        args["out"] = nc.dram_tensor(f"out_{i}", shape, _mybir.dt.from_np(np.dtype(dtype)), kind="ExternalOutput").ap()
    args["xres"] = nc.dram_tensor("xres", (NP, D), _mybir.dt.float32, kind="Internal").ap()
    resnorm_gnn_kernel(nc, **args)
    r = _run(nc, [arrays], core_ids=[0])
    return r.results[0]["out_0"]
```

```python
import concourse.bass as bass
from concourse import mybir
from contextlib import ExitStack
import numpy as np

N, D, E = 1250, 512, 21250
REL, BASES = 2, 30
P = 128
NT = -(-N // P)
NP = NT * P
LAST = N - (NT - 1) * P
KT = D // P
WIN = 64
NWIN = NP // WIN
CHUNKS = 170
PAD = 4000
OH = 4
LEAST = 3
EPS = 1e-5
LN_SCALE = 512.0
TOP = 2.0 ** 14

UNITS = [
    dict(mats=["W0"], nz=1, own=None, zexp=24, bias=None, ln=True),
    dict(mats=["Wn1", "Ws1"], nz=1, own=1, zexp=18, bias="b1", ln=False),
    dict(mats=["Wn2", "Ws2"], nz=1, own=1, zexp=24, bias="b2", ln=True),
    dict(mats=["acc0", "acc1", "root1"], nz=2, own=2, zexp=18, bias="rb1", ln=False),
    dict(mats=["acc0", "acc1", "root2"], nz=2, own=2, zexp=24, bias="rb2", ln=True),
    dict(mats=["V1"], nz=1, own=0, zexp=18, bias="vb1", ln=False),
    dict(mats=["V2"], nz=0, own=0, zexp=0, bias="vb2", ln=True),
]


def resnorm_gnn_kernel(nc, x, src_t, dst_t, typ_t, dst_r, W0, b0, gamma, beta,
                       Ws1, Wn1, b1, Ws2, Wn2, b2,
                       basis1, att1, gate1, root1, rb1, basis2, att2, gate2, root2, rb2,
                       V1, vb1, V2, vb2, out, xres):
    f32, f16, i32, u16 = mybir.dt.float32, mybir.dt.float16, mybir.dt.int32, mybir.dt.uint16
    ALU, ACT, AX = mybir.AluOpType, mybir.ActivationFunctionType, mybir.AxisListType
    RMAX = bass.bass_isa.ReduceOp.max
    dram = dict(W0=W0, Wn1=Wn1, Ws1=Ws1, Wn2=Wn2, Ws2=Ws2, root1=root1, root2=root2, V1=V1, V2=V2,
                b1=b1, b2=b2, rb1=rb1, rb2=rb2, vb1=vb1, vb2=vb2)
    NU = len(UNITS)
    ctx = ExitStack()
    with ctx:
        def sb(name, shape, dt):
            return ctx.enter_context(nc.sbuf_tensor(name, shape, dt))

        def sem(name):
            return ctx.enter_context(nc.semaphore(name))

        A = sb("A", [P, REL, NT, NP], f16)
        AT = sb("AT", [P, NT, NP], f16)
        S = sb("S", [P, NT, D], f32)
        S16 = S[:, :, :].bitcast(f16)
        Zraw = sb("Zraw", [P, REL * 2 * NT * D], f16)
        Z = Zraw[:, :].rearrange("p (r h t d) -> p r h t d", r=REL, h=2, t=NT)
        hT = sb("hT", [P, 2, 2, D], f16)
        W = sb("W", [P, 3, 2, KT, D], f16)
        acc = sb("acc", [P, REL, KT, D], f32)
        stage = sb("stage", [P, KT, D], f32)
        w1 = sb("w1", [P, 2, D], f32)
        w2 = sb("w2", [P, 2, D], f32)
        xr = sb("xr", [P, 2, D], f32)
        bias = sb("bias", [P, D], f32)
        gw = sb("gw", [P, REL, D], f32)
        ident = sb("ident", [P, P], f16)
        att = sb("att", [P, REL, BASES], f32)
        dg = sb("dg", [P, REL, NT], f32)
        dout = sb("dout", [P, NT], f32)
        deg = sb("deg", [P, NT], f32)
        rdeg = sb("rdeg", [P, NT], f32)
        dinv = sb("dinv", [P, NT], f32)
        zsc0 = sb("zsc0", [P, NT], f32)
        zsc = sb("zsc", [P, REL, NT], f32)
        aggc = sb("aggc", [P, NU, NT], f32)
        mcol = sb("mcol", [P, 2 * KT], f32)
        mw = sb("mw", [P, 2], f32)
        mwg = sb("mwg", [P, NU], f32)
        mb = sb("mb", [P, 1], f32)
        gin = sb("gin", [P, 2], f32)
        gmax = sb("gmax", [P, 2], f32)
        xin = sb("xin", [P, 1], f32)
        xmax = sb("xmax", [P, 1], f32)
        sW = sb("sW", [P, NU], f32)
        iW = sb("iW", [P, NU], f32)
        s_in = sb("s_in", [P, NU], f32)
        i_in = sb("i_in", [P, NU], f32)
        ownc = sb("ownc", [P, NU], f32)
        tmpc = sb("tmpc", [P, 4], f32)
        stt = sb("stt", [P, 2, 6], f32)
        mv = sb("mv", [P, NT, 2], f32)
        mvr = sb("mvr", [P, 2, 2], f32)
        glr = sb("glr", [P, 2, REL], f32)
        sd = sb("sd", [P, NT], f32)
        rs = sb("rs", [P, NT], f32)
        rsl = sb("rsl", [P, NT], f32)
        glog = sb("glog", [P, REL, NT], f32)
        gate = sb("gate", [P, REL, NT], f32)
        epsc = sb("epsc", [P, 1], f32)
        tbl = sb("tbl", [1, NWIN], i32)

        def carver(flat):
            at = [0]

            def view(nbytes):
                a = at[0]
                at[0] += nbytes // 2
                assert at[0] <= flat.shape[-1]
                return flat[:, a:at[0]]
            return view

        zview = carver(Zraw[:, :])
        wview = carver(w2[:, :, :].rearrange("p a d -> p (a d)").bitcast(f16))
        hview = carver(hT[:, :, :, :].rearrange("p a h d -> p (a h d)"))

        oh_src = zview(2 * NP * 2 * OH)
        oh_dst = zview(2 * P * 2 * OH)
        iota_n = hview(2 * NP)
        code = hview(2 * P)
        negw = hview(4 * NWIN).bitcast(f32)
        src_i, dst_i, typ_i = (wview(4 * CHUNKS).bitcast(i32) for _ in range(3))
        src_f, key_f = (wview(4 * CHUNKS).bitcast(f32) for _ in range(2))
        HC = CHUNKS // 2
        dstr = hview(4 * 2 * P).bitcast(i32).rearrange("p (g e) -> p g e", g=2)
        wlo = wview(4 * NWIN).bitcast(f32)
        whi = wview(4 * NWIN).bitcast(f32)
        cid = wview(4 * 4).bitcast(f32)
        mnx = wview(4 * 4).bitcast(f32)
        fl = wview(4 * 2 * NWIN).bitcast(f32)
        rng = wview(4 * 2 * NWIN).bitcast(f32)
        rngr = wview(4 * 2 * NWIN).bitcast(f32)
        w_st = zview(4 * NWIN).bitcast(f32)
        w_n = zview(4 * NWIN).bitcast(i32)
        w_p = zview(4 * NWIN).bitcast(f32)
        w_c = [zview(4 * NWIN).bitcast(f32) for _ in range(2)]
        b0b, gamb, betb, mean, bnsc, csum, csq, shift = (zview(4 * D).bitcast(f32) for _ in range(8))
        onesn = zview(4 * P).bitcast(f32)

        x_first = Zraw[:, 0:5 * 2 * D].bitcast(f32).rearrange("p (t d) -> p t d", t=5)
        x_next = W[:, 2, :, :, :].rearrange("p h k d -> p (h k d)").bitcast(f32).rearrange("p (t d) -> p t d", t=4)

        def x_again(t):
            return x_first[:, t, :] if t < 5 else x_next[:, t - 5, :] if t < 9 else xr[:, 1, :]

        T = ctx.enter_context(nc.psum_tensor("T", [P, 2, D], f32))
        Dp = ctx.enter_context(nc.psum_tensor("Dp", [P, 2, 3, D], f32))
        Df = Dp[:, :, :, :].rearrange("p a j d -> p a (j d)")

        LN = [u for u in range(NU) if UNITS[u]["ln"]]
        e_src, e_dst, e_typ, e_row, e_x = (sem(n) for n in ("e_src", "e_dst", "e_typ", "e_row", "e_x"))
        s_pad = sem("s_pad")
        s_const = sem("s_const")
        s_chain = sem("s_chain")
        s_carry_dve = sem("s_carry_dve")
        s_carry_act, s_carry_sp = sem("s_carry_act"), sem("s_carry_sp")
        s_pch = sem("s_pch")
        s_rng = sem("s_rng")
        s_rngr = sem("s_rngr")
        s_tbl = sem("s_tbl")
        s_oh = sem("s_oh")
        s_ohu = sem("s_ohu")
        s_win = sem("s_win")
        s_wev = sem("s_wev")
        s_at = sem("s_at")
        s_ate = sem("s_ate")
        s_xin, s_xmax, s_s0 = sem("s_xin"), sem("s_xmax"), sem("s_s0")
        s_gin = sem("s_gin")
        s_gmax = sem("s_gmax")
        s_dsq = sem("s_dsq")
        s_dout = sem("s_dout")
        s_att = [sem("s_att0"), sem("s_att1")]
        st_full = [sem(f"st_full{q}") for q in range(KT)]
        st_free = [sem(f"st_free{q}") for q in range(KT)]
        st_free_b = {q: sem(f"st_free_b{q}") for q in (1, 3)}
        s_bt = sem("s_bt")
        s_bq = sem("s_bq")
        s_bias = sem("s_bias")
        s_gw = sem("s_gw")
        s_bn = sem("s_bn")
        s_mw = sem("s_mw")
        s_mwr = sem("s_mwr")
        s_sW = sem("s_sW")
        s_wsc = sem("s_wsc")
        s_whi = sem("s_whi")
        s_wlo = sem("s_wlo")
        s_t = sem("s_t")
        s_hT = sem("s_hT")
        s_d = sem("s_d")
        s_ready = {u: sem(f"s_ready{u}") for u in range(NU)}
        s_zhi = {u: sem(f"s_zhi{u}") for u in range(6)}
        s_zlo = {u: sem(f"s_zlo{u}") for u in range(6)}
        s_zlp = {u: sem(f"s_zlp{u}") for u in (3, 4)}
        s_own = {u: sem(f"s_own{u}") for u in range(1, 7)}
        s_agg = {u: sem(f"s_agg{u}") for u in range(6)}
        s_pre = {u: sem(f"s_pre{u}") for u in range(1, 6)}
        s_v = {u: sem(f"s_v{u}") for u in LN}
        s_bs = sem("s_bs")
        s_mv = {u: sem(f"s_mv{u}") for u in LN}
        s_sd0 = sem("s_sd0")
        s_sd = sem("s_sd")
        s_rs = sem("s_rs")
        s_r = {u: sem(f"s_r{u}") for u in range(NU)}
        s_hi = {u: sem(f"s_hi{u}") for u in range(6)}
        s_xs = {u: sem(f"s_xs{u}") for u in LN[:3]}
        s_gl = sem("s_gl")
        s_gt, s_gz = sem("s_gt"), sem("s_gz")
        s_xl = {u: [sem(f"s_xl{u}_{j}") for j in range(2)] for u in LN[1:]}
        s_xst = {u: [sem(f"s_xst{u}_{j}") for j in range(2)] for u in LN}
        s_xa = [sem(f"s_xa{j}") for j in range(2)]
        b_h, b_sum, b_mean, b_shift, b_c, b_sq, b_q, b_var, b_sd, b_vr = (
            sem("b_" + n) for n in ("h", "sum", "mean", "shift", "c", "sq", "q", "var", "sd", "vr"))
        b_n1, b_n2, b_g = sem("b_n1"), sem("b_n2"), sem("b_g")
        x_sc, x_hi = sem("x_sc"), sem("x_hi")

        ds = bass.ds

        def wait(eng, s, n):
            if not isinstance(n, int) or n > 0:
                eng.wait_ge(s, n)

        def tile_moved(eng, s, t, j):
            if not isinstance(t, int) or t >= 0:
                eng.wait_ge(s[j], (t + (2 - j)) * 8)

        def tiles(eng, body, hook=None):
            def pair(place, p):
                for j in range(2):
                    body(p * 2 + j, j)
                    if hook:
                        hook(place, p, j)
            pair("P0", 0)
            pair("P1", 1)
            with eng.Fori(2, 4) as p:
                pair("loop", p)
            if hook:
                hook("after", 3, 1)
            pair("P4", 4)

        plan, events = {}, []

        def schedule(phase, place, kind, what, loop=1):
            g = sum(e[3] for e in events)
            events.append((kind, what, loop, loop * (what[2] if kind == "basis" else 1), g))
            plan.setdefault((phase, place), []).append((kind, what, g))

        def bases(phase, counts, b, L):
            for place in ("P0", "P1", "loop", "after", "P4"):
                n = counts.get(place, 0)
                if n:
                    loop = 2 if place == "loop" else 1
                    schedule(phase, place, "basis", (L, b, n), loop)
                    b += n * loop
                weights(phase, place)
            return b

        def plain_mats(u):
            return [m for m in UNITS[u]["mats"] if m[:3] != "acc"]

        WHERE = {u: ("P0", "P1", "after") for u in range(6)}
        WHERE[3] = ("after", "after", "after")

        def weights(phase, place):
            kind, u = phase
            if kind != "agg":
                return
            mats, u = UNITS[u + 1]["mats"], u + 1
            mx, first, rest = WHERE[u - 1]
            half = (len(mats) + 1) // 2
            for m, name in enumerate(mats):
                if place == mx and name[:3] != "acc":
                    schedule(phase, place + "+", "max", (u, m))
            for m, name in enumerate(mats):
                if place == (first if m < half else rest) and name[:3] != "acc":
                    schedule(phase, place + "+", "split", (u, m))

        schedule(("dense", -1), "", "max", (0, 0))
        schedule(("dense", -1), "", "split", (0, 0))
        b = bases(("dense", 0), dict(P1=1, P4=2), 0, 0)
        b = bases(("agg", 0), dict(loop=1), b, 0)
        SOLO = b
        b = bases(("dense", 1), dict(P0=2, P1=2, loop=2, P4=3), b, 0)
        b = bases(("agg", 1), dict(P0=1, loop=1), b, 0)
        b = bases(("dense", 2), dict(P0=2, P1=2, loop=2, P4=3), b, 0)
        assert b == BASES, b
        b = 0
        IN_Z = 2 * (BASES - SOLO + b)
        bases(("agg", 2), {}, 0, 1)
        b = bases(("dense", 3), dict(P0=3, P1=3, loop=3, P4=4), b, 1)
        b = bases(("agg", 3), dict(P0=5, P1=5, loop=2), b, 1)
        assert b == BASES, b
        for u in (4, 5):
            bases(("dense", u), {}, 0, 0)
            bases(("agg", u), {}, 0, 0)

        BASIS_END = {}
        for kind, what, loop, n, g in events:
            if kind == "basis":
                BASIS_END[3 if what[0] == 0 else 4] = g + n
        Z_SCALED = 37

        def halves_split(u):
            return sum(2 * len(v["mats"]) for v in UNITS[:u + 1])

        def window_range(eng, w):
            word = eng.value_load(tbl[0:1, ds(w, 1)], min_val=0, max_val=(NWIN * CHUNKS // 2 << 16) - 1)
            why = "packed so, from values clamped there"
            first = nc.s_assert_within(eng.snap(word & 255), 0, CHUNKS - 2 * LEAST, skip_runtime_bounds_check_because=why)
            pairs = nc.s_assert_within(eng.snap((word >> 8) & 255), LEAST, CHUNKS // 2, skip_runtime_bounds_check_because=why)
            return first, pairs, eng.snap(word >> 16)

        def planned_bases(phase, place, p, j, step):
            for kind, what, g in plan.get((phase, place), []):
                L, b0_, count = what
                for n in range(2 * count)[count * j:count * (j + 1)]:
                    s, h = n // 2, n % 2
                    if isinstance(p, int):
                        bb, gg = b0_ + s, g + s
                    else:
                        bb, gg = p * count + (b0_ + s - 2 * count), p * count + (g + s - 2 * count)
                    step(phase, L, bb, gg, h)

        def scaled(phase, q):
            if phase[1] == 3:
                return xr[:, q // 2, :]
            return Z[:, 1, 1, 0:4, :].rearrange("p t d -> p (t d)").bitcast(f32)[:, (q // 2) * D:(q // 2 + 1) * D]

        block = ctx.enter_context(nc.Block())

        @block.sync
        def _(sp):
            sp.dma_start(dstr[0:HC, :, :], dst_r).then_inc(e_row, 16)
            sp.dma_start(dst_i, dst_t).then_inc(e_dst, 16)
            sp.dma_start(typ_i, typ_t).then_inc(e_typ, 16)
            sp.dma_start(src_i, src_t).then_inc(e_src, 16)
            sp.wait_ge(s_pad, 1)
            sp.dma_start(S[:, 0:NT - 1, :], x[0:(NT - 1) * P, :].rearrange("(t p) d -> p t d", p=P)).then_inc(e_x, 16)
            sp.dma_start(S[0:LAST, NT - 1, :], x[(NT - 1) * P:N, :]).then_inc(e_x, 16)
            for tile, vec in ((b0b, b0), (gamb, gamma), (betb, beta)):
                sp.dma_start(tile, vec.rearrange("(a d) -> a d", a=1).broadcast_to([P, D])).then_inc(s_bn, 16)
            seen = set()

            def load_bias(u):
                if u >= 2:
                    sp.wait_ge(s_own[u - 1], NT)
                sp.dma_start(bias[:, :], dram[UNITS[u]["bias"]].rearrange("(a d) -> a d", a=1)
                             .broadcast_to([P, D])).then_inc(s_bias, 16)
                if u == 3:
                    load_gates(gate1)

            def load_gates(g):
                for r in range(REL):
                    sp.dma_start(gw[:, r, :], g[r:r + 1, :, 0].broadcast_to([P, D])).then_inc(s_gw, 16)

            def load_att(L):
                sp.dma_start(att[:, :, :].rearrange("p r b -> p (r b)"),
                             (att1, att2)[L].rearrange("(a r) b -> a (r b)", a=1)
                             .broadcast_to([P, REL * BASES])).then_inc(s_att[L], 16)

            shared_before = 0
            for kind, what, loop, n, g in events:
                if kind == "basis":
                    L, b0_, count = what
                    shared = L or b0_ >= SOLO
                    if shared:
                        shared_before += n
                    if b0_ == 0:
                        load_att(L)

                    def basis_loads(i):
                        for q in range(KT):
                            used, used_b = i + g, i + (L * BASES + b0_ - SOLO + 1)
                            wait(sp, st_free[q], used)
                            if shared and q % 2:
                                sp.sem_inc(s_carry_sp, 1)
                                sp.wait_ge(st_free_b[q], used_b)
                            sp.dma_start(stage[:, q:q + 1, :], (basis1, basis2)[L]
                                         [ds(i + b0_, 1), q * P:(q + 1) * P, :]
                                         .rearrange("a p d -> p a d")).then_inc(st_full[q], 16)

                    if n > 2:
                        with sp.Fori(0, n) as i:
                            basis_loads(i)
                    else:
                        for i in range(n):
                            basis_loads(i)
                    if L and b0_ == 0:
                        sp.wait_ge(s_gl, 3 * NT)
                        load_gates(gate2)
                else:
                    u, m = what
                    if kind == "max" and u not in seen and UNITS[u]["bias"]:
                        load_bias(u)
                        seen.add(u)
                    for q in range(KT):
                        wait(sp, st_free[q], g)
                        if shared_before and q % 2:
                            sp.wait_ge(st_free_b[q], shared_before + 1)
                        sp.dma_start(stage[:, q, :], dram[UNITS[u]["mats"][m]][q * P:(q + 1) * P, :]).then_inc(st_full[q], 16)

            def store(t, j):
                sp.wait_ge(s_r[NU - 1], t + 1)
                if isinstance(t, int) and t == NT - 1:
                    sp.dma_start(out[t * P:N, :], w1[0:LAST, j, :]).then_inc(s_xst[NU - 1][j], 16)
                else:
                    sp.dma_start(out[ds(t * P, P), :], w1[:, j, :]).then_inc(s_xst[NU - 1][j], 16)

            tiles(sp, store)
            for j in range(2):
                sp.wait_ge(s_xst[NU - 1][j], 8 * NT)

        @block.gpsimd
        def _(pool):
            kw = dict(allow_small_or_imprecise_dtypes=True)
            pool.iota(wlo, [[WIN, NWIN]], base=0, channel_multiplier=0, **kw).then_inc(s_const, 1)
            pool.iota(whi, [[WIN, NWIN]], base=WIN - 1, channel_multiplier=0, **kw).then_inc(s_const, 1)
            pool.iota(cid[:, 0:2], [[-1, 2]], base=256, channel_multiplier=-2, **kw).then_inc(s_const, 1)
            pool.iota(cid[:, 2:4], [[1, 2]], base=1, channel_multiplier=2, **kw).then_inc(s_const, 1)
            pool.memset(rng, 0.0).then_inc(s_const, 1)
            pool.iota(negw, [[-2 * WIN, NWIN]], base=0, channel_multiplier=0, **kw).then_inc(s_const, 1)
            pool.iota(code, [[1, REL], [2, WIN]], base=0, channel_multiplier=0, **kw).then_inc(s_const, 1)
            pool.iota(iota_n, [[1, NP]], base=0, channel_multiplier=0, **kw).then_inc(s_const, 1)
            pool.memset(ident[:, :], 0.0).then_inc(s_pch, 1)
            pool.wait_ge(s_pch, 1)
            pool.affine_select(out=ident[:, :], in_=ident[:, :], compare_op=ALU.not_equal, fill=1.0, base=0,
                               pattern=[[-1, P]], channel_multiplier=1).then_inc(s_const, 1)
            pool.wait_ge(s_rng, 1)
            pool.partition_all_reduce(rngr, rng, P, RMAX).then_inc(s_rngr, 1)
            pool.memset(epsc[:, :], EPS).then_inc(s_const, 1)
            pool.memset(onesn, 1.0 / N).then_inc(s_const, 1)
            pool.memset(csum, 0.0).then_inc(s_const, 1)
            pool.memset(csq, 0.0).then_inc(s_const, 1)

            def reduce_weights(u):
                pool.wait_ge(s_mw, u + 1)
                pool.partition_all_reduce(mwg[:, u:u + 1], mw[:, u % 2:u % 2 + 1], P, RMAX).then_inc(s_mwr, 1)

            def low_weights(u, m):
                for h in range(2):
                    n = halves_split(u - 1) + 2 * m + h
                    of_acc = UNITS[u]["mats"][m][:3] == "acc"
                    source = acc[:, m, 2 * h:2 * h + 2, :] if of_acc else stage[:, 2 * h:2 * h + 2, :]
                    pool.wait_ge(s_whi, n + 1)
                    pool.tensor_tensor(W[:, m, 1, 2 * h:2 * h + 2, :], source, W[:, m, 0, 2 * h:2 * h + 2, :],
                                       ALU.subtract).then_inc(s_wlo, 1)
                    if not of_acc:
                        pool.wait_ge(s_wlo, n + 1)
                        for q in (2 * h, 2 * h + 1):
                            pool.sem_inc(st_free[q], 1)

            def weight_work(u, place, j):
                mats = UNITS[u + 1]["mats"]
                mx, first, rest = WHERE[u]
                half = (len(mats) + 1) // 2
                if j == 1 and place == mx:
                    reduce_weights(u + 1)
                for m in range(len(mats)):
                    if j == 1 and place == (first if m < half else rest):
                        low_weights(u + 1, m)

            pool.wait_ge(s_xin, 1)
            pool.partition_all_reduce(xmax[:, :], xin[:, :], P, RMAX).then_inc(s_xmax, 1)
            reduce_weights(0)
            for t in range(NT):
                pool.wait_ge(x_hi, t + 1)
                pool.tensor_tensor(S16[:, t, D:2 * D], w1[:, t % 2, :], S16[:, t, 0:D], ALU.subtract).then_inc(s_ready[0], 1)
            low_weights(0, 0)

            for t in range(NT):
                rows = P if t < NT - 1 else LAST
                for src, total, ready, done in ((S[:, t, :], csum, b_c, b_sum), (w1[:, t % 2, :], csq, b_sq, b_q)):
                    pool.wait_ge(ready, t + 1)
                    wait(pool, done, t)
                    pool.tensor_tensor(total[0:rows, :], total[0:rows, :], src[0:rows, :], ALU.add).then_inc(done, 1)
                weight_work(0, {1: "P0", 3: "P1", NT - 1: "after"}.get(t), 1)
            pool.wait_ge(s_gin, 1)
            pool.partition_all_reduce(gmax[:, :], gin[:, :], P, RMAX).then_inc(s_gmax, 1)

            for u in range(0, 6):
                def low_part(t, j):
                    r = w1 if UNITS[u]["ln"] else w2
                    pool.wait_ge(s_hi[u], t + 1)
                    pool.tensor_tensor(S16[:, ds(t, 1), D:2 * D], r[:, j:j + 1, :], S16[:, ds(t, 1), 0:D],
                                       ALU.subtract).then_inc(s_ready[u + 1], 1)

                def low_product(t, j):
                    if u == 3 and isinstance(t, int) and t == 0:
                        pool.wait_ge(s_bq, IN_Z)
                    pool.wait_ge(s_zhi[u], t * 2 + 2)
                    pool.tensor_tensor(Z[:, 1, 1, ds(t, 1), :], w1[:, j:j + 1, :], Z[:, 1, 0, ds(t, 1), :],
                                       ALU.subtract).then_inc(s_zlp[u], 1)

                def add_scaled(phase, L, b, g, h):
                    q, n = 2 * h + 1, b * 2 + (2 * (L * BASES - SOLO) + h)
                    pool.wait_ge(s_bt, n + 1)
                    if isinstance(b, int) and b == 0:
                        pool.sem_inc(s_bq, 1)
                        return
                    wait(pool, s_bq, n - 1)
                    pool.tensor_tensor(acc[:, 1, q, :], acc[:, 1, q, :], scaled(phase, q), ALU.add).then_inc(s_bq, 1)

                def in_dense(place, p, j):
                    planned_bases(("dense", u), place, p, j, add_scaled)

                def in_agg(place, p, j):
                    planned_bases(("agg", u), place, p, j, add_scaled)
                    weight_work(u, place, j)

                if UNITS[u]["nz"] == 2:
                    tiles(pool, low_product, in_dense)
                elif u:
                    tiles(pool, lambda t, j: None, in_dense)
                if u == 0:
                    pool.wait_ge(b_vr, 2)
                    for t in range(NT):
                        wait(pool, b_g, t - 1)
                        pool.tensor_tensor(w1[:, t % 2, :], S[:, t, :], bnsc, ALU.mult).then_inc(b_n1, 1)
                    for t in range(NT):
                        low_part(t, t % 2)
                else:
                    tiles(pool, low_part, in_agg)

        @block.tensor
        def _(pe):
            def pair_product(ready, slot, j, start, stop):
                pe.wait_ge(s_oh, ready)
                for q in range(2):
                    for c in range(0, NP, D):
                        w = min(D, NP - c)
                        last = nc.tensor.matmul(Df[:, j, c:c + w], oh_dst[:, ds(slot * (2 * P) + q * P, P)],
                                                oh_src[:, ds(slot * (2 * NP) + (q * NP + c), w)],
                                                start=start and q == 0, stop=stop and q == 1)
                last.then_inc(s_win if stop else s_ohu, 1)

            def window(w, j):
                _, pairs, base = window_range(pe, w)
                wait(pe, s_wev, w * 2 - 2)
                pair_product(base + 1, pe.snap(base & (OH - 1)), j, True, False)
                with pe.Fori(1, pairs - 1) as i:
                    pair_product(base + i + 1, pe.snap((base + i) & (OH - 1)), j, False, False)
                pair_product(base + pairs, pe.snap((base + pairs + (OH - 1)) & (OH - 1)), j, False, True)
                pe.wait_ge(s_win, w + 1)
                pe.sem_inc(s_ohu, 1)

            def turn_counts(t, g):
                pe.wait_ge(s_wev, t * 4 + 4)
                wait(pe, s_ate, t * 3 + (g - (1, 3, 2)[g] + 1))
                for q, m in enumerate(range(4 * g, min(4 * g + 4, NT))):
                    for r in range(REL):
                        last = nc.tensor.matmul(T[:, g % 2, q * P:(q + 1) * P],
                                                A[:, r, ds(t, 1), m * P:(m + 1) * P].rearrange("p a c -> p (a c)"),
                                                ident[:, :], start=(r == 0), stop=(r == REL - 1))
                last.then_inc(s_at, 1)

            pe.sem_inc(s_ohu, OH)
            pe.wait_ge(s_const, 9)
            pe.wait_ge(s_tbl, 1)
            window(0, 0)
            window(1, 1)
            for t in range(1, 2):
                window(2 * t, 0)
                turn_counts(t - 1, 0)
                turn_counts(t - 1, 1)
                window(2 * t + 1, 1)
                turn_counts(t - 1, 2)
            with pe.Fori(2, NT) as t:
                window(t * 2, 0)
                turn_counts(t - 1, 0)
                turn_counts(t - 1, 1)
                window(t * 2 + 1, 1)
                turn_counts(t - 1, 2)
            for g in range(3):
                turn_counts(NT - 1, g)
            pe.wait_ge(s_ate, 3 * NT)

            for u, unit in enumerate(UNITS):
                nm, nz = len(unit["mats"]), unit["nz"]

                def turn(t, j, u=u):
                    pe.wait_ge(s_ready[u], t + 1)
                    wait(pe, s_hT, t + NT * u)
                    for h in range(2):
                        for k in range(KT):
                            last = nc.tensor.matmul(T[:, h, k * P:(k + 1) * P],
                                                    S16[:, ds(t, 1), h * D + k * P:h * D + (k + 1) * P]
                                                    .rearrange("p a c -> p (a c)"), ident[:, :], start=True, stop=True)
                    last.then_inc(s_t, 1)

                def dense(t, j):
                    if not (isinstance(t, int) and t == NT - 1):
                        turn(t + 1, 1 - j)
                    pe.wait_ge(s_hT, t + (NT * u + 1))
                    if nz:
                        wait(pe, s_zlo[u], t - 1)
                    if nz == 2:
                        wait(pe, s_zlp[u], t - 1)
                    if unit["own"] is not None:
                        wait(pe, s_own[u], t - 1)
                    if isinstance(t, int) and t < 2 and nm == 3:
                        pe.wait_ge(s_pre[u - 1], NT - 1 + t)
                    for m in range(nm):
                        if isinstance(t, int) and t == 0:
                            pe.wait_ge(s_wlo, halves_split(u - 1) + 2 * m + 2)
                        n = 0
                        for hp, wp in ((0, 0), (1, 0), (0, 1)):
                            for k in range(KT):
                                last = nc.tensor.matmul(Dp[:, j, m, :], hT[:, j, hp, k * P:(k + 1) * P],
                                                        W[:, m, wp, k, :], start=(n == 0), stop=(n == 3 * KT - 1))
                                n += 1
                    last.then_inc(s_d, 1)

                def agg(t, j):
                    wait(pe, s_pre[u] if u else b_h, t - 1)
                    if nm == 3 and isinstance(t, int) and t < 2:
                        pe.wait_ge(s_own[u], NT - 1 + t)
                    if u and isinstance(t, int) and t == NT - 2:
                        turn(0, 0, u + 1)
                    rels = [(A[:, r], r) for r in range(REL)] if nz == 2 else [(AT, 0)]
                    n, count = 0, 2 * NT * nz
                    for a, r in rels:
                        for k in range(NT):
                            if isinstance(t, int) and t == 0:
                                pe.wait_ge(s_zlp[u] if r else s_zlo[u], k + 1)
                            for h in range(2):
                                last = nc.tensor.matmul(Dp[:, j, 2, :], a[:, k, ds(t * P, P)], Z[:, r, h, k, :],
                                                        start=(n == 0), stop=(n == count - 1 and u > 0))
                                n += 1
                    if u == 0:
                        for h in range(2):
                            last = nc.tensor.matmul(Dp[:, j, 2, :], ident[:, :],
                                                    Z[:, 0, h, ds(t, 1), :].rearrange("p a d -> p (a d)"),
                                                    start=False, stop=(h == 1))
                    last.then_inc(s_agg[u], 1)
                    if u == 0 and isinstance(t, int) and t == 1:
                        column_sum(0, S[:, 0, :], b_h, 1)

                def column_sum(bank, total, ready, n):
                    pe.wait_ge(ready, n)
                    nc.tensor.matmul(T[:, bank, :], onesn, total, start=True, stop=True).then_inc(b_mean, 1)

                if u < 2:
                    turn(0, 0)
                tiles(pe, dense)
                if nz:
                    if u == 0:
                        pe.wait_ge(s_hT, NT)
                        pe.wait_ge(s_const, 11)
                    tiles(pe, agg)
                if u == 0:
                    pe.wait_ge(b_shift, 1)
                    column_sum(0, csum, b_sum, NT)
                    column_sum(1, csq, b_q, NT)

        @block.scalar
        def _(act):
            def window_out(w, j, t):
                act.wait_ge(s_win, w + 1)
                for r in range(REL):
                    nc.scalar.activation(A[WIN * j:WIN * (j + 1), r, ds(t, 1), :],
                                         Dp[WIN * r:WIN * (r + 1), j, :, :].rearrange("p j d -> p (j d)")[:, 0:NP],
                                         ACT.Copy, accum_out=dg[WIN * j:WIN * (j + 1), r, ds(t, 1)]).then_inc(s_wev, 1)

            def turned_out(t, g):
                act.wait_ge(s_at, t * 3 + (g + 1))
                n = min(4, NT - 4 * g)
                nc.scalar.activation(AT[:, 4 * g:4 * g + n, ds(t * P, P)],
                                     T[:, g % 2, 0:n * P].rearrange("p (m c) -> p m c", m=n), ACT.Copy).then_inc(s_ate, 1)

            def tile_out(t):
                window_out(t * 2, 0, t)
                turned_out(t - 1, 0)
                turned_out(t - 1, 1)
                window_out(t * 2 + 1, 1, t)
                turned_out(t - 1, 2)

            def split_x(t):
                wait(act, s_ready[0], t - 1)
                nc.scalar.activation(w1[:, t % 2, :], S[:, t, :], ACT.Copy, scale=s_in[:, 0:1]).then_inc(x_sc, 1)
                act.wait_ge(x_sc, t + 1)
                nc.scalar.activation(S16[:, t, 0:D], w1[:, t % 2, :], ACT.Copy).then_inc(x_hi, 1)

            def high_weights(u, m, g):
                of_acc = UNITS[u]["mats"][m][:3] == "acc"
                act.wait_ge(s_sW, u + 1)
                n = halves_split(u - 1) + 2 * m
                source = [acc[:, m, 2 * h:2 * h + 2, :] if of_acc else stage[:, 2 * h:2 * h + 2, :] for h in range(2)]
                for h in range(2):
                    if not of_acc:
                        for q in (2 * h, 2 * h + 1):
                            act.wait_ge(st_full[q], 16 * (g + 1))
                    nc.scalar.activation(source[h], source[h], ACT.Copy, scale=sW[:, u:u + 1]).then_inc(s_wsc, 1)
                for h in range(2):
                    act.wait_ge(s_wsc, n + h + 1)
                    nc.scalar.activation(W[:, m, 0, 2 * h:2 * h + 2, :], source[h], ACT.Copy).then_inc(s_whi, 1)

            def weight_work(u, place, j):
                mats = UNITS[u + 1]["mats"]
                _, first, rest = WHERE[u]
                half = (len(mats) + 1) // 2
                for m in range(len(mats)):
                    if m < half:
                        planned_at, done_at = first, ("P4", 0) if u == 3 else (first, 1)
                    else:
                        planned_at, done_at = rest, ("P4", 1 if u == 3 else 0)
                    if (place, j) == done_at:
                        at_g = {what[1]: g for kind, what, g in plan.get((("agg", u), planned_at + "+"), [])
                                if kind == "split"}
                        high_weights(u + 1, m, at_g.get(m))

            def scale_basis(phase, L, b, g, h):
                first = isinstance(b, int) and b == 0
                if first:
                    act.wait_ge(s_att[L], 16)
                    act.wait_ge(s_wlo, halves_split(2) + 4)
                q, n = 2 * h + 1, b * 2 + (2 * (L * BASES - SOLO) + h)
                act.wait_ge(st_full[q], (g + 1) * 16)
                act.sem_inc(s_carry_act, 1)
                wait(act, s_bq, n - 1)
                act.sem_inc(s_carry_act, 1)
                nc.scalar.activation(acc[:, 1, q, :] if first else scaled(phase, q), stage[:, q, :],
                                     ACT.Copy, scale=att[:, 1, ds(b, 1)]).then_inc(s_bt, 1)
                act.wait_ge(s_bt, n + 1)
                act.sem_inc(st_free_b[q], 1)

            for q in (1, 3):
                act.sem_inc(st_free_b[q], 1)
            window_out(0, 0, 0)
            window_out(1, 1, 0)
            tile_out(1)
            with act.Fori(2, NT - 2) as t:
                tile_out(t)
            act.wait_ge(s_s0, 1)
            for t in range(0, 5):
                split_x(t)
            tile_out(NT - 2)
            for t in range(5, NT):
                split_x(t)
            high_weights(0, 0, 1)
            tile_out(NT - 1)
            act.wait_ge(s_dsq, 1)
            nc.scalar.activation(dinv[:, :], dinv[:, :], ACT.Sqrt).then_inc(s_dsq, 1)
            for g in range(3):
                turned_out(NT - 1, g)

            for u, unit in enumerate(UNITS):
                nz = unit["nz"]

                def hT_out(t, j, u=u):
                    act.wait_ge(s_t, t + (NT * u + 1))
                    wait(act, s_d, t + (NT * u - 1))
                    nc.scalar.activation(hT[:, j, :, :], T[:, :, :], ACT.Copy).then_inc(s_hT, 1)

                def load_residual(t, j):
                    act.dma_start(xr[:, j, :], xres[ds(t * P, P), :]).then_inc(s_xl[u][j], 16)

                def ln_step(t, j):
                    if isinstance(t, int) and t == NT - 2:
                        hT_out(0, 0, u + 1)
                    act.wait_ge(s_mv[u], t + 1)
                    nc.scalar.activation(sd[:, ds(t, 1)], mvr[:, j, 1:2], ACT.Sqrt,
                                         bias=epsc[:, 0:1]).then_inc(s_sd, 1)
                    if not (isinstance(t, int) and t >= NT - 2):
                        load_residual(t + 2, j)
                    act.wait_ge(s_r[u], t + 1)
                    nc.scalar.activation(S16[:, ds(t, 1), 0:D], w1[:, j:j + 1, :], ACT.Copy).then_inc(s_hi[u], 1)
                    nc.scalar.activation(w2[:, j, :], w1[:, j, :], ACT.Copy, scale=1.0 / LN_SCALE).then_inc(s_xs[u], 1)
                    act.wait_ge(s_xs[u], t + 1)
                    act.dma_start(xres[ds(t * P, P), :], w2[:, j, :]).then_inc(s_xst[u][j], 16)

                def last_deviation(t, j):
                    act.wait_ge(s_mv[u], t + 1)
                    nc.scalar.activation(sd[:, ds(t, 1)], mvr[:, j, 1:2], ACT.Sqrt,
                                         bias=epsc[:, 0:1]).then_inc(s_sd, 1)
                    if not (isinstance(t, int) and t >= NT - 2):
                        load_residual(t + 2, j)

                def z_out(t, j):
                    if not (isinstance(t, int) and (t == NT - 1 or t == 0 and u in (1, 3, 4))):
                        hT_out(t + 1, 1 - j)
                    if not nz:
                        if not (isinstance(t, int) and t == 0):
                            last_deviation(t - 1, 1 - j)
                        return
                    act.wait_ge(s_d, t + (NT * u + 1))
                    for r in range(nz):
                        if u == 0:
                            scale = zsc0[:, ds(t, 1)]
                        elif nz == 2:
                            scale = zsc[:, r, ds(t, 1)]
                        else:
                            scale = 2.0 ** -unit["zexp"]
                        nc.scalar.activation(Z[:, r, 0, ds(t, 1), :], Dp[:, j, r:r + 1, :], ACT.Copy,
                                             scale=scale).then_inc(s_zhi[u], 1)
                        if nz == 2 and r == 0:
                            if isinstance(t, int) and t < 2:
                                act.wait_ge(s_ready[u], NT - 1 + t)
                                if u == 3:
                                    act.wait_ge(s_xs[2], NT - 1 + t)
                            wait(act, s_zlp[u], t - 1)
                            nc.scalar.activation(w1[:, j, :], Dp[:, j, 1, :], ACT.Copy,
                                                 scale=zsc[:, 1, ds(t, 1)])

                if u == 1:
                    for j in range(2):
                        act.wait_ge(s_xst[0][j], 8 * NT)
                if nz == 2:
                    hT_out(1, 1)
                    act.wait_ge(s_gl, 3 * NT * (u - 2))
                    nc.scalar.activation(gate[:, :, :], glog[:, :, :], ACT.Sigmoid,
                                         scale=i_in[:, u:u + 1]).then_inc(s_gt, 1)
                    act.wait_ge(s_gz, u - 2)
                if u == 0:
                    act.wait_ge(s_chain, Z_SCALED)
                if unit["ln"] and u:
                    for j in range(2):
                        act.wait_ge(s_xst[u - 2][j], 8 * NT)
                    load_residual(0, 0)
                    load_residual(1, 1)
                if u == 0:
                    hT_out(0, 0)
                tiles(act, z_out, lambda place, p, j: u and planned_bases(("dense", u), place, p, j, scale_basis))

                def relu_step(t, j):
                    if isinstance(t, int) and t == NT - 2:
                        hT_out(0, 0, u + 1)
                    act.wait_ge(s_pre[u], t + 1)
                    wait(act, s_ready[u + 1], t - 1)
                    if u == 3:
                        if not (isinstance(t, int) and t < 2):
                            act.wait_ge(s_gl, t * 3 + (3 * NT - 3))
                    nc.scalar.activation(w2[:, j, :], w1[:, j, :], ACT.Relu, scale=s_in[:, u + 1:u + 2]).then_inc(s_r[u], 1)
                    nc.scalar.activation(S16[:, ds(t, 1), 0:D], w1[:, j:j + 1, :], ACT.Relu,
                                         scale=s_in[:, u + 1:u + 2]).then_inc(s_hi[u], 1)

                def square_step(t, j):
                    act.wait_ge(b_c, t + 1)
                    wait(act, b_q, t - 1)
                    nc.scalar.activation(w1[:, j:j + 1, :], S[:, ds(t, 1), :], ACT.Square).then_inc(b_sq, 1)
                    wait(act, s_dout, t)
                    nc.scalar.activation(W[:, 2, :, :, :].rearrange("p h k d -> p (h k d)")[:, 0:NP]
                                         .rearrange("p (a c) -> p a c", a=1), AT[:, ds(t, 1), :], ACT.Copy,
                                         accum_out=dout[:, ds(t, 1)]).then_inc(s_dout, 1)

                def hook(place, p, j):
                    if u:
                        planned_bases(("agg", u), place, p, j, scale_basis)
                    weight_work(u, place, j)

                if not nz:
                    last_deviation(NT - 1, 1)
                elif not unit["ln"]:
                    for j in range(2):
                        act.wait_ge(s_xst[u - 1][j], 8 * NT)
                    tiles(act, relu_step, hook)
                elif u:
                    tiles(act, ln_step, hook)
                else:
                    tiles(act, square_step, hook)
                    act.wait_ge(s_agg[0], NT)
                    act.wait_ge(s_dout, NT)
                    act.dma_start(x_first, x[0:5 * P, :].rearrange("(t p) d -> p t d", p=P)).then_inc(s_xa[0], 16)
                    act.dma_start(x_next, x[5 * P:9 * P, :].rearrange("(t p) d -> p t d", p=P)).then_inc(s_xa[1], 16)
                    act.wait_ge(s_pad, 2)
                    act.dma_start(xr[0:LAST, 1, :], x[9 * P:N, :]).then_inc(s_xa[1], 16)
                    act.wait_ge(b_vr, 1)
                    nc.scalar.activation(csq, bnsc, ACT.Sqrt).then_inc(b_sd, 1)
                    for t in range(NT):
                        act.wait_ge(b_n2, t + 1)
                        wait(act, s_v[0], t - 1)
                        nc.scalar.activation(w2[:, t % 2, :], w1[:, t % 2, :], ACT.Gelu).then_inc(b_g, 1)
                    act.wait_ge(s_mv[0], NT)
                    nc.scalar.activation(sd[:, :], mv[:, :, 1], ACT.Sqrt, bias=epsc[:, 0:1]).then_inc(s_sd0, 1)
                    for t in range(NT):
                        act.wait_ge(s_r[0], t + 1)
                        nc.scalar.activation(S16[:, t, 0:D], w1[:, t % 2, :], ACT.Copy).then_inc(s_hi[0], 1)
                        act.wait_ge(s_xs[0], t + 1)
                        act.dma_start(xres[t * P:(t + 1) * P, :], x_again(t)).then_inc(s_xst[0][t % 2], 16)
                        if t == 3:
                            hT_out(0, 0, 1)
                        if t == 6:
                            hT_out(1, 1, 1)

        @block.vector
        def _(dve):
            v = nc.vector
            chain = [0]

            def link(ins):
                chain[0] += 1
                ins.then_inc(s_chain, 1)
                dve.wait_ge(s_chain, chain[0])

            v.memset(S[:, NT - 1, :], 0.0).then_inc(s_pad, 1)
            v.memset(xr[:, 1, :], 0.0).then_inc(s_pad, 1)
            dve.wait_ge(e_row, 16)
            v.tensor_reduce(mnx[0:HC, 0:2], dstr[0:HC, :, :], AX.X, ALU.min)
            link(v.tensor_reduce(mnx[0:HC, 2:4], dstr[0:HC, :, :], AX.X, ALU.max))
            dve.wait_ge(s_const, 5)
            for g in range(2):
                link(v.tensor_scalar(fl[0:HC, 0:NWIN], wlo[0:HC, :], mnx[0:HC, 2 + g:3 + g], None, ALU.is_le))
                link(v.scalar_tensor_tensor(fl[0:HC, NWIN:2 * NWIN], whi[0:HC, :], mnx[0:HC, g:g + 1],
                                            fl[0:HC, 0:NWIN], ALU.is_ge, ALU.mult))
                for q in range(2):
                    part = rng[0:HC, q * NWIN:(q + 1) * NWIN]
                    last = v.scalar_tensor_tensor(part, fl[0:HC, NWIN:2 * NWIN], cid[0:HC, 2 * q + g:2 * q + g + 1],
                                                  part, ALU.mult, ALU.max)
                link(last)
            v.nop().then_inc(s_rng, 1)
            dve.wait_ge(e_typ, 16)
            dve.wait_ge(e_dst, 16)
            dve.wait_ge(e_src, 16)
            v.tensor_copy(src_f, src_i)
            link(v.tensor_copy(key_f, typ_i))
            link(v.scalar_tensor_tensor(key_f, dst_i, 2.0, key_f, ALU.mult, ALU.add))
            dve.wait_ge(s_rngr, 1)
            link(v.tensor_scalar(w_st, rngr[:, 0:NWIN], -1.0, 256.0, ALU.mult, ALU.add))
            link(v.tensor_scalar(w_st, w_st, float(CHUNKS - 2 * LEAST), None, ALU.min))
            link(v.tensor_tensor(w_n, rngr[:, NWIN:2 * NWIN], w_st, ALU.subtract))
            link(v.tensor_scalar(w_n, w_n, float(2 * LEAST), 1.0, ALU.max, ALU.add))
            link(v.tensor_scalar(w_n, w_n, 0x1FE, None, ALU.bitwise_and))
            link(v.tensor_scalar(w_p, w_n, 0.5, None, ALU.mult))
            a, step = 0, 1
            while step < NWIN:
                source = w_c[a] if step > 1 else w_p
                v.tensor_copy(w_c[1 - a][:, 0:step], source[:, 0:step])
                link(v.tensor_tensor(w_c[1 - a][:, step:NWIN], source[:, step:NWIN], source[:, 0:NWIN - step], ALU.add))
                a, step = 1 - a, 2 * step
            halfword = tbl[0:1, :].bitcast(u16).rearrange("p (w h) -> p w h", h=2)
            v.scalar_tensor_tensor(halfword[:, :, 0], w_p[0:1, :], 256.0, w_st[0:1, :], ALU.mult, ALU.add)
            v.tensor_tensor(halfword[:, :, 1], w_c[a][0:1, :], w_p[0:1, :], ALU.subtract).then_inc(s_tbl, 1)
            dve.wait_ge(s_tbl, 1)
            dve.wait_ge(s_const, 8)

            def windows(w0, w1_):
                with dve.Fori(w0, w1_) as w:
                    first, pairs, base = window_range(dve, w)
                    with dve.Fori(0, pairs) as i:
                        c = nc.s_assert_within(dve.snap(first + i * 2), 0, CHUNKS - 2, skip_runtime_bounds_check_because=
                                               "the chunks of a window end at the last chunk")
                        n = dve.snap(base + i)
                        slot = dve.snap(n & (OH - 1))
                        dve.wait_ge(s_ohu, n + 1)
                        v.scalar_tensor_tensor(oh_dst[:, ds(slot * (2 * P), 2 * P)].rearrange("p (c o) -> p c o", c=2),
                                               key_f[:, ds(c, 2)].rearrange("p (c o) -> p c o", o=1).broadcast_to([P, 2, P]),
                                               negw[:, ds(w, 1)],
                                               code.rearrange("p (c o) -> p c o", c=1).broadcast_to([P, 2, P]),
                                               ALU.add, ALU.is_equal)
                        for q in range(2):
                            last = v.tensor_scalar(oh_src[:, ds(slot * (2 * NP) + q * NP, NP)], iota_n,
                                                   src_f[:, ds(c + q, 1)], None, ALU.is_equal)
                        last.then_inc(s_oh, 1)

            def power_scale(s, i, m):
                link(v.tensor_scalar(tmpc[:, 0:1], m, 1e-30, None, ALU.max))
                link(v.tensor_scalar(tmpc[:, 1:2].bitcast(i32), tmpc[:, 0:1].bitcast(i32), 0x7F800000, None,
                                     ALU.bitwise_and))
                link(v.tensor_scalar(i, tmpc[:, 1:2], 1.0 / TOP, None, ALU.mult))
                link(v.reciprocal(s, i))

            def weights_max(u, gs):
                k = 0
                for m, name in enumerate(UNITS[u]["mats"]):
                    if name[:3] == "acc":
                        for q in range(KT):
                            dve.wait_ge(st_free[q], BASIS_END[u])
                        dve.wait_ge(s_bq, 2 * (BASES * (u - 2) - SOLO))
                        v.tensor_reduce(mcol[:, k:k + 1], acc[:, m, :, :].rearrange("p q d -> p (q d)"), AX.X, ALU.max,
                                        apply_absolute_value=True)
                        k += 1
                        continue
                    for q in range(KT):
                        dve.wait_ge(st_full[q], 16 * (gs[m] + 1))
                        v.tensor_reduce(mcol[:, k:k + 1], stage[:, q, :], AX.X, ALU.max,
                                        apply_absolute_value=True).then_inc(st_free[q], 1)
                        k += 1
                dve.wait_ge(st_free[KT - 1], gs[m] + 1)
                v.tensor_reduce(mw[:, u % 2:u % 2 + 1], mcol[:, 0:k], AX.X, ALU.max).then_inc(s_mw, 1)

            def scales(u):
                unit = UNITS[u]
                dve.wait_ge(s_mwr, u + 1)
                power_scale(sW[:, u:u + 1], iW[:, u:u + 1], mwg[:, u:u + 1])
                v.nop().then_inc(s_sW, 1)
                link(v.tensor_tensor(ownc[:, u:u + 1], i_in[:, u:u + 1], iW[:, u:u + 1], ALU.mult))
                if unit["nz"] and u:
                    up = 2.0 ** unit["zexp"]
                    if u in (1, 2):
                        link(v.tensor_scalar(aggc[:, u, :], rdeg[:, :], ownc[:, u:u + 1], up, ALU.mult, ALU.mult))
                    else:
                        link(v.tensor_scalar(aggc[:, u, 0:1], ownc[:, u:u + 1], up, None, ALU.mult))
                if unit["bias"]:
                    dve.wait_ge(s_bias, 16 * u)
                if unit["nz"] and not unit["ln"]:
                    link(v.tensor_reduce(mb[:, :], bias[:, :], AX.X, ALU.max, apply_absolute_value=True))
                    if u == 1:
                        link(v.tensor_scalar(tmpc[:, 2:3], mwg[:, u:u + 1], 2.0 * D, None, ALU.mult))
                    else:
                        g = 1 if u == 3 else 0
                        dve.wait_ge(s_gmax, 1)
                        link(v.tensor_scalar(tmpc[:, 2:3], gmax[:, g:g + 1], 1.0, float(D), ALU.add, ALU.mult))
                        link(v.tensor_tensor(tmpc[:, 2:3], tmpc[:, 2:3], mwg[:, u:u + 1], ALU.mult))
                    link(v.tensor_tensor(tmpc[:, 3:4], tmpc[:, 2:3], mb[:, :], ALU.add))
                    power_scale(s_in[:, u + 1:u + 2], i_in[:, u + 1:u + 2], tmpc[:, 3:4])

            def basis_step(phase, L, b, g, h):
                if isinstance(b, int) and b == 0:
                    dve.wait_ge(s_att[L], 16)
                    if L:
                        dve.wait_ge(s_wlo, halves_split(2) + 4)
                solo = phase[1] == 0
                for q in (2 * h, 2 * h + 1):
                    dve.wait_ge(st_full[q], (g + 1) * 16)
                    for r in range(REL if solo or q == 2 * h else 1):
                        part = acc[:, r, q, :]
                        a = att[:, r, ds(b, 1)]
                        if isinstance(b, int) and b == 0:
                            last = v.tensor_scalar(part, stage[:, q, :], a, None, ALU.mult)
                        else:
                            last = v.scalar_tensor_tensor(part, stage[:, q, :], a, part, ALU.mult, ALU.add)
                    last.then_inc(st_free[q], 1)

            def planned(phase, place, p, j):
                planned_bases(phase, place, p, j, basis_step)
                kind, u = phase
                if kind != "agg" or j == 0:
                    return
                gs = {what[1]: g for k, what, g in plan.get((phase, place + "+"), []) if k == "max"}
                if place == WHERE[u][0]:
                    weights_max(u + 1, gs)
                if place == WHERE[u][1]:
                    scales(u + 1)

            windows(0, 6)
            for u in (1, 3, 5):
                v.memset(s_in[:, u:u + 1], LN_SCALE)
                link(v.memset(i_in[:, u:u + 1], 1.0 / LN_SCALE))
            weights_max(0, {0: 0})
            dve.wait_ge(e_x, 32)
            v.tensor_reduce(xin[:, :], S[:, :, :].rearrange("p t d -> p (t d)"), AX.X, ALU.max,
                            apply_absolute_value=True).then_inc(s_xin, 1)
            windows(6, 12)
            dve.wait_ge(s_xmax, 1)
            power_scale(s_in[:, 0:1], i_in[:, 0:1], xmax[:, :])
            v.nop().then_inc(s_s0, 1)
            scales(0)
            windows(12, NWIN)

            dve.wait_ge(s_wev, 2 * NWIN)
            link(v.tensor_tensor(deg[:, :], dg[:, 0, :], dg[:, 1, :], ALU.add))
            link(v.tensor_scalar(dinv[:, :], deg[:, :], 1.0, None, ALU.add))
            v.reciprocal(dinv[:, :], dinv[:, :]).then_inc(s_dsq, 1)
            v.tensor_reduce(gin[:, 0:1], deg[:, :], AX.X, ALU.max)
            link(v.tensor_scalar(rdeg[:, :], deg[:, :], 1.0, None, ALU.max))
            link(v.reciprocal(rdeg[:, :], rdeg[:, :]))
            dve.wait_ge(s_dsq, 2)
            link(v.tensor_scalar(zsc0[:, :], dinv[:, :], 2.0 ** -UNITS[0]["zexp"], None, ALU.mult))
            assert chain[0] == Z_SCALED, chain[0]
            link(v.tensor_scalar(aggc[:, 0, :], dinv[:, :], ownc[:, 0:1], 2.0 ** UNITS[0]["zexp"], ALU.mult, ALU.mult))

            for u, unit in enumerate(UNITS):
                nz = unit["nz"]

                def z_low(t, j):
                    if u == 0:
                        scale = zsc0[:, ds(t, 1)]
                    elif nz == 2:
                        scale = zsc[:, 0, ds(t, 1)]
                    else:
                        scale = 2.0 ** -unit["zexp"]
                    dve.wait_ge(s_zhi[u], t * nz + 1)
                    v.scalar_tensor_tensor(Z[:, 0, 1, ds(t, 1), :], Dp[:, j, 0:1, :], scale,
                                           Z[:, 0, 0, ds(t, 1), :], ALU.mult, ALU.subtract).then_inc(s_zlo[u], 1)
                    if unit["own"] is not None:
                        o = unit["own"]
                        v.scalar_tensor_tensor(S[:, ds(t, 1), :], Dp[:, j, o:o + 1, :], ownc[:, u:u + 1],
                                               bias[:, :].rearrange("p (a d) -> p a d", a=1),
                                               ALU.mult, ALU.add).then_inc(s_own[u], 1)

                def stats(t, j):
                    dve.wait_ge(s_v[u], t + 1)
                    v.bn_stats(stt[:, j, :], w2[:, j, :]).then_inc(s_bs, 1)
                    dve.wait_ge(s_bs, t + (LN.index(u) * NT + 1))
                    dve.sem_inc(s_carry_dve, 1)
                    v.bn_aggr(mvr[:, j, :], stt[:, j, :]).then_inc(s_mv[u], 1)

                def normalize(t, j, scale, source):
                    before = (LN.index(u) - 1) * NT
                    dve.wait_ge(s_sd, t + (before + 1))
                    v.reciprocal(rs[:, ds(t, 1)], sd[:, ds(t, 1)]).then_inc(s_rs, 1)
                    dve.wait_ge(s_rs, t * 2 + (2 * before + 1))
                    v.tensor_scalar(rsl[:, ds(t, 1)], rs[:, ds(t, 1)], scale, None, ALU.mult).then_inc(s_rs, 1)
                    dve.wait_ge(s_rs, t * 2 + (2 * before + 2))
                    v.tensor_scalar(w1[:, j:j + 1, :], source, mvr[:, j, 0:1],
                                    rsl[:, ds(t, 1)], ALU.subtract, ALU.mult).then_inc(s_r[u], 1)

                def gates(t, j, operand):
                    dve.wait_ge(s_r[u], t + 1)
                    if u == 3:
                        dve.wait_ge(s_hi[u], t + 1)
                    products = Z[:, 1, 0, 0, :] if u == 2 else w1[:, j, :]
                    for r in range(REL):
                        wait(dve, s_gl, t * 3 + (3 * NT * (u - 2) + r))
                        v.tensor_tensor_reduce(out=products, in0=operand[:, j, :], in1=gw[:, r, :], scale=1.0,
                                               scalar=0.0, op0=ALU.mult, op1=ALU.add,
                                               accum_out=glr[:, j, r:r + 1]).then_inc(s_gl, 1)
                    dve.wait_ge(s_gl, t * 3 + (3 * NT * (u - 2) + 2))
                    v.tensor_copy(glog[:, :, ds(t, 1)], glr[:, j, :]).then_inc(s_gl, 1)

                def after_agg(t, j):
                    dve.wait_ge(s_agg[u], t + 1)
                    if unit["ln"]:
                        wait(dve, s_ready[u + 1], t - 1)
                        wait(dve, s_xs[u], t - 1)
                    else:
                        wait(dve, s_hi[u], t - 1)
                        if u == 3:
                            if not (isinstance(t, int) and t < 2):
                                dve.wait_ge(s_gl, t * 3 + (3 * NT - 3))
                    c = aggc[:, u, ds(t, 1)] if u in (1, 2) else aggc[:, u, 0:1]
                    v.scalar_tensor_tensor(w1[:, j:j + 1, :], Dp[:, j, 2:3, :], c, S[:, ds(t, 1), :],
                                           ALU.mult, ALU.add).then_inc(s_pre[u], 1)
                    first = isinstance(t, int) and t == 0
                    if unit["ln"]:
                        join_residual(t, j, ALU.max if u == 2 else ALU.add)
                        stats(t, j)
                        if u == 2 and not first:
                            gates(t - 1, 1 - j, w1)
                        normalize(t, j, LN_SCALE, w2[:, j:j + 1, :])
                    elif u == 3 and not first:
                        gates(t - 1, 1 - j, w2)
                    if u in (2, 3) and isinstance(t, int) and t == NT - 1:
                        gates(t, j, w1 if u == 2 else w2)

                def join_residual(t, j, op):
                    dve.wait_ge(s_pre[u], t + 1)
                    tile_moved(dve, s_xl[u], t, j)
                    tile_moved(dve, s_xst[u], t - 2, j)
                    v.scalar_tensor_tensor(w2[:, j, :], w1[:, j, :], 0.0, xr[:, j, :], op, ALU.add).then_inc(s_v[u], 1)

                def last_tile(t, j):
                    dve.wait_ge(s_d, t + (NT * u + 1))
                    v.scalar_tensor_tensor(acc[:, 0, j, :], Dp[:, j, 0, :], ownc[:, u:u + 1], bias[:, :],
                                           ALU.mult, ALU.add).then_inc(s_own[u], 1)
                    dve.wait_ge(s_own[u], t + 1)
                    tile_moved(dve, s_xl[u], t, j)
                    if isinstance(t, int) and t < 2:
                        dve.wait_ge(s_ready[u], NT - 1 + t)
                    v.tensor_tensor(w2[:, j, :], acc[:, 0, j, :], xr[:, j, :], ALU.add).then_inc(s_v[u], 1)
                    stats(t, j)
                    if not (isinstance(t, int) and t == 0):
                        normalize_last(t - 1, 1 - j)

                def normalize_last(t, j):
                    tile_moved(dve, s_xst[u], t - 2, j)
                    normalize(t, j, 1.0, w2[:, j:j + 1, :])

                def conv_step(t, j):
                    dve.wait_ge(s_agg[0], t + 1)
                    v.scalar_tensor_tensor(S[:, ds(t, 1), :], Dp[:, j, 2:3, :], aggc[:, 0, ds(t, 1)],
                                           b0b.rearrange("p (a d) -> p a d", a=1), ALU.mult, ALU.add).then_inc(b_h, 1)
                    if isinstance(t, int) and t == 0:
                        return
                    if isinstance(t, int) and t == 1:
                        dve.wait_ge(b_mean, 1)
                        v.tensor_scalar(shift, T[:, 0, :], float(N) / P, None, ALU.mult).then_inc(b_shift, 1)
                        dve.wait_ge(b_shift, 1)
                        center(0)
                    center(t)

                def center(t):
                    dve.wait_ge(b_h, t + 1)
                    v.tensor_tensor(S[:, ds(t, 1), :], S[:, ds(t, 1), :], shift.rearrange("p (a d) -> p a d", a=1),
                                    ALU.subtract).then_inc(b_c, 1)

                if nz == 2:
                    dve.wait_ge(s_gt, u - 2)
                    v.tensor_scalar(zsc[:, :, :], gate[:, :, :], 2.0 ** -unit["zexp"], None, ALU.mult).then_inc(s_gz, 1)
                    dve.wait_ge(s_gz, u - 2)
                if not nz:
                    tiles(dve, last_tile)
                    normalize_last(NT - 1, 1)
                    break
                tiles(dve, z_low, lambda place, p, j: planned(("dense", u), place, p, j))
                if u in (2, 3):
                    dve.wait_ge(s_gw, 32 * (u - 1))
                if u:
                    dve.wait_ge(s_own[u], NT)
                if u == 0:
                    dve.wait_ge(s_bn, 48)
                tiles(dve, conv_step if u == 0 else after_agg, lambda place, p, j: planned(("agg", u), place, p, j))
                if u > 0:
                    continue

                dve.wait_ge(s_dout, NT)
                v.tensor_reduce(gin[:, 1:2], dout[:, :], AX.X, ALU.max).then_inc(s_gin, 1)
                dve.wait_ge(b_mean, 3)
                link(v.tensor_copy(mean, T[:, 0, :]))
                link(v.tensor_tensor(bnsc, mean, mean, ALU.mult))
                link(v.tensor_tensor(bnsc, T[:, 1, :], bnsc, ALU.subtract))
                v.tensor_scalar(bnsc, bnsc, 0.0, EPS, ALU.max, ALU.add).then_inc(b_vr, 1)
                dve.wait_ge(b_sd, 1)
                link(v.reciprocal(csum, csq))
                v.tensor_tensor(bnsc, csum, gamb, ALU.mult).then_inc(b_vr, 1)
                dve.wait_ge(b_vr, 2)
                link(v.tensor_tensor(mean, mean, bnsc, ALU.mult))
                link(v.tensor_tensor(mean, betb, mean, ALU.subtract))

                def shift_tile(t):
                    dve.wait_ge(b_n1, t + 1)
                    v.tensor_tensor(w1[:, t % 2, :], w1[:, t % 2, :], mean, ALU.add).then_inc(b_n2, 1)

                def join_tile(t):
                    dve.wait_ge(b_g, t + 1)
                    dve.wait_ge(s_xa[0 if t < 5 else 1], 16 if t < 5 else 32)
                    v.scalar_tensor_tensor(S[:, t, :], x_again(t), 2.0, w2[:, t % 2, :],
                                           ALU.mult, ALU.add).then_inc(s_v[0], 1)
                    dve.wait_ge(s_v[0], t + 1)
                    v.bn_stats(stt[:, t % 2, :], S[:, t, :]).then_inc(s_bs, 1)
                    dve.wait_ge(s_bs, t + 1)
                    v.bn_aggr(mv[:, t, :], stt[:, t % 2, :]).then_inc(s_mv[0], 1)

                shift_tile(0)
                for t in range(1, NT):
                    shift_tile(t)
                    join_tile(t - 1)
                join_tile(NT - 1)
                dve.wait_ge(s_sd0, 1)
                link(v.reciprocal(rs[:, :], sd[:, :]))
                link(v.tensor_scalar(rsl[:, :], rs[:, :], LN_SCALE, None, ALU.mult))
                for t in range(NT):
                    v.tensor_scalar(x_again(t), S[:, t, :], mv[:, t, 0:1], rs[:, t:t + 1],
                                    ALU.subtract, ALU.mult).then_inc(s_xs[0], 1)
                    wait(dve, s_ready[1], t - 1)
                    v.tensor_scalar(w1[:, t % 2, :], S[:, t, :], mv[:, t, 0:1], rsl[:, t:t + 1],
                                    ALU.subtract, ALU.mult).then_inc(s_r[0], 1)


_OUTS = [((N, D), "float32")]


def kernel(**inputs):
    import concourse.bacc as _bacc
    from concourse import mybir as _mybir
    from concourse.bass_utils import run_bass_kernel_spmd as _run

    def chunked(a):
        flat = np.full((CHUNKS * P,), PAD, a.dtype)
        flat[:E] = a
        return flat.reshape(CHUNKS, P)

    g = {k: np.asarray(v) for k, v in inputs.items()}
    src, dst, typ = chunked(g["src"]), chunked(g["dst"]), chunked(g["edge_type_2"])
    typ = np.where(np.arange(CHUNKS * P).reshape(CHUNKS, P) < E, typ, 0).astype(typ.dtype)
    lay = {
        "x": g["x"], "src_t": src.T, "dst_t": dst.T, "typ_t": typ.T, "dst_r": dst.reshape(CHUNKS // 2, 2, P),
        "W0": g["L0_gnn_W"].T, "b0": g["L0_gnn_b"], "gamma": g["L0_gnn_gamma"], "beta": g["L0_gnn_beta"],
        "Ws1": g["L1_gnn_W_self1"], "Wn1": g["L1_gnn_W_neigh1"], "b1": g["L1_gnn_b1"],
        "Ws2": g["L1_gnn_W_self2"], "Wn2": g["L1_gnn_W_neigh2"], "b2": g["L1_gnn_b2"],
    }
    for n in ("1", "2"):
        for a, b in (("basis", "basis"), ("att", "att"), ("gate", "gate_w"), ("root", "root"), ("rb", "bias")):
            lay[a + n] = g[f"L2_gnn_{b}{n}"]
    lay.update({"V1": g["L3_gnn_W1"], "vb1": g["L3_gnn_b1"], "V2": g["L3_gnn_W2"], "vb2": g["L3_gnn_b2"]})

    nc = _bacc.Bacc("TRN2", target_bir_lowering=False, num_devices=1)
    arrays, args = {}, {}
    for name, a in lay.items():
        a = np.ascontiguousarray(a)
        arrays[f"in_{name}"] = a
        args[name] = nc.dram_tensor(f"in_{name}", a.shape, _mybir.dt.from_np(a.dtype), kind="ExternalInput").ap()
    for i, (shape, dtype) in enumerate(_OUTS):
        args["out"] = nc.dram_tensor(f"out_{i}", shape, _mybir.dt.from_np(np.dtype(dtype)), kind="ExternalOutput").ap()
    args["xres"] = nc.dram_tensor("xres", (NP, D), _mybir.dt.float32, kind="Internal").ap()
    resnorm_gnn_kernel(nc, **args)
    r = _run(nc, [arrays], core_ids=[0])
    return r.results[0]["out_0"]
```
